# Optimizing a Trainium2 kernel written in Bass

```python
import numpy as np
import jax
import jax.numpy as jnp

def _softmax(x, axis=-1):
    return jax.nn.softmax(x, axis=axis)

def _gelu(x):
    return jax.nn.gelu(x, approximate=True)

def _silu(x):
    return jax.nn.silu(x)

def _sigmoid(x):
    return jax.nn.sigmoid(x)

def _layernorm(x, axis=-1, eps=1e-05):
    m = jnp.mean(x, axis=axis, keepdims=True)
    v = jnp.var(x, axis=axis, keepdims=True)
    return (x - m) / jnp.sqrt(v + eps)

def _scatter_add(tgt, idx, src, axis=0):
    return tgt.at[idx].add(src)

def _segment_sum(src, seg, n):
    return jax.ops.segment_sum(src, seg, n)
kernel_name = 'mk_prb_d2_jaxref_r8_a60465'

def setup_inputs(seed: int=0):
    np.random.seed(seed)
    _w = jnp.asarray

    def _L0_attn_setup():
        import jax, jax.numpy as jnp
        import numpy as np
        import math
        D_MODEL = 128
        N_HEADS = 16
        D_HEAD = D_MODEL // N_HEADS
        WINDOW = 32

        def _attention(x, Wq, bq, Wk, bk, Wv, bv, Wo, bo):
            B, T, C = x.shape
            W = min(WINDOW, T)
            scale = math.sqrt(D_HEAD)

            def proj(Wm, bm):
                return (x @ Wm.T + bm).reshape(B, T, N_HEADS, D_HEAD).transpose(0, 2, 1, 3)
            Q, K, V = (proj(Wq, bq), proj(Wk, bk), proj(Wv, bv))
            scores = jnp.einsum('bhqd,bhkd->bhqk', Q, K) / scale
            idx = jnp.arange(T)
            row = idx[:, None]
            col = idx[None, :]
            allowed = (col <= row) & (row - col < W)
            scores = jnp.where(allowed[None, None], scores, -jnp.inf)
            attn = jax.nn.softmax(scores, axis=-1)
            attn = jnp.nan_to_num(attn, nan=0.0)
            out = jnp.einsum('bhqk,bhkd->bhqd', attn, V)
            out = out.transpose(0, 2, 1, 3).reshape(B, T, C)
            return out @ Wo.T + bo
        key = jax.random.key(seed)
        ks = jax.random.split(key, 9)
        B, T = (2, 256)
        x = jax.random.normal(ks[0], (B, T, D_MODEL), dtype=jnp.float32)
        s = 1.0 / math.sqrt(D_MODEL)
        Wq = jax.random.uniform(ks[1], (D_MODEL, D_MODEL), jnp.float32, -s, s)
        bq = jax.random.uniform(ks[2], (D_MODEL,), jnp.float32, -s, s)
        Wk = jax.random.uniform(ks[3], (D_MODEL, D_MODEL), jnp.float32, -s, s)
        bk = jax.random.uniform(ks[4], (D_MODEL,), jnp.float32, -s, s)
        Wv = jax.random.uniform(ks[5], (D_MODEL, D_MODEL), jnp.float32, -s, s)
        bv = jax.random.uniform(ks[6], (D_MODEL,), jnp.float32, -s, s)
        Wo = jax.random.uniform(ks[7], (D_MODEL, D_MODEL), jnp.float32, -s, s)
        bo = jax.random.uniform(ks[8], (D_MODEL,), jnp.float32, -s, s)
        return {'x': x, 'Wq': Wq, 'bq': bq, 'Wk': Wk, 'bk': bk, 'Wv': Wv, 'bv': bv, 'Wo': Wo, 'bo': bo}
    _L0_attn_in = _L0_attn_setup()

    def _L0_ffn_setup():
        import jax, jax.numpy as jnp
        import numpy as np
        EMB = 128
        HEADS = 16
        SEQ = 256
        LATENT = 64
        N_EXP = 8
        TOP_K = 2
        EXP_DIM = 256
        BATCH = 2
        EPS = 1e-06

        def _rmsnorm(x, g):
            return x * jax.lax.rsqrt(jnp.mean(x * x, axis=-1, keepdims=True) + EPS) * g

        def _mla(h, Wq, Wdkv, Wuk, Wuv, Wo):
            B, S, D = h.shape
            hd = D // HEADS
            q = (h @ Wq).reshape(B, S, HEADS, hd)
            c = h @ Wdkv
            k = (c @ Wuk).reshape(B, S, HEADS, hd)
            v = (c @ Wuv).reshape(B, S, HEADS, hd)
            scores = jnp.einsum('bqhd,bkhd->bhqk', q, k) / jnp.sqrt(jnp.asarray(hd, h.dtype))
            causal = jnp.tril(jnp.ones((S, S), bool))
            scores = jnp.where(causal, scores, jnp.asarray(-1000000000.0, h.dtype))
            a = jax.nn.softmax(scores, axis=-1)
            out = jnp.einsum('bhqk,bkhd->bqhd', a, v).reshape(B, S, D)
            return out @ Wo

        def _moe(h, gate_w, w1, w2):
            B, S, D = h.shape
            t = h.reshape(B * S, D)
            logits = t @ gate_w
            top_v, top_i = jax.lax.top_k(logits, TOP_K)
            gates = jax.nn.softmax(top_v, axis=-1)
            T = t.shape[0]
            combine = jnp.zeros((T, N_EXP), t.dtype).at[jnp.arange(T)[:, None], top_i].add(gates)
            hid = jax.nn.silu(jnp.einsum('td,edh->teh', t, w1))
            ye = jnp.einsum('teh,ehd->ted', hid, w2)
            out = jnp.einsum('te,ted->td', combine, ye)
            return out.reshape(B, S, D)
        key = jax.random.key(seed)
        ks = jax.random.split(key, 12)
        s = 0.02
        return {'x': jax.random.normal(ks[0], (BATCH, SEQ, EMB), jnp.float32), 'g1': jnp.ones((EMB,), jnp.float32), 'Wq': jax.random.normal(ks[1], (EMB, EMB), jnp.float32) * s, 'Wdkv': jax.random.normal(ks[2], (EMB, LATENT), jnp.float32) * s, 'Wuk': jax.random.normal(ks[3], (LATENT, EMB), jnp.float32) * s, 'Wuv': jax.random.normal(ks[4], (LATENT, EMB), jnp.float32) * s, 'Wo': jax.random.normal(ks[5], (EMB, EMB), jnp.float32) * s, 'g2': jnp.ones((EMB,), jnp.float32), 'gate_w': jax.random.normal(ks[6], (EMB, N_EXP), jnp.float32) * s, 'w1': jax.random.normal(ks[7], (N_EXP, EMB, EXP_DIM), jnp.float32) * s, 'w2': jax.random.normal(ks[8], (N_EXP, EXP_DIM, EMB), jnp.float32) * s}
    _L0_ffn_in = _L0_ffn_setup()

    def _L1_attn_setup():
        import jax, jax.numpy as jnp
        import numpy as np
        D_MODEL = 128
        N_HEADS = 16
        HEAD_DIM = D_MODEL // N_HEADS
        MAX_LEN = 256
        BATCH = 2
        SEQ = 256
        key = jax.random.key(seed)
        ks = jax.random.split(key, 10)
        s = 1.0 / np.sqrt(D_MODEL)
        inp = {'x': jax.random.normal(ks[0], (BATCH, SEQ, D_MODEL), dtype=jnp.float32), 'Wq': jax.random.uniform(ks[1], (D_MODEL, D_MODEL), jnp.float32, -s, s), 'bq': jax.random.uniform(ks[2], (D_MODEL,), jnp.float32, -s, s), 'Wk': jax.random.uniform(ks[3], (D_MODEL, D_MODEL), jnp.float32, -s, s), 'bk': jax.random.uniform(ks[4], (D_MODEL,), jnp.float32, -s, s), 'Wv': jax.random.uniform(ks[5], (D_MODEL, D_MODEL), jnp.float32, -s, s), 'bv': jax.random.uniform(ks[6], (D_MODEL,), jnp.float32, -s, s), 'Wo': jax.random.uniform(ks[7], (D_MODEL, D_MODEL), jnp.float32, -s, s), 'bo': jax.random.uniform(ks[8], (D_MODEL,), jnp.float32, -s, s), 'rel_emb': jax.random.normal(ks[9], (MAX_LEN * 2 - 1, HEAD_DIM), dtype=jnp.float32)}
        return inp
    _L1_attn_in = _L1_attn_setup()

    def _L1_ffn_setup():
        import jax, jax.numpy as jnp
        import numpy as np
        E = 8
        K = 2
        D = 128
        H = 342
        B, S = (2, 256)

        def _moe_forward(x, centroid, Wg, bg, W1, b1, W2, b2):
            T = x.shape[0] * x.shape[1]
            xs = x.reshape(T, D)
            d2 = jnp.sum(xs * xs, axis=-1, keepdims=True) + jnp.sum(centroid * centroid, axis=-1)[None, :] - 2.0 * (xs @ centroid.T)
            dist = jnp.sqrt(jnp.maximum(d2, 1e-12))
            w, sel = jax.lax.top_k(dist, K)
            w = jax.nn.softmax(w.astype(jnp.float32), axis=1).astype(x.dtype)
            we = jnp.zeros((T, E), dtype=x.dtype).at[jnp.arange(T)[:, None], sel].add(w)
            out = jnp.zeros_like(xs)
            for e in range(E):
                h = jax.nn.silu(xs @ Wg[e] + bg[e]) * (xs @ W1[e] + b1[e])
                out = out + we[:, e:e + 1] * (h @ W2[e] + b2[e])
            return out.reshape(x.shape)
        key = jax.random.key(seed)
        ks = jax.random.split(key, 9)
        scale = 0.02
        return {'x': jax.random.normal(ks[0], (B, S, D), dtype=jnp.float32), 'centroid': jax.random.normal(ks[1], (E, D), dtype=jnp.float32), 'Wg': jax.random.normal(ks[2], (E, D, H), dtype=jnp.float32) * scale, 'bg': jnp.zeros((E, H), dtype=jnp.float32), 'W1': jax.random.normal(ks[3], (E, D, H), dtype=jnp.float32) * scale, 'b1': jnp.zeros((E, H), dtype=jnp.float32), 'W2': jax.random.normal(ks[4], (E, H, D), dtype=jnp.float32) * scale, 'b2': jnp.zeros((E, D), dtype=jnp.float32)}
    _L1_ffn_in = _L1_ffn_setup()
    _d = {'L0_attn_x': _L0_attn_in['x'], 'L0_attn_Wq': _L0_attn_in['Wq'], 'L0_attn_bq': _L0_attn_in['bq'], 'L0_attn_Wk': _L0_attn_in['Wk'], 'L0_attn_bk': _L0_attn_in['bk'], 'L0_attn_Wv': _L0_attn_in['Wv'], 'L0_attn_bv': _L0_attn_in['bv'], 'L0_attn_Wo': _L0_attn_in['Wo'], 'L0_attn_bo': _L0_attn_in['bo'], 'L0_ffn_g1': _L0_ffn_in['g1'], 'L0_ffn_Wq': _L0_ffn_in['Wq'], 'L0_ffn_Wdkv': _L0_ffn_in['Wdkv'], 'L0_ffn_Wuk': _L0_ffn_in['Wuk'], 'L0_ffn_Wuv': _L0_ffn_in['Wuv'], 'L0_ffn_Wo': _L0_ffn_in['Wo'], 'L0_ffn_g2': _L0_ffn_in['g2'], 'L0_ffn_gate_w': _L0_ffn_in['gate_w'], 'L0_ffn_w1': _L0_ffn_in['w1'], 'L0_ffn_w2': _L0_ffn_in['w2'], 'L1_attn_Wq': _L1_attn_in['Wq'], 'L1_attn_bq': _L1_attn_in['bq'], 'L1_attn_Wk': _L1_attn_in['Wk'], 'L1_attn_bk': _L1_attn_in['bk'], 'L1_attn_Wv': _L1_attn_in['Wv'], 'L1_attn_bv': _L1_attn_in['bv'], 'L1_attn_Wo': _L1_attn_in['Wo'], 'L1_attn_bo': _L1_attn_in['bo'], 'L1_attn_rel_emb': _L1_attn_in['rel_emb'], 'L1_ffn_centroid': _L1_ffn_in['centroid'], 'L1_ffn_Wg': _L1_ffn_in['Wg'], 'L1_ffn_bg': _L1_ffn_in['bg'], 'L1_ffn_W1': _L1_ffn_in['W1'], 'L1_ffn_b1': _L1_ffn_in['b1'], 'L1_ffn_W2': _L1_ffn_in['W2'], 'L1_ffn_b2': _L1_ffn_in['b2']}
    _x0 = _d['L0_attn_x']
    _d['L0_attn_x'] = jax.random.normal(jax.random.fold_in(jax.random.key(seed), 1), (16, 512, 128), dtype=_x0.dtype)
    del _x0
    return _d

def reference(L0_attn_x, L0_attn_Wq, L0_attn_bq, L0_attn_Wk, L0_attn_bk, L0_attn_Wv, L0_attn_bv, L0_attn_Wo, L0_attn_bo, L0_ffn_g1, L0_ffn_Wq, L0_ffn_Wdkv, L0_ffn_Wuk, L0_ffn_Wuv, L0_ffn_Wo, L0_ffn_g2, L0_ffn_gate_w, L0_ffn_w1, L0_ffn_w2, L1_attn_Wq, L1_attn_bq, L1_attn_Wk, L1_attn_bk, L1_attn_Wv, L1_attn_bv, L1_attn_Wo, L1_attn_bo, L1_attn_rel_emb, L1_ffn_centroid, L1_ffn_Wg, L1_ffn_bg, L1_ffn_W1, L1_ffn_b1, L1_ffn_W2, L1_ffn_b2):

    def _L0_attn_ref(x, Wq, bq, Wk, bk, Wv, bv, Wo, bo):
        import jax, jax.numpy as jnp
        import numpy as np
        import math
        D_MODEL = 128
        N_HEADS = 16
        D_HEAD = D_MODEL // N_HEADS
        WINDOW = 32

        def _attention(x, Wq, bq, Wk, bk, Wv, bv, Wo, bo):
            B, T, C = x.shape
            W = min(WINDOW, T)
            scale = math.sqrt(D_HEAD)

            def proj(Wm, bm):
                return (x @ Wm.T + bm).reshape(B, T, N_HEADS, D_HEAD).transpose(0, 2, 1, 3)
            Q, K, V = (proj(Wq, bq), proj(Wk, bk), proj(Wv, bv))
            scores = jnp.einsum('bhqd,bhkd->bhqk', Q, K) / scale
            idx = jnp.arange(T)
            row = idx[:, None]
            col = idx[None, :]
            allowed = (col <= row) & (row - col < W)
            scores = jnp.where(allowed[None, None], scores, -jnp.inf)
            attn = jax.nn.softmax(scores, axis=-1)
            attn = jnp.nan_to_num(attn, nan=0.0)
            out = jnp.einsum('bhqk,bhkd->bhqd', attn, V)
            out = out.transpose(0, 2, 1, 3).reshape(B, T, C)
            return out @ Wo.T + bo
        return _attention(x, Wq, bq, Wk, bk, Wv, bv, Wo, bo)

    def _L0_ffn_ref(x, g1, Wq, Wdkv, Wuk, Wuv, Wo, g2, gate_w, w1, w2):
        import jax, jax.numpy as jnp
        import numpy as np
        EMB = 128
        HEADS = 16
        SEQ = 256
        LATENT = 64
        N_EXP = 8
        TOP_K = 2
        EXP_DIM = 256
        BATCH = 2
        EPS = 1e-06

        def _rmsnorm(x, g):
            return x * jax.lax.rsqrt(jnp.mean(x * x, axis=-1, keepdims=True) + EPS) * g

        def _mla(h, Wq, Wdkv, Wuk, Wuv, Wo):
            B, S, D = h.shape
            hd = D // HEADS
            q = (h @ Wq).reshape(B, S, HEADS, hd)
            c = h @ Wdkv
            k = (c @ Wuk).reshape(B, S, HEADS, hd)
            v = (c @ Wuv).reshape(B, S, HEADS, hd)
            scores = jnp.einsum('bqhd,bkhd->bhqk', q, k) / jnp.sqrt(jnp.asarray(hd, h.dtype))
            causal = jnp.tril(jnp.ones((S, S), bool))
            scores = jnp.where(causal, scores, jnp.asarray(-1000000000.0, h.dtype))
            a = jax.nn.softmax(scores, axis=-1)
            out = jnp.einsum('bhqk,bkhd->bqhd', a, v).reshape(B, S, D)
            return out @ Wo

        def _moe(h, gate_w, w1, w2):
            B, S, D = h.shape
            t = h.reshape(B * S, D)
            logits = t @ gate_w
            top_v, top_i = jax.lax.top_k(logits, TOP_K)
            gates = jax.nn.softmax(top_v, axis=-1)
            T = t.shape[0]
            combine = jnp.zeros((T, N_EXP), t.dtype).at[jnp.arange(T)[:, None], top_i].add(gates)
            hid = jax.nn.silu(jnp.einsum('td,edh->teh', t, w1))
            ye = jnp.einsum('teh,ehd->ted', hid, w2)
            out = jnp.einsum('te,ted->td', combine, ye)
            return out.reshape(B, S, D)
        x = x + _mla(_rmsnorm(x, g1), Wq, Wdkv, Wuk, Wuv, Wo)
        x = x + _moe(_rmsnorm(x, g2), gate_w, w1, w2)
        return x

    def _L1_attn_ref(x, Wq, bq, Wk, bk, Wv, bv, Wo, bo, rel_emb):
        import jax, jax.numpy as jnp
        import numpy as np
        D_MODEL = 128
        N_HEADS = 16
        HEAD_DIM = D_MODEL // N_HEADS
        MAX_LEN = 256
        BATCH = 2
        SEQ = 256
        B, L, _ = x.shape

        def lin(x, W, b):
            return jnp.einsum('bld,ed->ble', x, W) + b

        def split_heads(t):
            return t.reshape(B, L, N_HEADS, HEAD_DIM).transpose(0, 2, 1, 3)
        q = split_heads(lin(x, Wq, bq))
        k = split_heads(lin(x, Wk, bk))
        v = split_heads(lin(x, Wv, bv))
        r = jnp.arange(L)
        idx = r[None, :] - r[:, None] + (MAX_LEN - 1)
        rel = rel_emb[idx]
        qk = jnp.einsum('bhld,bhrd->bhlr', q, k) / np.sqrt(HEAD_DIM)
        qk = qk + jnp.einsum('bhld,lrd->bhlr', q, rel)
        att = jax.nn.softmax(qk, axis=-1)
        out = jnp.einsum('bhlr,bhrd->bhld', att, v)
        out = out.transpose(0, 2, 1, 3).reshape(B, L, D_MODEL)
        return lin(out, Wo, bo)

    def _L1_ffn_ref(x, centroid, Wg, bg, W1, b1, W2, b2):
        import jax, jax.numpy as jnp
        import numpy as np
        E = 8
        K = 2
        D = 128
        H = 342
        B, S = (2, 256)

        def _moe_forward(x, centroid, Wg, bg, W1, b1, W2, b2):
            T = x.shape[0] * x.shape[1]
            xs = x.reshape(T, D)
            d2 = jnp.sum(xs * xs, axis=-1, keepdims=True) + jnp.sum(centroid * centroid, axis=-1)[None, :] - 2.0 * (xs @ centroid.T)
            dist = jnp.sqrt(jnp.maximum(d2, 1e-12))
            w, sel = jax.lax.top_k(dist, K)
            w = jax.nn.softmax(w.astype(jnp.float32), axis=1).astype(x.dtype)
            we = jnp.zeros((T, E), dtype=x.dtype).at[jnp.arange(T)[:, None], sel].add(w)
            out = jnp.zeros_like(xs)
            for e in range(E):
                h = jax.nn.silu(xs @ Wg[e] + bg[e]) * (xs @ W1[e] + b1[e])
                out = out + we[:, e:e + 1] * (h @ W2[e] + b2[e])
            return out.reshape(x.shape)
        return _moe_forward(x, centroid, Wg, bg, W1, b1, W2, b2)
    x = L0_attn_x
    xn = _layernorm(x, axis=-1)
    x = x + _L0_attn_ref(xn, L0_attn_Wq, L0_attn_bq, L0_attn_Wk, L0_attn_bk, L0_attn_Wv, L0_attn_bv, L0_attn_Wo, L0_attn_bo) + _L0_ffn_ref(xn, L0_ffn_g1, L0_ffn_Wq, L0_ffn_Wdkv, L0_ffn_Wuk, L0_ffn_Wuv, L0_ffn_Wo, L0_ffn_g2, L0_ffn_gate_w, L0_ffn_w1, L0_ffn_w2)
    xn = _layernorm(x, axis=-1)
    x = x + _L1_attn_ref(xn, L1_attn_Wq, L1_attn_bq, L1_attn_Wk, L1_attn_bk, L1_attn_Wv, L1_attn_bv, L1_attn_Wo, L1_attn_bo, L1_attn_rel_emb) + _L1_ffn_ref(xn, L1_ffn_centroid, L1_ffn_Wg, L1_ffn_bg, L1_ffn_W1, L1_ffn_b1, L1_ffn_W2, L1_ffn_b2)
    return x

_drawn_inputs = setup_inputs


def setup_inputs(seed=0):
    import zlib

    import numpy as np

    out = dict(_drawn_inputs(seed))
    spreads = {'L0_ffn_g1': (1.0, 0.6),
     'L0_ffn_g2': (1.0, 0.6),
     'L1_ffn_bg': (0.0, 0.8),
     'L1_ffn_b1': (0.0, 0.8),
     'L1_ffn_b2': (0.0, 0.8)}
    factors = {'L0_attn_Wq': 4.783,
     'L0_attn_bq': 8.0,
     'L0_attn_Wk': 4.777,
     'L0_attn_bk': 64.0,
     'L0_attn_bv': 3.46,
     'L0_ffn_Wq': 8.0,
     'L0_ffn_Wdkv': 8.0,
     'L0_ffn_Wuk': 8.0,
     'L0_ffn_Wuv': 8.0,
     'L0_ffn_Wo': 8.0,
     'L0_ffn_gate_w': 4.635,
     'L0_ffn_w1': 4.089,
     'L0_ffn_w2': 4.066,
     'L1_attn_bq': 26.798,
     'L1_attn_Wk': 5.571,
     'L1_attn_bk': 64.0,
     'L1_attn_bv': 16.393,
     'L1_ffn_Wg': 8.0,
     'L1_ffn_W1': 8.0,
     'L1_ffn_W2': 8.0,
     'L1_attn_Wq': 2.724,
     'L1_attn_bo': 8.0,
     'L1_attn_rel_emb': 3.399}
    for name, (base, spread) in spreads.items():
        noise = np.random.default_rng([zlib.crc32(name.encode()), seed]).standard_normal(out[name].shape)
        drawn = base * np.exp(spread * noise) if base else spread * noise
        out[name] = jnp.asarray(drawn.astype(out[name].dtype))
    for name, factor in factors.items():
        out[name] = (out[name] * factor).astype(out[name].dtype)
    return out
```

```python
from contextlib import ExitStack

import concourse.bass as bass
from concourse import mybir

F32 = mybir.dt.float32
BF16 = mybir.dt.bfloat16
ALU = mybir.AluOpType
ACT = mybir.ActivationFunctionType
AX = mybir.AxisListType


def two_layers(nc, dram):
    B, T, D = dram["L0_attn_x"].shape
    H, DH = 16, 8
    P = 128
    NT = T // P
    E = dram["L0_ffn_gate_w"].shape[1]
    F0 = dram["L0_ffn_w1"].shape[2]
    F1 = dram["L1_ffn_Wg"].shape[2]
    C0 = F0 // P
    C1 = 3
    CW = F1 // C1
    LAT = dram["L0_ffn_Wdkv"].shape[1]
    WIN = 32
    WQ = P + WIN
    SCALE = float(DH) ** -0.5
    LOW = -1e30
    NREL = dram["L1_attn_rel_emb"].shape[0]
    QP = 3 * T + 1
    SHIFT = 112
    HT = H // 2
    LB = 32
    NCONST = 28
    MLA_MAX = [(j, h0, n, n // 2) for j, n in ((0, 8), (1, 4), (2, 2), (3, 2)) for h0 in range(0, H, n)]
    NS = 8

    ctx = ExitStack()
    with ctx:
        def sb(name, shape, dt=F32):
            return ctx.enter_context(nc.sbuf_tensor(name, shape, dt))

        def sem(name):
            return ctx.enter_context(nc.semaphore(name))

        names = ["L0_attn_Wq", "L0_attn_Wk", "L0_attn_Wv", "L0_attn_Wo", "L0_ffn_Wq", "L0_ffn_Wo",
                 "L1_attn_Wq", "L1_attn_Wk", "L1_attn_Wv", "L1_attn_Wo"]
        W = {n: sb("w_" + n, [P, D]) for n in names}
        wdkv = sb("wdkv", [P, LAT])
        wuk = sb("wuk", [LAT, D])
        wuv = sb("wuv", [LAT, D])
        gate_w = sb("gate_w", [P, E])
        w1 = sb("w1", [P, E, F0])
        w2 = sb("w2", [P, E, C0, D])
        wg = sb("wg", [P, E, F1])
        wu = sb("wu", [P, E, F1])
        wd = sb("wd", [CW, E, C1, D])
        cen_t = sb("cen_t", [P, E])
        b2 = sb("b2", [E, D])
        cols = ["L0_attn_bq", "L0_attn_bk", "L0_attn_bo", "L1_attn_bq", "L1_attn_bk", "L1_attn_bo",
                "L0_ffn_g1", "L0_ffn_g2"]
        col = {n: sb("c_" + n, [P, 1]) for n in cols}
        bg = sb("bg", [CW, E, C1])
        bu = sb("bu", [CW, E, C1])
        bv0 = sb("bv0", [P, D])
        bv1 = sb("bv1", [P, D])
        bk0s = sb("bk0s", [P, 1])
        bk1s = sb("bk1s", [P, 1])
        cnorm = sb("cnorm", [P, E])
        ident = sb("ident", [P, P])
        identb = sb("identb", [P, P], BF16)
        causal_qk = sb("causal_qk", [P, P], BF16)
        causal_kq = sb("causal_kq", [P, P], BF16)
        band_qk = sb("band_qk", [P, WQ], BF16)
        band_kq = sb("band_kq", [P, WQ], BF16)
        sel_w = sb("sel_w", [P, E, P], BF16)
        sel_c = sb("sel_c", [P, 2, P], BF16)
        rev = sb("rev", [P, NT, E])
        power = sb("power", [P, 2, NT * E])
        rel_stack = sb("rel_stack", [P, 2 * T], BF16)
        q_stack = sb("q_stack", [P, H, T], BF16)
        k_stack = sb("k_stack", [P, H, T], BF16)
        probs = sb("probs", [P, 2 * 4 * 1280])
        v0 = sb("v0", [P, NT, H, 32])
        vm = sb("vm", [P, NT, H, 32])
        x = sb("x", [P, NT, D])
        xn = sb("xn", [P, NT, D])
        x1 = sb("x1", [P, NT, D])
        tmp = sb("tmp", [P, NT, D])
        xn_t = sb("xn_t", [P, T])
        h_t = sb("h_t", [P, T])
        c_t = sb("c_t", [LAT, T])
        q_f = sb("q_f", [P, T])
        k_f = sb("k_f", [P, T])
        q_parts = sb("q_parts", [P, 2 * QP], BF16)
        k_parts = sb("k_parts", [P, 3, T], BF16)
        o_raw = sb("o_raw", [P, 4, T])
        o_t = {"win": sb("o_t_win", [P, T]), "mla": sb("o_t_mla", [P, T])}
        o_t["rel"] = o_t["mla"]
        o_tok = tmp
        stats = sb("stats", [P, NT, 6])
        mv = sb("mv", [P, NT, 2])
        rstd = sb("rstd", [P, NT])
        rvar = sb("rvar", [P, NT])
        wt_full = sb("wt_full", [E, T])
        wt_mid = sb("wt_mid", [E, T], BF16)
        negmax = sb("negmax", [P, 2 * H, NT])
        cpart = sb("cpart", [NT * H, 2, P], BF16)
        rden = sb("rden", [P, NT, H])
        top = sb("top", [P, 8, NT, E])
        tc = sb("tc", [P, 8, NT])
        wparts = sb("wparts", [P, T], BF16)
        wt_f = c_t[0:E, :]
        q_win = sb("q_win", [P, H, P], BF16)
        rel_win = sb("rel_win", [P, 640], BF16)
        mcol = sb("mcol", [P, 2, HT * LB])
        cm = sb("cm", [P, 2])
        pause = sb("pause", [P, 1])
        crow = sb("crow", [P, P], BF16)
        crow_mid = sb("crow_mid", [2, P])
        hid_a = probs[:, 0:3 * T].rearrange("p (n t) -> p n t", n=3)
        hid_b = probs[:, 3 * T:6 * T].rearrange("p (n t) -> p n t", n=3)
        hid_c = probs[:, 6 * T:9 * T].rearrange("p (n t) -> p n t", n=3)
        y_t = probs[:, 9 * T:10 * T]
        PS = ctx.enter_context(nc.psum_tensor("ps", [P, 8, 512], F32))

        scr = {(a, n): nc.dram_tensor(f"scr_{a}_{n}", [3 * DH, H, T], BF16, kind="Internal").ap()
               for a in ("win", "mla", "rel") for n in ("qe", "qo", "k")}
        zrow_d = nc.dram_tensor("zrow_d", [2, H * T], BF16, kind="Internal").ap()
        rel_d = nc.dram_tensor("rel_d", [3, DH, 1024], BF16, kind="Internal").ap()

        ATT = ("win", "mla", "rel")
        s_load = sem("weights_loaded")
        s_relx = sem("rel_table_loaded")
        s_const = sem("constants_made")
        s_vset = sem("vector_setup")
        s_rel_sp = sem("rel_parts_stored")
        s_rel_ld = sem("rel_stack_loaded")
        s_x = sem("x_loaded")
        s_link = sem("vector_chain")
        s_pow = sem("powers_done")
        s_gs = sem("power_inputs_ready")
        s_link0 = sem("vector_setup_chain")
        s_xn = sem("xn_done")
        s_xr = sem("xr_done")
        s_tr = sem("xn_transposed")
        s_xnt = sem("xn_t_copied")
        s_proj = {a: sem("qk_projected_" + a) for a in ATT}
        s_vproj = {a: sem("v_projected_" + a) for a in ATT}
        s_lat = sem("latent_projected")
        s_ct = sem("c_t_copied")
        s_qkf = {a: sem("qk_copied_" + a) for a in ATT}
        s_parts = {a: sem("parts_split_" + a) for a in ATT}
        s_v = {a: sem("v_copied_" + a) for a in ATT}
        s_scr = {a: sem("parts_stored_" + a) for a in ATT}
        s_stk = {a: sem("stack_loaded_" + a) for a in ATT}
        s_sc = {a: sem("scores_for_max_" + a) for a in ("win", "mla")}
        s_mx = {a: sem("max_taken_" + a) for a in ("win", "mla")}
        s_mxt = {a: sem("max_transposed_" + a) for a in ("win", "mla")}
        s_cp = {a: sem("max_split_" + a) for a in ("win", "mla")}
        s_sh = {a: sem("shift_rows_loaded_" + a) for a in ("win", "mla")}
        s_st = {a: sem("scores_t_" + a) for a in ("win", "mla")}
        s_ex = {a: sem("probs_ready_" + a) for a in ATT}
        s_pv = {a: sem("pv_done_" + a) for a in ATT}
        s_or = {a: sem("o_raw_copied_" + a) for a in ATT}
        s_ort = {a: sem("o_raw_transposed_" + a) for a in ATT}
        s_on = {a: sem("o_normalised_" + a) for a in ATT}
        s_ot = {a: sem("o_transposed_" + a) for a in ATT}
        s_otc = {a: sem("o_t_copied_" + a) for a in ATT}
        s_mo = sem("mla_out_projected")
        s_moc = sem("mla_out_copied")
        s_mot = sem("mla_out_transposed")
        s_rr = sem("moe_input_normed")
        s_rt = sem("moe_input_transposed")
        s_h2 = sem("moe_input_t_copied")
        s_lg = {0: sem("logits_0"), 1: sem("logits_1")}
        s_gd = {0: sem("gate_gap_0"), 1: sem("gate_gap_1")}
        s_ge = {0: sem("gate_exp_0"), 1: sem("gate_exp_1")}
        s_cb = {0: sem("combine_0"), 1: sem("combine_1")}
        s_cbt = {0: sem("combine_transposed_0"), 1: sem("combine_transposed_1")}
        s_wp = {0: sem("combine_split_0"), 1: sem("combine_split_1")}
        s_wb = {0: sem("combine_spread_0"), 1: sem("combine_spread_1")}
        s_up = {0: sem("up_done_0"), 1: sem("up_done_1")}
        s_si = {0: sem("silu_done_0"), 1: sem("silu_done_1")}
        s_hu = sem("gated_up_1")
        s_hid = {0: sem("hidden_scaled_0"), 1: sem("hidden_scaled_1")}
        s_dn = {0: sem("down_done_0"), 1: sem("down_done_1")}
        s_yo = {0: sem("layer_out_done_0"), 1: sem("layer_out_done_1")}
        s_yc = {0: sem("layer_out_copied_0"), 1: sem("layer_out_copied_1")}
        s_yt = {0: sem("layer_out_transposed_0"), 1: sem("layer_out_transposed_1")}
        s_dist = sem("squared_distance")
        s_x1 = sem("x1_done")
        s_x2 = sem("x2_done")
        s_out = sem("zero_rows_and_out_stored")
        s_qw = sem("rel_windows_copied")
        s_rs = sem("rel_scores")
        s_rm = sem("rel_max_over_key_tiles")
        s_rmt = sem("rel_max_transposed")
        s_rc = sem("rel_max_over_keys")
        s_rct = sem("rel_max_row_transposed")
        s_rcs = sem("rel_max_split")
        s_rsh = sem("rel_scores_shifted")
        s_link2 = sem("rel_vector_chain")

        block = ctx.enter_context(nc.Block())

        col_loads = [(col[n][:], dram[n].rearrange("(p o) -> p o", o=1)) for n in cols]
        loads = [(W[n][:], dram[n]) for n in names] + [
            (wdkv[:], dram["L0_ffn_Wdkv"]), (wuk[:], dram["L0_ffn_Wuk"]), (wuv[:], dram["L0_ffn_Wuv"]),
            (gate_w[:], dram["L0_ffn_gate_w"]), (cen_t[:], dram["centroid_t"]), (b2[:], dram["L1_ffn_b2"]),
            (w1[:], dram["L0_ffn_w1"].rearrange("e c f -> c e f")),
            (wg[:], dram["L1_ffn_Wg"].rearrange("e c f -> c e f")),
            (wu[:], dram["L1_ffn_W1"].rearrange("e c f -> c e f")),
            (bv0[:], dram["L0_attn_bv"].rearrange("(o d) -> o d", o=1).to_broadcast([P, D])),
            (bv1[:], dram["L1_attn_bv"].rearrange("(o d) -> o d", o=1).to_broadcast([P, D])),
            (tmp[:].rearrange("p a b -> p (a b)"),
             dram["L1_ffn_centroid"].rearrange("(o e) d -> o (e d)", o=1)[:, 0:4 * D].to_broadcast([P, 4 * D])),
            (x1[:].rearrange("p a b -> p (a b)"),
             dram["L1_ffn_centroid"].rearrange("(o e) d -> o (e d)", o=1)[:, 4 * D:8 * D].to_broadcast([P, 4 * D])),
        ] + col_loads
        for e in range(E):
            loads.append((w2[:, e, :, :], dram["L0_ffn_w2"][e].rearrange("(c p) d -> p c d", p=P)))
            loads.append((wd[:, e, :, :], dram["L1_ffn_W2"][e].rearrange("(c p) d -> p c d", p=CW)))
        bias_loads = [(bg[:], dram["L1_ffn_bg"]),
                      (bu[:], dram["L1_ffn_b1"])]
        NLOAD = 16 * (len(loads) + 2)

        @block.sync
        def _(sp):
            rel_t = dram["rel_emb_t"]
            tail = NREL - 256
            relx = probs[0:DH, 0:1024]
            sp.dma_start(relx[:, 0:256], rel_t[:, tail:NREL]).then_inc(s_relx, 16)
            sp.dma_start(relx[:, 256:256 + NREL], rel_t).then_inc(s_relx, 16)
            with nc.allow_non_contiguous_dma(reason="one row repeated, and short biases"):
                for dst, src in bias_loads:
                    sp.dma_start(dst.rearrange("p e c -> p (e c)"), src).then_inc(s_load, 16)
                for dst, src in loads:
                    sp.dma_start(dst, src).then_inc(s_load, 16)
            sp.wait_ge(s_vset, 1)
            sp.dma_start(zrow_d.rearrange("a (b c) -> (a b) c", c=P), wparts[:, 0:P]).then_inc(s_out, 16)
            sp.wait_ge(s_vset, 2)
            for p in range(3):
                sp.dma_start(rel_d[p], k_stack[0:DH, 2 * p:2 * p + 2, :].rearrange("p a b -> p (a b)"))\
                  .then_inc(s_rel_sp, 16)
            sp.wait_ge(s_rel_sp, 48)
            for n in range(2):
                for s, p in enumerate((0, 1, 2, 0, 1, 0)):
                    sp.dma_start(rel_stack[64 * n + DH * s:64 * n + DH * s + DH, n:2 * T],
                                 rel_d[p][:, 0:2 * T - n]).then_inc(s_rel_ld, 16)
            sp.wait_ge(s_load, NLOAD)
            sp.wait_ge(s_vset, 3)
            sp.wait_ge(s_out, 16)
            with sp.Fori(0, B) as i:
                def store_parts(a):
                    sp.wait_ge(s_parts[a], i * 2 + 2)
                    for p in range(3):
                        for n, src in (("qe", q_parts[:, p * T:p * T + T]),
                                       ("qo", q_parts[:, 3 * T + p * T:3 * T + p * T + T]),
                                       ("k", k_parts[:, p, :])):
                            dst = scr[a, n][DH * p:DH * p + DH].rearrange("d h t -> h d t")
                            sp.dma_start(dst, src).then_inc(s_scr[a], 16)

                def load_stack(a):
                    sp.wait_ge(s_scr[a], i * 144 + 144)
                    sp.dma_start(q_stack[SHIFT:SHIFT + 2].rearrange("p h t -> p (h t)"), zrow_d)\
                      .then_inc(s_stk[a], 16)
                    for n, name in enumerate(("qe", "qo")):
                        for s, p in enumerate((0, 0, 0, 1, 1, 2)):
                            r = 64 * n + DH * s
                            sp.dma_start(q_stack[r:r + DH], scr[a, name][DH * p:DH * p + DH])\
                              .then_inc(s_stk[a], 16)
                        for s, m in ((0, 3), (3, 2), (5, 1)):
                            r = 64 * n + DH * s
                            sp.dma_start(k_stack[r:r + DH * m], scr[a, "k"][0:DH * m])\
                              .then_inc(s_stk[a], 16)

                def load_shift(a):
                    sp.wait_ge(s_cp[a], i + 1)
                    for p in range(2):
                        dst = q_stack[SHIFT + p:SHIFT + p + 1].rearrange("o h (j q) -> o (h j) q", j=NT)
                        sp.dma_start(dst, cpart[:, p, :]).then_inc(s_sh[a], 16)

                sp.dma_start(x[:], dram["L0_attn_x"][i].rearrange("(j p) d -> p j d", p=P)).then_inc(s_x, 16)
                store_parts("win")
                load_stack("win")
                store_parts("mla")
                load_shift("win")
                sp.wait_ge(s_pv["win"], i * 4 + 4)
                load_stack("mla")
                load_shift("mla")
                store_parts("rel")
                sp.wait_ge(s_pv["mla"], i * 4 + 4)
                load_stack("rel")
                sp.wait_ge(s_x2, i + 1)
                sp.dma_start(dram["out"][i].rearrange("(j p) d -> p j d", p=P), x1[:]).then_inc(s_out, 16)
            sp.wait_ge(s_out, 16 * B + 16)

        @block.gpsimd
        def _(pool):
            made = [0]

            def done(ins):
                made[0] += 1
                ins.then_inc(s_const, 1)

            def after():
                pool.wait_ge(s_const, made[0])

            done(pool.memset(ident[:], 0.0))
            done(pool.memset(causal_qk[:], 0.0))
            done(pool.memset(causal_kq[:], 0.0))
            done(pool.memset(band_qk[:], 0.0))
            done(pool.memset(band_kq[:], 0.0))
            done(pool.memset(sel_w[:], 0.0))
            done(pool.memset(sel_c[:], 0.0))
            done(pool.memset(power[:, 0, :], 0.5))
            done(pool.memset(power[:, 1, :], -0.5))
            for e in range(E):
                done(pool.memset(rev[:, :, e:e + 1], float(E - e)))
            after()

            def keep(t, op, fill, base, pattern, mult):
                done(pool.affine_select(out=t, in_=t, compare_op=op, fill=fill, base=base,
                                        pattern=pattern, channel_multiplier=mult))

            keep(ident[:], ALU.not_equal, 1.0, 0, [[-1, P]], 1)
            keep(causal_qk[:], ALU.is_ge, LOW, 0, [[-1, P]], 1)
            keep(causal_kq[:], ALU.is_ge, LOW, 0, [[1, P]], -1)
            keep(band_qk[:], ALU.is_ge, LOW, WIN, [[-1, WQ]], 1)
            keep(band_kq[:], ALU.is_ge, LOW, 0, [[1, WQ]], -1)
            for n in range(3):
                keep(sel_w[:], ALU.not_equal, 1.0, -32 * n, [[-1, E], [0, P]], 1)
                after()
            for n in range(2):
                keep(sel_c[:], ALU.not_equal, 1.0, -32 * n, [[-1, 2], [0, P]], 1)
                after()
            keep(band_qk[:], ALU.is_ge, LOW, WIN - 1 - WIN, [[1, WQ]], -1)
            keep(band_kq[:], ALU.is_ge, LOW, WIN - 1, [[-1, WQ]], 1)
            with pool.Fori(0, B) as i:
                for n in range(4):
                    pool.wait_ge(s_gs, i * 5 + n + 1)
                    nc.gpsimd.tensor_tensor(rstd[:], rvar[:], power[:, 1, 0:NT], ALU.pow).then_inc(s_pow, 1)
                pool.wait_ge(s_gs, i * 5 + 5)
                nc.gpsimd.tensor_tensor(top[:, 0], top[:, 7], power[:, 0, :].rearrange("p (j e) -> p j e", e=E),
                                        ALU.pow).then_inc(s_pow, 1)

        @block.scalar
        def _(act):
            def ident_of(out, in_, bias=0.0, scale=1.0):
                return nc.scalar.activation(out, in_, ACT.Identity, bias=bias, scale=scale)

            act.wait_ge(s_load, NLOAD)
            act.wait_ge(s_vset, 3)
            with act.Fori(0, B) as i:
                def copy_qk(a, qbank, kbank, bq, bks):
                    if a != "win":
                        act.wait_ge(s_parts[{"mla": "win", "rel": "mla"}[a]], i * 2 + 2)
                    act.wait_ge(s_proj[a], i * 2 + 1)
                    ident_of(q_f[:], PS[:, qbank, :], bias=bq).then_inc(s_qkf[a], 1)
                    act.wait_ge(s_proj[a], i * 2 + 2)
                    ident_of(k_f[:], PS[:, kbank, :], bias=bks, scale=SCALE).then_inc(s_qkf[a], 1)

                act.wait_ge(s_tr, i * 3 + 1)
                ident_of(xn_t[:], PS[:, 0, :]).then_inc(s_xnt, 1)
                act.wait_ge(s_tr, i * 3 + 2)
                ident_of(h_t[:], PS[:, 1, :], scale=col["L0_ffn_g1"][:, 0:1]).then_inc(s_xnt, 1)
                act.wait_ge(s_lat, i + 1)
                ident_of(c_t[:], PS[0:LAT, 6, :]).then_inc(s_ct, 1)
                copy_qk("win", 2, 3, col["L0_attn_bq"][:, 0:1], bk0s[:, 0:1])
                copy_qk("mla", 5, 7, 0.0, 0.0)
                for n in range(H // 2):
                    if n >= 4 and n % 2 == 0:
                        act.wait_ge(s_pv["win"], i * 4 + n // 2 - 1)
                    act.wait_ge(s_st["win"], i * (H // 2) + n + 1)
                    b = 3 * (n % 2)
                    p4 = probs[:, (n // 2) % 2 * 5120:(n // 2) % 2 * 5120 + 2560].rearrange("p (r c) -> p r c", r=4)
                    p2 = p4[:, 2 * (n % 2):2 * (n % 2) + 2, :]
                    nc.scalar.activation(p2[:, :, 0:3 * WQ], PS[:, b:b + 2, 0:3 * WQ], ACT.Exp)
                    nc.scalar.activation(p2[:, :, 3 * WQ:3 * WQ + P],
                                         PS[:, b + 2, 0:2 * P].rearrange("p (r c) -> p r c", r=2),
                                         ACT.Exp).then_inc(s_ex["win"], 1)
                act.wait_ge(s_pv["win"], i * 4 + 4)
                for h in range(H):
                    if h >= 8 and h % 4 == 0:
                        act.wait_ge(s_pv["mla"], i * 4 + h // 4 - 1)
                    act.wait_ge(s_st["mla"], i * H + h + 1)
                    b = 3 * (h % 2)
                    o = (h // 4) % 2 * 5120 + (h % 4) * 1280
                    nc.scalar.activation(probs[:, o:o + 1280],
                                         PS[:, b:b + 3, :].rearrange("p b c -> p (b c)")[:, 0:1280],
                                         ACT.Exp).then_inc(s_ex["mla"], 1)
                act.wait_ge(s_mo, i + 1)
                ident_of(y_t, PS[:, 5, :]).then_inc(s_moc, 1)
                act.wait_ge(s_rt, i + 1)
                ident_of(h_t[:], PS[:, 7, :], scale=col["L0_ffn_g2"][:, 0:1]).then_inc(s_h2, 1)
                act.wait_ge(s_gd[0], i + 1)
                nc.scalar.activation(tc[:, 5], tc[:, 4], ACT.Exp).then_inc(s_ge[0], 1)
                N0 = E * C0
                for n in range(N0):
                    act.wait_ge(s_up[0], i * N0 + n + 1)
                    if n >= 3:
                        act.wait_ge(s_hid[0], i * N0 + n - 2)
                    nc.scalar.activation(hid_a[:, n % 3], PS[:, n % 4, :], ACT.Silu).then_inc(s_si[0], 1)
                act.wait_ge(s_yo[0], i + 1)
                ident_of(y_t, PS[:, 6, :], bias=col["L0_attn_bo"][:, 0:1]).then_inc(s_yc[0], 1)
                act.wait_ge(s_tr, i * 3 + 3)
                ident_of(xn_t[:], PS[:, 0, :]).then_inc(s_xnt, 1)
                copy_qk("rel", 1, 2, col["L1_attn_bq"][:, 0:1], bk1s[:, 0:1])
                act.wait_ge(s_gd[1], i + 1)
                nc.scalar.activation(tc[:, 5], tc[:, 4], ACT.Exp).then_inc(s_ge[1], 1)
                pr = probs[:, 0:NT * H * P].rearrange("p (k h l) -> p k h l", k=NT, h=H)
                with act.Fori(0, NT) as lq:
                    for t in range(NS):
                        act.wait_ge(s_rsh, i * 32 + lq * 8 + t + 1)
                        lb, hh = t // 2, t % 2
                        b = 2 * (t % 3)
                        src = PS[:, b:b + 2, :].rearrange("p b (k h l) -> p (b k) h l", k=2, h=HT)
                        nc.scalar.activation(pr[:, :, hh * HT:hh * HT + HT, lb * LB:lb * LB + LB], src,
                                             ACT.Exp).then_inc(s_ex["rel"], 1)
                N1 = E * C1
                for n in range(N1):
                    act.wait_ge(s_up[1], i * N1 + n + 1)
                    if n >= 3:
                        act.wait_ge(s_hu, i * N1 + n - 2)
                    nc.scalar.activation(hid_a[0:CW, n % 3], PS[0:CW, 2 * (n % 2), :], ACT.Silu,
                                         bias=bg[:, n // C1, n % C1:n % C1 + 1]).then_inc(s_si[1], 1)
                act.wait_ge(s_yo[1], i + 1)
                ident_of(y_t, PS[:, 6, :], bias=col["L1_attn_bo"][:, 0:1]).then_inc(s_yc[1], 1)

        NLINK = 72

        @block.vector
        def _(dve):
            v = nc.vector
            cnt = [0]

            def link0(ins):
                cnt[0] += 1
                ins.then_inc(s_link0, 1)
                dve.wait_ge(s_link0, cnt[0])

            v.memset(wparts[:], 0.0).then_inc(s_vset, 1)
            v.memset(rel_stack[:], 0.0)
            v.memset(q_stack[:], 0.0)
            v.memset(k_stack[0:96], 0.0)
            v.memset(k_stack[96:P], 1.0)
            v.memset(crow[:], 0.0)
            v.memset(q_parts[:], 0.0)
            v.memset(negmax[:], 0.0)
            v.memset(v0[:], 0.0)
            link0(v.memset(vm[:], 0.0))
            v.memset(v0[:, :, :, DH:DH + 1], 1.0)
            v.memset(vm[:, :, :, DH:DH + 1], 1.0)
            dve.wait_ge(s_relx, 32)
            relx = probs[0:DH, 0:1024]
            link0(v.tensor_copy(relx[:, 256 + NREL:1024],
                                relx[:, 255 + NREL:256 + NREL].to_broadcast([DH, 1024 - 256 - NREL])))
            rp = [k_stack[0:DH, 2 * p:2 * p + 2, :].rearrange("p a b -> p (a b)") for p in range(3)]
            link0(v.tensor_copy(rp[0], relx))
            link0(v.tensor_tensor(relx, relx, rp[0], ALU.subtract))
            link0(v.tensor_copy(rp[1], relx))
            v.tensor_tensor(rp[2], relx, rp[1], ALU.subtract).then_inc(s_vset, 1)
            dve.wait_ge(s_const, NCONST)
            dve.wait_ge(s_load, NLOAD)
            v.tensor_copy(identb[:], ident[:])
            v.tensor_scalar_mul(bk0s[:], col["L0_attn_bk"][:], SCALE)
            v.tensor_scalar_mul(bk1s[:], col["L1_attn_bk"][:], SCALE)
            v.tensor_tensor(xn[:], tmp[:], tmp[:], ALU.mult)
            link0(v.tensor_tensor(x[:], x1[:], x1[:], ALU.mult))
            v.tensor_reduce(cnorm[:, 0:NT], xn[:], AX.X, ALU.add)
            v.tensor_reduce(cnorm[:, NT:E], x[:], AX.X, ALU.add).then_inc(s_vset, 1)
            dve.wait_ge(s_vset, 3)
            cnt[0] = 0
            with dve.Fori(0, B) as i:
                def link(ins):
                    cnt[0] += 1
                    ins.then_inc(s_link, 1)
                    dve.wait_ge(s_link, i * NLINK + cnt[0])

                def norm(src, dst, n, eps, rms, out_sem, out_value):
                    for j in range(NT):
                        last = v.bn_stats(stats[:, j], src[:, j])
                    link(last)
                    v.memset(pause[:], 0.0)
                    for j in range(NT):
                        last = v.bn_aggr(mv[:, j], stats[:, j])
                    link(last)
                    if rms:
                        link(v.tensor_tensor(rvar[:], mv[:, :, 0], mv[:, :, 0], ALU.mult))
                        link(v.tensor_tensor(rvar[:], rvar[:], mv[:, :, 1], ALU.add))
                        v.tensor_scalar_add(rvar[:], rvar[:], eps).then_inc(s_gs, 1)
                    else:
                        v.tensor_scalar_add(rvar[:], mv[:, :, 1], eps).then_inc(s_gs, 1)
                    dve.wait_ge(s_pow, i * 5 + n + 1)
                    for j in range(NT):
                        if rms:
                            last = v.tensor_scalar_mul(dst[:, j], src[:, j], rstd[:, j:j + 1])
                        else:
                            last = v.tensor_scalar(dst[:, j], src[:, j], mv[:, j, 0:1], rstd[:, j:j + 1],
                                                   ALU.subtract, ALU.mult)
                    last.then_inc(out_sem, 1)
                    dve.wait_ge(out_sem, out_value)

                def split_parts(a):
                    if a != "win":
                        dve.wait_ge(s_scr[{"mla": "win", "rel": "mla"}[a]], i * 144 + 144)
                    dve.wait_ge(s_qkf[a], i * 2 + 2)
                    q = q_f[:].rearrange("p (u n) -> p n u", n=2)
                    qp = q_parts[:].rearrange("p (n x) -> p n x", n=2)
                    qd = [qp[:, :, p * T:p * T + T - 1:2] for p in range(3)]
                    v.tensor_copy(qd[0], q)
                    link(v.tensor_copy(k_parts[:, 0], k_f[:]))
                    v.tensor_tensor(q, q, qd[0], ALU.subtract)
                    link(v.tensor_tensor(k_f[:], k_f[:], k_parts[:, 0], ALU.subtract))
                    v.tensor_copy(qd[1], q)
                    link(v.tensor_copy(k_parts[:, 1], k_f[:]))
                    v.tensor_tensor(qd[2], q, qd[1], ALU.subtract).then_inc(s_parts[a], 1)
                    v.tensor_tensor(k_parts[:, 2], k_f[:], k_parts[:, 1], ALU.subtract).then_inc(s_parts[a], 1)

                def copy_v(a, dst, bank, bias):
                    dve.wait_ge(s_vproj[a], i + 1)
                    out = dst[:, :, :, 0:DH]
                    src = PS[:, bank, :].rearrange("p (j h d) -> p j h d", j=NT, h=H)
                    if bias is None:
                        v.tensor_copy(out, src).then_inc(s_v[a], 1)
                    else:
                        for j in range(NT):
                            last = v.tensor_tensor(out[:, j], src[:, j],
                                                   bias[:].rearrange("p (h d) -> p h d", h=H), ALU.add)
                        last.then_inc(s_v[a], 1)

                def split_max(a):
                    dve.wait_ge(s_mxt[a], i + 1)
                    if a == "mla":
                        dve.wait_ge(s_sh["win"], i * 32 + 32)
                    src = PS[0:NT * H, 6, 0:P]
                    link(v.tensor_copy(cpart[:, 0], src))
                    v.tensor_tensor(cpart[:, 1], src, cpart[:, 0], ALU.subtract).then_inc(s_cp[a], 1)

                def copy_o_raw(a):
                    for g in range(4):
                        dve.wait_ge(s_pv[a], i * 4 + g + 1)
                        v.tensor_copy(o_raw[:, g, :], PS[:, 6 + g % 2, :]).then_inc(s_or[a], 1)

                def normalise(a):
                    dve.wait_ge(s_ort[a], i + 1)
                    src = PS[:, 0:4, :].rearrange("p j (h c) -> p j h c", h=H)
                    link(v.reciprocal(rden[:], src[:, :, :, DH]))
                    for j in range(NT):
                        last = v.tensor_tensor(o_tok[:, j].rearrange("p (h d) -> p h d", h=H), src[:, j, :, 0:DH],
                                               rden[:, j].rearrange("p (h o) -> p h o", o=1).to_broadcast([P, H, DH]),
                                               ALU.mult)
                    last.then_inc(s_on[a], 1)
                    dve.wait_ge(s_ot[a], i + 1)
                    v.tensor_copy(o_t[a][:], PS[:, 4, :]).then_inc(s_otc[a], 1)

                def spread(t):
                    return t.rearrange("p (j o) -> p j o", o=1).to_broadcast([P, NT, E])

                def top_two(k):
                    score = top[:, 0]
                    link(v.tensor_reduce(tc[:, 0], score, AX.X, ALU.max))
                    link(v.tensor_tensor(top[:, 1], score, spread(tc[:, 0]), ALU.is_equal))
                    link(v.tensor_tensor(top[:, 1], top[:, 1], rev[:], ALU.mult))
                    link(v.tensor_reduce(tc[:, 1], top[:, 1], AX.X, ALU.max))
                    link(v.tensor_tensor(top[:, 2], top[:, 1], spread(tc[:, 1]), ALU.is_equal))
                    link(v.scalar_tensor_tensor(top[:, 3], top[:, 2], -3e38, score, ALU.mult, ALU.add))
                    link(v.tensor_reduce(tc[:, 2], top[:, 3], AX.X, ALU.max))
                    v.tensor_tensor(tc[:, 4], tc[:, 2], tc[:, 0], ALU.subtract).then_inc(s_gd[k], 1)
                    link(v.tensor_tensor(top[:, 4], top[:, 3], spread(tc[:, 2]), ALU.is_equal))
                    link(v.tensor_tensor(top[:, 4], top[:, 4], rev[:], ALU.mult))
                    link(v.tensor_reduce(tc[:, 3], top[:, 4], AX.X, ALU.max))
                    link(v.tensor_tensor(top[:, 5], top[:, 4], spread(tc[:, 3]), ALU.is_equal))
                    dve.wait_ge(s_ge[k], i + 1)
                    link(v.tensor_scalar_add(tc[:, 6], tc[:, 5], 1.0))
                    link(v.reciprocal(tc[:, 6], tc[:, 6]))
                    link(v.tensor_tensor(tc[:, 7], tc[:, 5], tc[:, 6], ALU.mult))
                    v.tensor_tensor(top[:, 1], top[:, 2], spread(tc[:, 6]), ALU.mult)
                    link(v.tensor_tensor(top[:, 4], top[:, 5], spread(tc[:, 7]), ALU.mult))
                    v.tensor_tensor(top[:, 6], top[:, 1], top[:, 4], ALU.add).then_inc(s_cb[k], 1)

                def split_combine(k, bank):
                    dve.wait_ge(s_cbt[k], i + 1)
                    src = PS[0:E, bank, :]
                    v.tensor_copy(wt_full[:], src)
                    link(v.tensor_copy(wparts[0:E], src))
                    link(v.tensor_tensor(wt_f, src, wparts[0:E], ALU.subtract))
                    link(v.tensor_copy(wt_mid[:], wt_f))
                    v.tensor_copy(wparts[32:32 + E], wt_mid[:])
                    link(v.tensor_tensor(wt_f, wt_f, wt_mid[:], ALU.subtract))
                    v.tensor_copy(wparts[64:64 + E], wt_f).then_inc(s_wp[k], 1)

                dve.wait_ge(s_x, i * 16 + 16)
                norm(x, xn, 0, 1e-5, False, s_xn, i * 2 + 1)
                norm(xn, tmp, 1, 1e-6, True, s_xr, i + 1)
                split_parts("win")
                copy_v("win", v0, 4, bv0)
                split_parts("mla")
                copy_v("mla", vm, 0, None)
                for n in range(16):
                    j, g = n // 4, n % 4
                    b = 2 * (n % 3)
                    lo = WIN if j == 0 else 0
                    dve.wait_ge(s_sc["win"], i * 16 + n + 1)
                    src = PS[:, b:b + 2, 0:2 * WQ].rearrange("p b (h c) -> p b h c", h=2)[:, :, :, lo:WQ]
                    v.tensor_reduce(negmax[:, 4 * g:4 * g + 4, j], src, AX.X, ALU.max, negate=True)\
                     .then_inc(s_mx["win"], 1)
                split_max("win")
                copy_o_raw("win")
                normalise("win")
                for n, (j, h0, nh, per) in enumerate(MLA_MAX):
                    b = 2 * (n % 3)
                    keys = P * (j + 1)
                    dve.wait_ge(s_sc["mla"], i * len(MLA_MAX) + n + 1)
                    src = PS[:, b:b + 2, 0:per * keys].rearrange("p b (h c) -> p b h c", h=per)
                    v.tensor_reduce(negmax[:, h0:h0 + nh, j], src, AX.X, ALU.max, negate=True)\
                     .then_inc(s_mx["mla"], 1)
                split_max("mla")
                copy_o_raw("mla")
                normalise("mla")
                dve.wait_ge(s_mot, i + 1)
                link(v.tensor_tensor(xn[:].rearrange("p j d -> p (j d)"), PS[:, 6, :],
                                     xn[:].rearrange("p j d -> p (j d)"), ALU.add))
                norm(xn, tmp, 2, 1e-6, True, s_rr, i + 1)
                dve.wait_ge(s_out, i * 16 + 16)
                v.tensor_tensor(x1[:], x[:], xn[:], ALU.add).then_inc(s_x1, 1)
                dve.wait_ge(s_lg[0], i + 1)
                link(v.tensor_copy(top[:, 0], PS[:, 5, 0:NT * E].rearrange("p (j e) -> p j e", j=NT)))
                top_two(0)
                split_combine(0, 6)
                N0 = E * C0
                for n in range(N0):
                    dve.wait_ge(s_si[0], i * N0 + n + 1)
                    if n % C0 == 0:
                        dve.wait_ge(s_wb[0], i * E + n // C0 + 1)
                    if n >= 3:
                        dve.wait_ge(s_dn[0], i * N0 + n - 2)
                    v.tensor_tensor(hid_b[:, n % 3], hid_a[:, n % 3], PS[:, 4 + n // C0 % 2, :], ALU.mult)\
                     .then_inc(s_hid[0], 1)
                dve.wait_ge(s_yt[0], i + 1)
                dve.wait_ge(s_x1, i + 1)
                link(v.tensor_tensor(x1[:].rearrange("p j d -> p (j d)"), PS[:, 7, :],
                                     x1[:].rearrange("p j d -> p (j d)"), ALU.add))
                norm(x1, xn, 3, 1e-5, False, s_xn, i * 2 + 2)
                link(v.tensor_tensor(tmp[:], xn[:], xn[:], ALU.mult))
                link(v.tensor_reduce(mv[:, :, 0], tmp[:], AX.X, ALU.add))
                split_parts("rel")
                copy_v("rel", v0, 3, bv1)
                dve.wait_ge(s_dist, i + 1)
                dots = PS[:, 4, 0:NT * E].rearrange("p (j e) -> p j e", j=NT)
                link(v.tensor_scalar(top[:, 7], dots, -2.0, None, ALU.mult))
                link(v.tensor_tensor(top[:, 6], spread(mv[:, :, 0]),
                                     cnorm[:].rearrange("p (o e) -> p o e", o=1).to_broadcast([P, NT, E]), ALU.add))
                link(v.tensor_tensor(top[:, 7], top[:, 7], top[:, 6], ALU.add))
                v.tensor_scalar_max(top[:, 7], top[:, 7], 1e-12).then_inc(s_gs, 1)
                dve.wait_ge(s_pow, i * 5 + 5)
                top_two(1)
                split_combine(1, 5)
                with dve.Fori(0, NT) as lq:
                    dve.wait_ge(s_stk["rel"], i * 304 + 304)
                    v.tensor_copy(q_win[:], q_stack[:, :, bass.ds(lq * P, P)])
                    v.tensor_copy(rel_win[:], rel_stack[:, bass.ds(3 * P - lq * P, 640)]).then_inc(s_qw, 1)

                    def max_tile(t):
                        b = 2 * (t % 3)
                        dve.wait_ge(s_rs, i * 32 + lq * 8 + t + 1)
                        src = PS[:, b:b + 2, :].rearrange("p b (k c) -> p c (b k)", k=2)
                        if t >= 2:
                            dve.wait_ge(s_rmt, i * 32 + lq * 8 + t - 1)
                        v.tensor_reduce(mcol[:, t % 2], src, AX.X, ALU.max).then_inc(s_rm, 1)

                    def max_row(t):
                        dve.wait_ge(s_rmt, i * 32 + lq * 8 + t + 1)
                        v.tensor_reduce(cm[:], PS[:, 6, 0:2 * P].rearrange("p (c k) -> p c k", c=2), AX.X, ALU.max,
                                        negate=True).then_inc(s_rc, 1)
                        dve.wait_ge(s_rct, i * 32 + lq * 8 + t + 1)
                        src = PS[0:2, 6, 2 * P:3 * P]
                        if t >= 1:
                            dve.wait_ge(s_rsh, i * 32 + lq * 8 + t)
                        link2(v.tensor_copy(crow[0:2], src))
                        link2(v.tensor_tensor(crow_mid[:], src, crow[0:2], ALU.subtract))
                        v.tensor_copy(crow[32:34], crow_mid[:]).then_inc(s_rcs, 1)

                    cnt2 = [0]

                    def link2(ins):
                        cnt2[0] += 1
                        ins.then_inc(s_link2, 1)
                        dve.wait_ge(s_link2, i * 64 + lq * 16 + cnt2[0])

                    for t in range(NS + 1):
                        if t >= 1:
                            max_row(t - 1)
                        if t < NS:
                            max_tile(t)
                    dve.wait_ge(s_pv["rel"], i * 4 + lq + 1)
                    v.tensor_copy(o_raw[:, :, bass.ds(lq * P, P)],
                                  PS[:, 7, :].rearrange("p (g l) -> p g l", g=4)).then_inc(s_or["rel"], 1)
                normalise("rel")
                N1 = E * C1
                for n in range(N1):
                    e = n // C1
                    dve.wait_ge(s_si[1], i * N1 + n + 1)
                    v.scalar_tensor_tensor(hid_b[0:CW, n % 3], PS[0:CW, 2 * (n % 2) + 1, :],
                                           bu[:, e, n % C1:n % C1 + 1], hid_a[0:CW, n % 3],
                                           ALU.add, ALU.mult).then_inc(s_hu, 1)
                    dve.wait_ge(s_hu, i * N1 + n + 1)
                    if n % C1 == 0:
                        dve.wait_ge(s_wb[1], i * E + e + 1)
                    if n >= 3:
                        dve.wait_ge(s_dn[1], i * N1 + n - 2)
                    v.tensor_tensor(hid_c[0:CW, n % 3], hid_b[0:CW, n % 3], PS[0:CW, 4 + e % 2, :], ALU.mult)\
                     .then_inc(s_hid[1], 1)
                dve.wait_ge(s_yt[1], i + 1)
                v.tensor_tensor(x1[:].rearrange("p j d -> p (j d)"), PS[:, 7, :],
                                x1[:].rearrange("p j d -> p (j d)"), ALU.add).then_inc(s_x2, 1)
            assert cnt[0] == NLINK, cnt[0]

        @block.tensor
        def _(pe):
            mm = nc.tensor.matmul
            pe.wait_ge(s_load, NLOAD)
            pe.wait_ge(s_vset, 3)
            pe.wait_ge(s_rel_ld, 192)
            with pe.Fori(0, B) as i:
                def transpose_tiles(bank, src):
                    for j in range(NT):
                        last = nc.tensor.transpose(PS[:, bank, j * P:j * P + P], src[:, j, :], ident[:])
                    return last

                def by_token(bank, x_t, w, n):
                    for j in range(NT):
                        last = mm(PS[:, bank, j * n:j * n + n], x_t[:, j * P:j * P + P], w, start=True, stop=True)
                    return last

                def transpose_max(a, groups):
                    pe.wait_ge(s_mx[a], i * groups + groups)
                    nc.tensor.transpose(PS[:, 6, 0:P], negmax[:].rearrange("p h j -> p (h j)"), ident[:])\
                      .then_inc(s_mxt[a], 1)

                def finish(a):
                    for j in range(NT):
                        for g in range(4):
                            last = nc.tensor.transpose(PS[:, j, g * P:g * P + P], o_raw[:, g, j * P:j * P + P], ident[:])
                    last.then_inc(s_ort[a], 1)
                    pe.wait_ge(s_on[a], i + 1)
                    transpose_tiles(4, o_tok).then_inc(s_ot[a], 1)

                pe.wait_ge(s_xn, i * 2 + 1)
                transpose_tiles(0, xn).then_inc(s_tr, 1)
                pe.wait_ge(s_xr, i + 1)
                transpose_tiles(1, tmp).then_inc(s_tr, 1)
                pe.wait_ge(s_xnt, i * 3 + 1)
                mm(PS[:, 2, :], W["L0_attn_Wq"][:], xn_t[:], start=True, stop=True).then_inc(s_proj["win"], 1)
                mm(PS[:, 3, :], W["L0_attn_Wk"][:], xn_t[:], start=True, stop=True).then_inc(s_proj["win"], 1)
                by_token(4, xn_t, W["L0_attn_Wv"][:], D).then_inc(s_vproj["win"], 1)
                pe.wait_ge(s_xnt, i * 3 + 2)
                mm(PS[:, 5, :], W["L0_ffn_Wq"][:], h_t[:], start=True, stop=True).then_inc(s_proj["mla"], 1)
                mm(PS[0:LAT, 6, :], wdkv[:], h_t[:], start=True, stop=True).then_inc(s_lat, 1)
                pe.wait_ge(s_ct, i + 1)
                mm(PS[:, 7, :], wuk[:], c_t[:], start=True, stop=True).then_inc(s_proj["mla"], 1)
                by_token(0, c_t, wuv[:], D).then_inc(s_vproj["mla"], 1)

                pe.wait_ge(s_qkf["mla"], i * 2 + 2)
                pe.wait_ge(s_v["win"], i + 1)
                pe.wait_ge(s_v["mla"], i + 1)
                pe.wait_ge(s_stk["win"], i * 304 + 304)
                for n in range(16):
                    j, g = n // 4, n % 4
                    b = 2 * (n % 3)
                    lo = WIN if j == 0 else 0
                    if n >= 3:
                        pe.wait_ge(s_mx["win"], i * 16 + n - 2)
                    for r in range(4):
                        h = 4 * g + r
                        c = (r % 2) * WQ
                        out = PS[:, b + r // 2, c + lo:c + WQ]
                        mm(out, q_stack[:, h, j * P:j * P + P], k_stack[:, h, j * P - WIN + lo:j * P + P],
                           start=(r % 2 == 0), stop=True, skip_group_check=True)
                        last = mm(out, identb[:], band_qk[:, lo:WQ], start=False, stop=True, skip_group_check=True)
                    last.then_inc(s_sc["win"], 1)
                transpose_max("win", 16)
                pe.wait_ge(s_sh["win"], i * 32 + 32)

                def win_scores(n):
                    b = 3 * (n % 2)
                    if n >= 2:
                        pe.wait_ge(s_ex["win"], i * 8 + n - 1)
                    for r in range(2):
                        h = 2 * n + r
                        for kt in range(NT):
                            w = WQ if kt < NT - 1 else P
                            out = PS[:, b + r, kt * WQ:kt * WQ + w] if kt < NT - 1 else PS[:, b + 2, r * P:r * P + P]
                            first = kt == 0 or (kt == NT - 1 and r == 0)
                            mm(out, k_stack[:, h, kt * P:kt * P + P], q_stack[:, h, kt * P:kt * P + w],
                               start=first, stop=True, skip_group_check=True)
                            last = mm(out, identb[:], band_kq[:, 0:w], start=False, stop=True, skip_group_check=True)
                    last.then_inc(s_st["win"], 1)

                def win_pv(g):
                    pe.wait_ge(s_ex["win"], i * 8 + 2 * g + 2)
                    if g >= 2:
                        pe.wait_ge(s_or["win"], i * 4 + g - 1)
                    p4 = probs[:, g % 2 * 5120:g % 2 * 5120 + 2560].rearrange("p (r c) -> p r c", r=4)
                    for kt in range(NT):
                        w = WQ if kt < NT - 1 else P
                        for r in range(4):
                            last = mm(PS[32 * r:32 * r + 32, 6 + g % 2, kt * P:kt * P + w],
                                      v0[:, kt, 4 * g + r, :], p4[:, r, kt * WQ:kt * WQ + w],
                                      start=(kt == 0), stop=True, skip_group_check=True,
                                      tile_position=(0, 32 * r))
                    last.then_inc(s_pv["win"], 1)

                for n in range(8):
                    win_scores(n)
                    if n >= 2 and n % 2 == 0:
                        win_pv(n // 2 - 1)
                win_pv(3)
                pe.wait_ge(s_or["win"], i * 4 + 4)
                finish("win")

                pe.wait_ge(s_stk["mla"], i * 304 + 304)
                pe.wait_ge(s_otc["win"], i + 1)
                for n, (j, h0, nh, per) in enumerate(MLA_MAX):
                    b = 2 * (n % 3)
                    keys = P * (j + 1)
                    if n >= 3:
                        pe.wait_ge(s_mx["mla"], i * len(MLA_MAX) + n - 2)
                    for r in range(nh):
                        h = h0 + r
                        c = (r % per) * keys
                        mm(PS[:, b + r // per, c:c + keys], q_stack[:, h, j * P:j * P + P], k_stack[:, h, 0:keys],
                           start=(r % per == 0), stop=True, skip_group_check=True)
                        last = mm(PS[:, b + r // per, c + keys - P:c + keys], identb[:], causal_qk[:],
                                  start=False, stop=True, skip_group_check=True)
                    last.then_inc(s_sc["mla"], 1)
                transpose_max("mla", len(MLA_MAX))
                pe.wait_ge(s_sh["mla"], i * 32 + 32)

                def mla_scores(h):
                    b = 3 * (h % 2)
                    if h >= 2:
                        pe.wait_ge(s_ex["mla"], i * H + h - 1)
                    for kt, (bank, c, first) in enumerate(((0, 0, True), (1, 0, True), (2, 0, True), (1, 384, False))):
                        w = T - kt * P
                        mm(PS[:, b + bank, c:c + w], k_stack[:, h, kt * P:kt * P + P], q_stack[:, h, kt * P:T],
                           start=first, stop=True, skip_group_check=True)
                        last = mm(PS[:, b + bank, c:c + P], identb[:], causal_kq[:], start=False, stop=True,
                                  skip_group_check=True)
                    last.then_inc(s_st["mla"], 1)

                def mla_pv(g):
                    pe.wait_ge(s_ex["mla"], i * H + 4 * g + 4)
                    if g >= 2:
                        pe.wait_ge(s_or["mla"], i * 4 + g - 1)
                    p4 = probs[:, g % 2 * 5120:g % 2 * 5120 + 5120].rearrange("p (r c) -> p r c", r=4)
                    for kt, c in enumerate((0, 512, 1024, 896)):
                        w = T - kt * P
                        for r in range(4):
                            last = mm(PS[32 * r:32 * r + 32, 6 + g % 2, kt * P:T], vm[:, kt, 4 * g + r, :],
                                      p4[:, r, c:c + w], start=(kt == 0), stop=True, skip_group_check=True,
                                      tile_position=(0, 32 * r))
                    last.then_inc(s_pv["mla"], 1)

                for h in range(H):
                    mla_scores(h)
                    if h >= 5 and h % 4 == 1:
                        mla_pv(h // 4 - 1)
                mla_pv(3)
                pe.wait_ge(s_or["mla"], i * 4 + 4)
                finish("mla")
                pe.wait_ge(s_otc["mla"], i + 1)
                mm(PS[:, 5, :], W["L0_ffn_Wo"][:], o_t["mla"][:], start=True, stop=True).then_inc(s_mo, 1)
                pe.wait_ge(s_moc, i + 1)
                transpose_tiles(6, y_t.rearrange("p (j t) -> p j t", j=NT)).then_inc(s_mot, 1)
                pe.wait_ge(s_rr, i + 1)
                transpose_tiles(7, tmp).then_inc(s_rt, 1)
                pe.wait_ge(s_h2, i + 1)
                by_token(5, h_t, gate_w[:], E).then_inc(s_lg[0], 1)

                def spread_combine(k, e):
                    C = (C0, C1)[k]
                    if e >= 2:
                        pe.wait_ge(s_hid[k], i * E * C + (e - 1) * C)
                    mm(PS[:, 4 + e % 2, :], sel_w[:, e, :], wparts[:], start=True, stop=True).then_inc(s_wb[k], 1)

                def up0(n):
                    e, c = n // C0, n % C0
                    if n >= 4:
                        pe.wait_ge(s_si[0], i * E * C0 + n - 3)
                    mm(PS[:, n % 4, :], w1[:, e, c * P:c * P + P], h_t[:], start=True, stop=True)\
                      .then_inc(s_up[0], 1)

                for n in range(3):
                    up0(n)
                pe.wait_ge(s_cb[0], i + 1)
                for j in range(NT):
                    last = nc.tensor.transpose(PS[0:E, 6, j * P:j * P + P], top[:, 6, j, :], ident[:])
                last.then_inc(s_cbt[0], 1)
                pe.wait_ge(s_wp[0], i + 1)
                mm(PS[:, 6, :], W["L0_attn_Wo"][:], o_t["win"][:], start=True, stop=False, skip_group_check=True)
                for n in range(E * C0):
                    if n % C0 == 0:
                        spread_combine(0, n // C0)
                    if n + 3 < E * C0:
                        up0(n + 3)
                    pe.wait_ge(s_hid[0], i * E * C0 + n + 1)
                    last = mm(PS[:, 6, :], w2[:, n // C0, n % C0, :], hid_b[:, n % 3], start=False,
                              stop=(n == E * C0 - 1), skip_group_check=True)
                    last.then_inc(s_dn[0], 1)
                pe.wait_ge(s_dn[0], i * E * C0 + E * C0)
                pe.nop().then_inc(s_yo[0], 1)
                pe.wait_ge(s_yc[0], i + 1)
                transpose_tiles(7, y_t.rearrange("p (j t) -> p j t", j=NT)).then_inc(s_yt[0], 1)

                pe.wait_ge(s_xn, i * 2 + 2)
                transpose_tiles(0, xn).then_inc(s_tr, 1)
                pe.wait_ge(s_xnt, i * 3 + 3)
                mm(PS[:, 1, :], W["L1_attn_Wq"][:], xn_t[:], start=True, stop=True).then_inc(s_proj["rel"], 1)
                mm(PS[:, 2, :], W["L1_attn_Wk"][:], xn_t[:], start=True, stop=True).then_inc(s_proj["rel"], 1)
                by_token(3, xn_t, W["L1_attn_Wv"][:], D).then_inc(s_vproj["rel"], 1)
                by_token(4, xn_t, cen_t[:], E).then_inc(s_dist, 1)
                pe.wait_ge(s_cb[1], i + 1)
                for j in range(NT):
                    last = nc.tensor.transpose(PS[0:E, 5, j * P:j * P + P], top[:, 6, j, :], ident[:])
                last.then_inc(s_cbt[1], 1)
                with pe.Fori(0, NT) as lq:
                    pe.wait_ge(s_wp[1], i + 1)
                    pe.wait_ge(s_qkf["rel"], i * 2 + 2)
                    pe.wait_ge(s_v["rel"], i + 1)
                    pe.wait_ge(s_qw, i * 4 + lq + 1)
                    base = i * 32 + lq * 8

                    def scores(t, half):
                        lb, hh = t // 2, t % 2
                        bank = 2 * (t % 3) + half
                        if half == 0 and t >= 3:
                            pe.wait_ge(s_ex["rel"], base + t - 2)
                        qs = q_win[:, hh * HT:hh * HT + HT, lb * LB:lb * LB + LB]
                        out = PS[:, bank, :].rearrange("p (k h l) -> p k h l", k=2, h=HT)
                        for k in range(2):
                            kt = 2 * half + k
                            for h in range(HT):
                                mm(out[:, k, h, :], k_stack[:, hh * HT + h, kt * P:kt * P + P], qs[:, h, :],
                                   start=(k == 0 and h == 0), stop=True, skip_group_check=True)
                            for u in range(LB // 2):
                                c = kt * P + P - 1 - (lb * LB + 2 * u)
                                last = mm(out[:, k, :, 2 * u:2 * u + 2], rel_win[:, c:c + P], qs[:, :, 2 * u:2 * u + 2],
                                          start=False, stop=True, skip_group_check=True)
                        if half == 1:
                            last.then_inc(s_rs, 1)

                    def transpose_tile_max(t):
                        pe.wait_ge(s_rm, base + t + 1)
                        for c in range(2):
                            last = nc.tensor.transpose(PS[:, 6, c * P:c * P + P], mcol[:, t % 2, c * P:c * P + P],
                                                       ident[:])
                        last.then_inc(s_rmt, 1)

                    def transpose_row_max(t):
                        pe.wait_ge(s_rc, base + t + 1)
                        nc.tensor.transpose(PS[0:2, 6, 2 * P:3 * P], cm[:], ident[:]).then_inc(s_rct, 1)

                    def shift(t):
                        pe.wait_ge(s_rcs, base + t + 1)
                        for k in range(4):
                            for c in range(2):
                                last = mm(PS[:, 2 * (t % 3) + k // 2, (k % 2) * 2 * P + c * P:(k % 2) * 2 * P + c * P + P],
                                          sel_c[:, c, :], crow[:], start=False, stop=True, skip_group_check=True)
                        last.then_inc(s_rsh, 1)

                    for t in range(NS + 2):
                        if t < NS:
                            scores(t, 0)
                        if t >= 2:
                            shift(t - 2)
                        if 1 <= t <= NS:
                            transpose_tile_max(t - 1)
                        if t < NS:
                            scores(t, 1)
                        if 1 <= t <= NS:
                            transpose_row_max(t - 1)
                    pe.wait_ge(s_ex["rel"], base + NS)
                    pr = probs[:, 0:NT * H * P].rearrange("p (k h l) -> p k h l", k=NT, h=H)
                    for g in range(4):
                        for kt in range(NT):
                            for r in range(4):
                                last = mm(PS[32 * r:32 * r + 32, 7, g * P:g * P + P], v0[:, kt, 4 * g + r, :],
                                          pr[:, kt, 4 * g + r, :], start=(g == 0 and kt == 0), stop=True,
                                          skip_group_check=True, tile_position=(0, 32 * r))
                    last.then_inc(s_pv["rel"], 1)
                pe.wait_ge(s_or["rel"], i * 4 + 4)
                finish("rel")

                def up1(n):
                    e, c = n // C1, n % C1
                    if n >= 2:
                        pe.wait_ge(s_hu, i * E * C1 + n - 1)
                    mm(PS[0:CW, 2 * (n % 2), :], wg[:, e, c * CW:c * CW + CW], xn_t[:], start=True, stop=True)
                    mm(PS[0:CW, 2 * (n % 2) + 1, :], wu[:, e, c * CW:c * CW + CW], xn_t[:], start=True, stop=True)\
                      .then_inc(s_up[1], 1)

                pe.wait_ge(s_otc["rel"], i + 1)
                mm(PS[:, 6, :], W["L1_attn_Wo"][:], o_t["rel"][:], start=True, stop=False, skip_group_check=True)
                mm(PS[:, 6, :], b2[:], wt_full[:], start=False, stop=False, skip_group_check=True)
                up1(0)
                for n in range(E * C1):
                    if n % C1 == 0:
                        spread_combine(1, n // C1)
                    if n + 1 < E * C1:
                        up1(n + 1)
                    pe.wait_ge(s_hid[1], i * E * C1 + n + 1)
                    last = mm(PS[:, 6, :], wd[:, n // C1, n % C1, :], hid_c[0:CW, n % 3], start=False,
                              stop=(n == E * C1 - 1), skip_group_check=True)
                    last.then_inc(s_dn[1], 1)
                pe.wait_ge(s_dn[1], i * E * C1 + E * C1)
                pe.nop().then_inc(s_yo[1], 1)
                pe.wait_ge(s_yc[1], i + 1)
                transpose_tiles(7, y_t.rearrange("p (j t) -> p j t", j=NT)).then_inc(s_yt[1], 1)


_TRANSPOSED = ["L0_attn_Wq", "L0_attn_Wk", "L0_attn_Wv", "L0_attn_Wo",
               "L1_attn_Wq", "L1_attn_Wk", "L1_attn_Wv", "L1_attn_Wo"]


def kernel(**inputs):
    import numpy as np
    import concourse.bacc as bacc
    from concourse.bass_utils import run_bass_kernel_spmd

    nc = bacc.Bacc("TRN2", target_bir_lowering=False, num_devices=1)
    arrays, dram = {}, {}
    for name, a in inputs.items():
        a = np.asarray(a)
        if name in _TRANSPOSED:
            a = a.T
        if name in ("L1_ffn_bg", "L1_ffn_b1"):
            a = a.reshape(-1, a.shape[1] // 3).T
        arrays[name] = np.ascontiguousarray(a)
    arrays["centroid_t"] = np.ascontiguousarray(arrays["L1_ffn_centroid"].T)
    arrays["rel_emb_t"] = np.ascontiguousarray(arrays.pop("L1_attn_rel_emb").T)
    for name, a in arrays.items():
        dram[name] = nc.dram_tensor("in_" + name, a.shape, mybir.dt.from_np(a.dtype), kind="ExternalInput").ap()
    dram["L1_attn_rel_emb"] = inputs["L1_attn_rel_emb"]
    x = arrays["L0_attn_x"]
    dram["out"] = nc.dram_tensor("out", x.shape, mybir.dt.from_np(x.dtype), kind="ExternalOutput").ap()
    two_layers(nc, dram)
    r = run_bass_kernel_spmd(nc, [{"in_" + n: a for n, a in arrays.items()}], core_ids=[0])
    return r.results[0]["out"]
```

```python
from contextlib import ExitStack

import concourse.bass as bass
from concourse import mybir

F32 = mybir.dt.float32
BF16 = mybir.dt.bfloat16
ALU = mybir.AluOpType
ACT = mybir.ActivationFunctionType
AX = mybir.AxisListType


def two_layers(nc, dram):
    B, T, D = dram["L0_attn_x"].shape
    H, DH = 16, 8
    HT = H // 2
    LB = 32
    P = 128
    NT = T // P
    E = dram["L0_ffn_gate_w"].shape[1]
    F0 = dram["L0_ffn_w1"].shape[2]
    F1 = dram["L1_ffn_Wg"].shape[2]
    C0 = F0 // P
    C1 = 3
    CW = F1 // C1
    LAT = dram["L0_ffn_Wdkv"].shape[1]
    WIN = 32
    WQ = P + WIN
    SCALE = float(DH) ** -0.5
    LOW = -1e30
    NREL = dram["L1_attn_rel_emb"].shape[0]
    QP = 3 * T + 1
    VW = 16
    SHIFT = 112
    NCONST = 28
    MLA_MAX = [(j, h0, n, n // 2) for half in (0, HT) for j, n in ((0, 8), (1, 4), (2, 2), (3, 2))
               for h0 in range(half, half + HT, n)]
    WIN_MAX = [(j, h0) for half in (0, HT) for j in range(NT) for h0 in range(half, half + HT, 4)]
    NS = NT * (P // LB) * 2
    NSQ = NS // NT

    ctx = ExitStack()
    with ctx:
        def sb(name, shape, dt=F32):
            return ctx.enter_context(nc.sbuf_tensor(name, shape, dt))

        def sem(name):
            return ctx.enter_context(nc.semaphore(name))

        names = ["L0_attn_Wq", "L0_attn_Wk", "L0_attn_Wv", "L0_attn_Wo", "L0_ffn_Wq", "L0_ffn_Wo",
                 "L1_attn_Wq", "L1_attn_Wk", "L1_attn_Wv", "L1_attn_Wo"]
        W = {n: sb("w_" + n, [P, D]) for n in names}
        wdkv = sb("wdkv", [P, LAT])
        wuk = sb("wuk", [LAT, D])
        wuv = sb("wuv", [LAT, D])
        gate_w = sb("gate_w", [P, E])
        w1 = sb("w1", [P, E, F0])
        w2 = sb("w2", [P, E, C0, D])
        wg = sb("wg", [P, E, F1])
        wu = sb("wu", [P, E, F1])
        wd = sb("wd", [CW, E, C1, D])
        cen_t = sb("cen_t", [P, E])
        b2 = sb("b2", [E, D])
        cols = ["L0_attn_bq", "L0_attn_bk", "L0_attn_bo", "L1_attn_bq", "L1_attn_bk", "L1_attn_bo",
                "L0_ffn_g1", "L0_ffn_g2"]
        col = {n: sb("c_" + n, [P, 1]) for n in cols}
        bg = sb("bg", [CW, E, C1])
        bu = sb("bu", [CW, E, C1])
        bv0 = sb("bv0", [P, D])
        bv1 = sb("bv1", [P, D])
        bk0s = sb("bk0s", [P, 1])
        bk1s = sb("bk1s", [P, 1])
        cnorm = sb("cnorm", [P, E])
        ident = sb("ident", [P, P])
        identb = sb("identb", [P, P], BF16)
        causal_qk = sb("causal_qk", [P, P], BF16)
        causal_kq = sb("causal_kq", [P, P], BF16)
        band_qk = sb("band_qk", [P, WQ], BF16)
        band_kq = sb("band_kq", [P, WQ], BF16)
        sel_w = sb("sel_w", [P, E, P], BF16)
        sel_c = sb("sel_c", [P, 2, P], BF16)
        rev = sb("rev", [P, NT, E])
        power = sb("power", [P, 2, NT * E])
        rel_stack = sb("rel_stack", [P, 2 * T], BF16)
        q_stack = sb("q_stack", [P, H, T], BF16)
        k_stack = sb("k_stack", [P, H, T], BF16)
        probs = sb("probs", [P, 2 * 4 * 1280])
        v0 = sb("v0", [P, NT, H, VW])
        vm = sb("vm", [P, NT, H, VW])
        x = sb("x", [P, NT, D])
        xn = sb("xn", [P, NT, D])
        x1 = sb("x1", [P, NT, D])
        tmp = sb("tmp", [P, NT, D])
        xn_t = sb("xn_t", [P, T])
        h_t = sb("h_t", [P, T])
        c_t = sb("c_t", [LAT, T])
        q_f = sb("q_f", [P, T])
        k_f = sb("k_f", [P, T])
        q_parts = sb("q_parts", [P, 2 * QP], BF16)
        q_plain = sb("q_plain", [P, 3, T], BF16)
        k_parts = sb("k_parts", [P, 3, T], BF16)
        o_raw = sb("o_raw", [P, 4, T])
        o_t = {"win": sb("o_t_win", [P, T]), "mla": sb("o_t_mla", [P, T])}
        o_t["rel"] = o_t["mla"]
        o_tok = tmp
        stats = sb("stats", [P, NT, 6])
        mv = sb("mv", [P, NT, 2])
        rstd = sb("rstd", [P, NT])
        rvar = sb("rvar", [P, NT])
        wt_full = sb("wt_full", [E, T])
        wt_mid = sb("wt_mid", [E, T], BF16)
        negmax = sb("negmax", [P, 2, 4 * HT, NT])
        cpart = sb("cpart", [NT * HT, 2, 2, P], BF16)
        rden = sb("rden", [P, NT, H])
        top = sb("top", [P, 8, NT, E])
        tc = sb("tc", [P, 8, NT])
        wparts = sb("wparts", [P, T], BF16)
        wt_f = c_t[0:E, :]
        mcol = sb("mcol", [P, 2, HT * LB])
        cm = sb("cm", [P, 2])
        pause = sb("pause", [P, 1])
        crow = sb("crow", [P, P], BF16)
        crow_mid = sb("crow_mid", [2, P])
        hid_a = probs[:, 0:3 * T].rearrange("p (n t) -> p n t", n=3)
        hid_b = probs[:, 3 * T:6 * T].rearrange("p (n t) -> p n t", n=3)
        hid_c = probs[:, 6 * T:9 * T].rearrange("p (n t) -> p n t", n=3)
        y_t = probs[:, 9 * T:10 * T]
        PS = ctx.enter_context(nc.psum_tensor("ps", [P, 8, 512], F32))

        scr = {(a, n): nc.dram_tensor(f"scr_{a}_{n}", [3 * DH, H, T], BF16, kind="Internal").ap()
               for a, names in (("win", ("q", "k")), ("mla", ("q", "k")), ("rel", ("qe", "qo", "k")))
               for n in names}
        zrow_d = nc.dram_tensor("zrow_d", [2, H * T], BF16, kind="Internal").ap()
        rel_d = nc.dram_tensor("rel_d", [3, DH, 1024], BF16, kind="Internal").ap()

        ATT = ("win", "mla", "rel")
        s_load = sem("weights_loaded")
        s_relx = sem("rel_table_loaded")
        s_const = sem("constants_made")
        s_vset = sem("vector_setup")
        s_rel_sp = sem("rel_parts_stored")
        s_rel_ld = sem("rel_stack_loaded")
        s_x = sem("x_loaded")
        s_link = sem("vector_chain")
        s_pow = sem("powers_done")
        s_gs = sem("power_inputs_ready")
        s_link0 = sem("vector_setup_chain")
        s_xn = sem("xn_done")
        s_xr = sem("xr_done")
        s_tr = sem("xn_transposed")
        s_xnt = sem("xn_t_copied")
        s_proj = {a: sem("qk_projected_" + a) for a in ATT}
        s_vproj = {a: sem("v_projected_" + a) for a in ATT}
        s_lat = sem("latent_projected")
        s_ct = sem("c_t_copied")
        s_qkf = {a: sem("qk_copied_" + a) for a in ATT}
        s_parts = {a: sem("parts_split_" + a) for a in ATT}
        s_v = {a: sem("v_copied_" + a) for a in ATT}
        s_scr = {a: sem("parts_stored_" + a) for a in ATT}
        s_stk = {a: sem("q_stack_loaded_" + a) for a in ATT}
        s_zero = sem("upper_key_rows_cleared")
        s_stkk = {a: sem("k_stack_loaded_" + a) for a in ATT}
        s_sc = {a: sem("scores_for_max_" + a) for a in ("win", "mla")}
        s_mx = {a: sem("max_taken_" + a) for a in ("win", "mla")}
        s_mxt = {a: sem("max_transposed_" + a) for a in ("win", "mla")}
        s_cp = {a: sem("max_split_" + a) for a in ("win", "mla")}
        s_sh = {(a, n): sem(f"shift_rows_{n}_loaded_{a}") for a in ("win", "mla") for n in range(2)}
        s_st = {a: sem("scores_t_" + a) for a in ("win", "mla")}
        s_ex = {a: sem("probs_ready_" + a) for a in ATT}
        s_pv = {a: sem("pv_done_" + a) for a in ATT}
        s_or = {a: sem("o_raw_copied_" + a) for a in ATT}
        s_ort = {a: sem("o_raw_transposed_" + a) for a in ATT}
        s_on = {a: sem("o_normalised_" + a) for a in ATT}
        s_ot = {a: sem("o_transposed_" + a) for a in ATT}
        s_otc = {a: sem("o_t_copied_" + a) for a in ATT}
        s_mo = sem("mla_out_projected")
        s_moc = sem("mla_out_copied")
        s_mot = sem("mla_out_transposed")
        s_rr = sem("moe_input_normed")
        s_rt = sem("moe_input_transposed")
        s_h2 = sem("moe_input_t_copied")
        s_lg = {0: sem("logits_0"), 1: sem("logits_1")}
        s_gd = {0: sem("gate_gap_0"), 1: sem("gate_gap_1")}
        s_ge = {0: sem("gate_exp_0"), 1: sem("gate_exp_1")}
        s_cb = {0: sem("combine_0"), 1: sem("combine_1")}
        s_cbt = {0: sem("combine_transposed_0"), 1: sem("combine_transposed_1")}
        s_wp = {0: sem("combine_split_0"), 1: sem("combine_split_1")}
        s_wb = {0: sem("combine_spread_0"), 1: sem("combine_spread_1")}
        s_up = {0: sem("up_done_0"), 1: sem("up_done_1")}
        s_si = {0: sem("silu_done_0"), 1: sem("silu_done_1")}
        s_hu = sem("gated_up_1")
        s_hid = {0: sem("hidden_scaled_0"), 1: sem("hidden_scaled_1")}
        s_dn = {0: sem("down_done_0"), 1: sem("down_done_1")}
        s_yo = {0: sem("layer_out_done_0"), 1: sem("layer_out_done_1")}
        s_yc = {0: sem("layer_out_copied_0"), 1: sem("layer_out_copied_1")}
        s_yt = {0: sem("layer_out_transposed_0"), 1: sem("layer_out_transposed_1")}
        s_dist = sem("squared_distance")
        s_x1 = sem("x1_done")
        s_x2 = sem("x2_done")
        s_out = sem("zero_rows_and_out_stored")
        s_rs = sem("rel_scores")
        s_rm = sem("rel_max_over_key_tiles")
        s_rmt = sem("rel_max_transposed")
        s_rc = sem("rel_max_over_keys")
        s_rct = sem("rel_max_row_transposed")
        s_rcs = sem("rel_max_split")
        s_rsh = sem("rel_scores_shifted")
        s_link2 = sem("rel_vector_chain")

        block = ctx.enter_context(nc.Block())

        col_loads = [(col[n][:], dram[n].rearrange("(p o) -> p o", o=1)) for n in cols]
        loads = [(W[n][:], dram[n]) for n in names] + [
            (wdkv[:], dram["L0_ffn_Wdkv"]), (wuk[:], dram["L0_ffn_Wuk"]), (wuv[:], dram["L0_ffn_Wuv"]),
            (gate_w[:], dram["L0_ffn_gate_w"]), (cen_t[:], dram["centroid_t"]), (b2[:], dram["L1_ffn_b2"]),
            (w1[:], dram["L0_ffn_w1"].rearrange("e c f -> c e f")),
            (wg[:], dram["L1_ffn_Wg"].rearrange("e c f -> c e f")),
            (wu[:], dram["L1_ffn_W1"].rearrange("e c f -> c e f")),
            (bv0[:], dram["L0_attn_bv"].rearrange("(o d) -> o d", o=1).to_broadcast([P, D])),
            (bv1[:], dram["L1_attn_bv"].rearrange("(o d) -> o d", o=1).to_broadcast([P, D])),
            (tmp[:].rearrange("p a b -> p (a b)"),
             dram["L1_ffn_centroid"].rearrange("(o e) d -> o (e d)", o=1)[:, 0:4 * D].to_broadcast([P, 4 * D])),
            (x1[:].rearrange("p a b -> p (a b)"),
             dram["L1_ffn_centroid"].rearrange("(o e) d -> o (e d)", o=1)[:, 4 * D:8 * D].to_broadcast([P, 4 * D])),
        ] + col_loads
        for e in range(E):
            loads.append((w2[:, e, :, :], dram["L0_ffn_w2"][e].rearrange("(c p) d -> p c d", p=P)))
            loads.append((wd[:, e, :, :], dram["L1_ffn_W2"][e].rearrange("(c p) d -> p c d", p=CW)))
        bias_loads = [(bg[:], dram["L1_ffn_bg"]),
                      (bu[:], dram["L1_ffn_b1"])]
        NLOAD = 16 * (len(loads) + 2)
        SCR = {"win": 16 * 6, "mla": 16 * 6, "rel": 16 * 9}
        QST = {"win": 16 * 4, "mla": 16 * 4, "rel": 16 * 7}
        KST = {"win": 16 * 3, "mla": 16 * 3, "rel": 16 * 6}

        @block.sync
        def _(sp):
            rel_t = dram["rel_emb_t"]
            tail = NREL - 256
            relx = probs[0:DH, 0:1024]
            sp.dma_start(relx[:, 0:256], rel_t[:, tail:NREL]).then_inc(s_relx, 16)
            sp.dma_start(relx[:, 256:256 + NREL], rel_t).then_inc(s_relx, 16)
            with nc.allow_non_contiguous_dma(reason="one row repeated, and short biases"):
                for dst, src in bias_loads:
                    sp.dma_start(dst.rearrange("p e c -> p (e c)"), src).then_inc(s_load, 16)
                for dst, src in loads:
                    sp.dma_start(dst, src).then_inc(s_load, 16)
            sp.wait_ge(s_vset, 1)
            sp.dma_start(zrow_d.rearrange("a (b c) -> (a b) c", c=P), wparts[:, 0:P]).then_inc(s_out, 16)
            sp.wait_ge(s_vset, 2)
            sp.wait_ge(s_out, 16)
            sp.dma_start(k_stack[64:SHIFT].rearrange("p h t -> p (h t)"),
                         zrow_d[0:1].to_broadcast([SHIFT - 64, H * T])).then_inc(s_zero, 16)
            for p in range(3):
                sp.dma_start(rel_d[p], k_stack[0:DH, 2 * p:2 * p + 2, :].rearrange("p a b -> p (a b)"))\
                  .then_inc(s_rel_sp, 16)
            sp.wait_ge(s_rel_sp, 48)
            for n in range(2):
                for s, p in enumerate((0, 1, 2, 0, 1, 0)):
                    sp.dma_start(rel_stack[64 * n + DH * s:64 * n + DH * s + DH, n:2 * T],
                                 rel_d[p][:, 0:2 * T - n]).then_inc(s_rel_ld, 16)
            sp.wait_ge(s_load, NLOAD)
            sp.wait_ge(s_vset, 3)
            sp.wait_ge(s_out, 16)
            with sp.Fori(0, B) as i:
                def store_parts(a):
                    sp.wait_ge(s_parts[a], i * 2 + 2)
                    for p in range(3):
                        if a == "rel":
                            parts = (("qe", q_parts[:, p * T:p * T + T]),
                                     ("qo", q_parts[:, 3 * T + p * T:3 * T + p * T + T]))
                        else:
                            parts = (("q", q_plain[:, p, :]),)
                        for n, src in parts + (("k", k_parts[:, p, :]),):
                            dst = scr[a, n][DH * p:DH * p + DH].rearrange("d h t -> h d t")
                            sp.dma_start(dst, src).then_inc(s_scr[a], 16)

                def load_q_stack(a):
                    sp.wait_ge(s_scr[a], i * SCR[a] + SCR[a])
                    sp.dma_start(q_stack[SHIFT:SHIFT + 2].rearrange("p h t -> p (h t)"), zrow_d)\
                      .then_inc(s_stk[a], 16)
                    for n, name in enumerate(("qe", "qo") if a == "rel" else ("q",)):
                        for s, m, p in ((0, 3, 0), (3, 2, 1), (5, 1, 2)):
                            r = 64 * n + DH * s
                            src = scr[a, name][DH * p:DH * p + DH].rearrange("(o d) h t -> o d (h t)", o=1)
                            sp.dma_start(q_stack[r:r + DH * m], src.to_broadcast([m, DH, H * T]))\
                              .then_inc(s_stk[a], 16)

                def load_shift(a, half):
                    sp.wait_ge(s_cp[a], i * 2 + half + 1)
                    for p in range(2):
                        dst = q_stack[SHIFT + p:SHIFT + p + 1, half * HT:half * HT + HT]\
                            .rearrange("o h (j q) -> o (h j) q", j=NT)
                        sp.dma_start(dst, cpart[:, half, p, :]).then_inc(s_sh[a, half], 16)

                sp.dma_start(x[:], dram["L0_attn_x"][i].rearrange("(j p) d -> p j d", p=P)).then_inc(s_x, 16)
                store_parts("win")
                load_q_stack("win")
                store_parts("mla")
                load_shift("win", 0)
                load_shift("win", 1)
                sp.wait_ge(s_pv["win"], i * 4 + 4)
                load_q_stack("mla")
                load_shift("mla", 0)
                load_shift("mla", 1)
                store_parts("rel")
                sp.wait_ge(s_pv["mla"], i * 4 + 4)
                load_q_stack("rel")
                sp.wait_ge(s_rsh, i * NS + NS)
                sp.dma_start(k_stack[64:SHIFT].rearrange("p h t -> p (h t)"),
                             zrow_d[0:1].to_broadcast([SHIFT - 64, H * T])).then_inc(s_zero, 16)
                sp.wait_ge(s_x2, i + 1)
                sp.dma_start(dram["out"][i].rearrange("(j p) d -> p j d", p=P), x1[:]).then_inc(s_out, 16)
            sp.wait_ge(s_out, 16 * B + 16)

        @block.gpsimd
        def _(pool):
            made = [0]

            def done(ins):
                made[0] += 1
                ins.then_inc(s_const, 1)

            def after():
                pool.wait_ge(s_const, made[0])

            done(pool.memset(ident[:], 0.0))
            done(pool.memset(causal_qk[:], 0.0))
            done(pool.memset(causal_kq[:], 0.0))
            done(pool.memset(band_qk[:], 0.0))
            done(pool.memset(band_kq[:], 0.0))
            done(pool.memset(sel_w[:], 0.0))
            done(pool.memset(sel_c[:], 0.0))
            done(pool.memset(power[:, 0, :], 0.5))
            done(pool.memset(power[:, 1, :], -0.5))
            for e in range(E):
                done(pool.memset(rev[:, :, e:e + 1], float(E - e)))
            after()

            def keep(t, op, fill, base, pattern, mult):
                done(pool.affine_select(out=t, in_=t, compare_op=op, fill=fill, base=base,
                                        pattern=pattern, channel_multiplier=mult))

            keep(ident[:], ALU.not_equal, 1.0, 0, [[-1, P]], 1)
            keep(causal_qk[:], ALU.is_ge, LOW, 0, [[-1, P]], 1)
            keep(causal_kq[:], ALU.is_ge, LOW, 0, [[1, P]], -1)
            keep(band_qk[:], ALU.is_ge, LOW, WIN, [[-1, WQ]], 1)
            keep(band_kq[:], ALU.is_ge, LOW, 0, [[1, WQ]], -1)
            for n in range(3):
                keep(sel_w[:], ALU.not_equal, 1.0, -32 * n, [[-1, E], [0, P]], 1)
                after()
            for n in range(2):
                keep(sel_c[:], ALU.not_equal, 1.0, -32 * n, [[-1, 2], [0, P]], 1)
                after()
            keep(band_qk[:], ALU.is_ge, LOW, WIN - 1 - WIN, [[1, WQ]], -1)
            keep(band_kq[:], ALU.is_ge, LOW, WIN - 1, [[-1, WQ]], 1)
            with pool.Fori(0, B) as i:
                def power_of(n):
                    pool.wait_ge(s_gs, i * 5 + n + 1)
                    if n == 4:
                        nc.gpsimd.tensor_tensor(top[:, 0], top[:, 7],
                                                power[:, 0, :].rearrange("p (j e) -> p j e", e=E),
                                                ALU.pow).then_inc(s_pow, 1)
                    else:
                        nc.gpsimd.tensor_tensor(rstd[:], rvar[:], power[:, 1, 0:NT], ALU.pow).then_inc(s_pow, 1)

                power_of(0)
                power_of(1)
                power_of(2)
                power_of(3)
                power_of(4)

        @block.scalar
        def _(act):
            def ident_of(out, in_, bias=0.0, scale=1.0):
                return nc.scalar.activation(out, in_, ACT.Identity, bias=bias, scale=scale)

            act.wait_ge(s_load, NLOAD)
            act.wait_ge(s_vset, 3)
            with act.Fori(0, B) as i:
                def copy_qk(a, qbank, kbank, bq, bks):
                    if a != "win":
                        act.wait_ge(s_parts[{"mla": "win", "rel": "mla"}[a]], i * 2 + 2)
                    act.wait_ge(s_proj[a], i * 2 + 1)
                    ident_of(q_f[:], PS[:, qbank, :], bias=bq).then_inc(s_qkf[a], 1)
                    act.wait_ge(s_proj[a], i * 2 + 2)
                    ident_of(k_f[:], PS[:, kbank, :], bias=bks, scale=SCALE).then_inc(s_qkf[a], 1)

                def load_k_stack(a):
                    act.wait_ge(s_scr[a], i * SCR[a] + SCR[a])
                    for n in range(2 if a == "rel" else 1):
                        for s, m in ((0, 3), (3, 2), (5, 1)):
                            r = 64 * n + DH * s
                            act.dma_start(k_stack[r:r + DH * m], scr[a, "k"][0:DH * m]).then_inc(s_stkk[a], 16)

                act.wait_ge(s_tr, i * 3 + 1)
                ident_of(xn_t[:], PS[:, 0, :]).then_inc(s_xnt, 1)
                act.wait_ge(s_tr, i * 3 + 2)
                ident_of(h_t[:], PS[:, 1, :], scale=col["L0_ffn_g1"][:, 0:1]).then_inc(s_xnt, 1)
                act.wait_ge(s_lat, i + 1)
                ident_of(c_t[:], PS[0:LAT, 6, :]).then_inc(s_ct, 1)
                copy_qk("win", 2, 3, col["L0_attn_bq"][:, 0:1], bk0s[:, 0:1])
                copy_qk("mla", 5, 7, 0.0, 0.0)
                load_k_stack("win")
                for n in range(H // 2):
                    if n >= 4 and n % 2 == 0:
                        act.wait_ge(s_pv["win"], i * 4 + n // 2 - 1)
                    act.wait_ge(s_st["win"], i * (H // 2) + n + 1)
                    b = 3 * (n % 2)
                    p4 = probs[:, (n // 2) % 2 * 5120:(n // 2) % 2 * 5120 + 2560].rearrange("p (r c) -> p r c", r=4)
                    p2 = p4[:, 2 * (n % 2):2 * (n % 2) + 2, :]
                    nc.scalar.activation(p2[:, :, 0:3 * WQ], PS[:, b:b + 2, 0:3 * WQ], ACT.Exp)
                    nc.scalar.activation(p2[:, :, 3 * WQ:3 * WQ + P],
                                         PS[:, b + 2, 0:2 * P].rearrange("p (r c) -> p r c", r=2),
                                         ACT.Exp).then_inc(s_ex["win"], 1)
                act.wait_ge(s_pv["win"], i * 4 + 4)
                load_k_stack("mla")
                for h in range(H):
                    if h >= 8 and h % 4 == 0:
                        act.wait_ge(s_pv["mla"], i * 4 + h // 4 - 1)
                    act.wait_ge(s_st["mla"], i * H + h + 1)
                    b = 3 * (h % 2)
                    o = (h // 4) % 2 * 5120 + (h % 4) * 1280
                    nc.scalar.activation(probs[:, o:o + 1280],
                                         PS[:, b:b + 3, :].rearrange("p b c -> p (b c)")[:, 0:1280],
                                         ACT.Exp).then_inc(s_ex["mla"], 1)
                act.wait_ge(s_mo, i + 1)
                ident_of(y_t, PS[:, 5, :]).then_inc(s_moc, 1)
                act.wait_ge(s_rt, i + 1)
                ident_of(h_t[:], PS[:, 7, :], scale=col["L0_ffn_g2"][:, 0:1]).then_inc(s_h2, 1)
                act.wait_ge(s_gd[0], i + 1)
                nc.scalar.activation(tc[:, 5], tc[:, 4], ACT.Exp).then_inc(s_ge[0], 1)
                N0 = E * C0
                for n in range(N0):
                    act.wait_ge(s_up[0], i * N0 + n + 1)
                    if n >= 3:
                        act.wait_ge(s_hid[0], i * N0 + n - 2)
                    nc.scalar.activation(hid_a[:, n % 3], PS[:, n % 4, :], ACT.Silu).then_inc(s_si[0], 1)
                act.wait_ge(s_yo[0], i + 1)
                ident_of(y_t, PS[:, 6, :], bias=col["L0_attn_bo"][:, 0:1]).then_inc(s_yc[0], 1)
                act.wait_ge(s_tr, i * 3 + 3)
                ident_of(xn_t[:], PS[:, 0, :]).then_inc(s_xnt, 1)
                copy_qk("rel", 1, 2, col["L1_attn_bq"][:, 0:1], bk1s[:, 0:1])
                load_k_stack("rel")
                act.wait_ge(s_gd[1], i + 1)
                nc.scalar.activation(tc[:, 5], tc[:, 4], ACT.Exp).then_inc(s_ge[1], 1)
                pr = probs[:, 0:NT * H * P].rearrange("p (k h l) -> p k h l", k=NT, h=H)
                for t in range(NS):
                    q, hh = t // 2, t % 2
                    if t >= NSQ and t % NSQ == 0:
                        act.wait_ge(s_pv["rel"], i * 4 + t // NSQ)
                    act.wait_ge(s_rsh, i * NS + t + 1)
                    b = 2 * (t % 3)
                    l = q % (P // LB) * LB
                    nc.scalar.activation(pr[:, :, hh * HT:hh * HT + HT, l:l + LB],
                                         PS[:, b:b + 2, :].rearrange("p b (k h l) -> p (b k) h l", k=2, h=HT),
                                         ACT.Exp).then_inc(s_ex["rel"], 1)
                N1 = E * C1
                for n in range(N1):
                    act.wait_ge(s_up[1], i * N1 + n + 1)
                    if n >= 3:
                        act.wait_ge(s_hu, i * N1 + n - 2)
                    nc.scalar.activation(hid_a[0:CW, n % 3], PS[0:CW, 2 * (n % 2), :], ACT.Silu,
                                         bias=bg[:, n // C1, n % C1:n % C1 + 1]).then_inc(s_si[1], 1)
                act.wait_ge(s_yo[1], i + 1)
                ident_of(y_t, PS[:, 6, :], bias=col["L1_attn_bo"][:, 0:1]).then_inc(s_yc[1], 1)

        NLINK = 74

        @block.vector
        def _(dve):
            v = nc.vector
            cnt = [0]

            def link0(ins):
                cnt[0] += 1
                ins.then_inc(s_link0, 1)
                dve.wait_ge(s_link0, cnt[0])

            v.memset(wparts[:], 0.0).then_inc(s_vset, 1)
            v.memset(rel_stack[:], 0.0)
            v.memset(q_stack[:], 0.0)
            v.memset(k_stack[0:96], 0.0)
            v.memset(k_stack[96:P], 1.0)
            v.memset(crow[:], 0.0)
            v.memset(q_parts[:], 0.0)
            v.memset(negmax[:], 0.0)
            v.memset(PS[:, 6:8, :], 0.0)
            v.memset(v0[:], 0.0)
            link0(v.memset(vm[:], 0.0))
            v.memset(v0[:, :, :, DH:DH + 1], 1.0)
            v.memset(vm[:, :, :, DH:DH + 1], 1.0)
            dve.wait_ge(s_relx, 32)
            relx = probs[0:DH, 0:1024]
            link0(v.tensor_copy(relx[:, 256 + NREL:1024],
                                relx[:, 255 + NREL:256 + NREL].to_broadcast([DH, 1024 - 256 - NREL])))
            rp = [k_stack[0:DH, 2 * p:2 * p + 2, :].rearrange("p a b -> p (a b)") for p in range(3)]
            link0(v.tensor_copy(rp[0], relx))
            link0(v.tensor_tensor(relx, relx, rp[0], ALU.subtract))
            link0(v.tensor_copy(rp[1], relx))
            v.tensor_tensor(rp[2], relx, rp[1], ALU.subtract).then_inc(s_vset, 1)
            dve.wait_ge(s_const, NCONST)
            dve.wait_ge(s_load, NLOAD)
            v.tensor_copy(identb[:], ident[:])
            v.tensor_scalar_mul(bk0s[:], col["L0_attn_bk"][:], SCALE)
            v.tensor_scalar_mul(bk1s[:], col["L1_attn_bk"][:], SCALE)
            v.tensor_tensor(xn[:], tmp[:], tmp[:], ALU.mult)
            link0(v.tensor_tensor(x[:], x1[:], x1[:], ALU.mult))
            v.tensor_reduce(cnorm[:, 0:NT], xn[:], AX.X, ALU.add)
            v.tensor_reduce(cnorm[:, NT:E], x[:], AX.X, ALU.add).then_inc(s_vset, 1)
            dve.wait_ge(s_vset, 3)
            cnt[0] = 0
            with dve.Fori(0, B) as i:
                def link(ins):
                    cnt[0] += 1
                    ins.then_inc(s_link, 1)
                    dve.wait_ge(s_link, i * NLINK + cnt[0])

                def norm(src, dst, n, eps, rms, out_sem, out_value):
                    for j in range(NT):
                        last = v.bn_stats(stats[:, j], src[:, j])
                    link(last)
                    v.memset(pause[:], 0.0)
                    for j in range(NT):
                        last = v.bn_aggr(mv[:, j], stats[:, j])
                    link(last)
                    if rms:
                        link(v.tensor_tensor(rvar[:], mv[:, :, 0], mv[:, :, 0], ALU.mult))
                        link(v.tensor_tensor(rvar[:], rvar[:], mv[:, :, 1], ALU.add))
                        v.tensor_scalar_add(rvar[:], rvar[:], eps).then_inc(s_gs, 1)
                    else:
                        v.tensor_scalar_add(rvar[:], mv[:, :, 1], eps).then_inc(s_gs, 1)
                    dve.wait_ge(s_pow, i * 5 + n + 1)
                    for j in range(NT):
                        if rms:
                            last = v.tensor_scalar_mul(dst[:, j], src[:, j], rstd[:, j:j + 1])
                        else:
                            last = v.tensor_scalar(dst[:, j], src[:, j], mv[:, j, 0:1], rstd[:, j:j + 1],
                                                   ALU.subtract, ALU.mult)
                    last.then_inc(out_sem, 1)
                    dve.wait_ge(out_sem, out_value)

                def split_parts(a):
                    if a != "win":
                        before = {"mla": "win", "rel": "mla"}[a]
                        dve.wait_ge(s_scr[before], i * SCR[before] + SCR[before])
                    dve.wait_ge(s_qkf[a], i * 2 + 2)
                    if a == "rel":
                        q = q_f[:].rearrange("p (u n) -> p n u", n=2)
                        qp = q_parts[:].rearrange("p (n x) -> p n x", n=2)
                        qd = [qp[:, :, p * T:p * T + T - 1:2] for p in range(3)]
                    else:
                        q = q_f[:]
                        qd = [q_plain[:, p] for p in range(3)]
                    v.tensor_copy(qd[0], q)
                    link(v.tensor_copy(k_parts[:, 0], k_f[:]))
                    v.tensor_tensor(q, q, qd[0], ALU.subtract)
                    link(v.tensor_tensor(k_f[:], k_f[:], k_parts[:, 0], ALU.subtract))
                    v.tensor_copy(qd[1], q)
                    link(v.tensor_copy(k_parts[:, 1], k_f[:]))
                    v.tensor_tensor(qd[2], q, qd[1], ALU.subtract).then_inc(s_parts[a], 1)
                    v.tensor_tensor(k_parts[:, 2], k_f[:], k_parts[:, 1], ALU.subtract).then_inc(s_parts[a], 1)

                def copy_v(a, dst, bank, bias):
                    dve.wait_ge(s_vproj[a], i + 1)
                    out = dst[:, :, :, 0:DH]
                    src = PS[:, bank, :].rearrange("p (j h d) -> p j h d", j=NT, h=H)
                    if bias is None:
                        v.tensor_copy(out, src).then_inc(s_v[a], 1)
                    else:
                        for j in range(NT):
                            last = v.tensor_tensor(out[:, j], src[:, j],
                                                   bias[:].rearrange("p (h d) -> p h d", h=H), ALU.add)
                        last.then_inc(s_v[a], 1)

                def split_max(a, half):
                    dve.wait_ge(s_mxt[a], i * 2 + half + 1)
                    if a == "mla":
                        dve.wait_ge(s_sh["win", half], i * 32 + 32)
                    src = PS[0:NT * HT, 6, half * P:half * P + P]
                    link(v.tensor_copy(cpart[:, half, 0], src))
                    v.tensor_tensor(cpart[:, half, 1], src, cpart[:, half, 0], ALU.subtract).then_inc(s_cp[a], 1)

                def copy_o_raw(a):
                    for g in range(4):
                        dve.wait_ge(s_pv[a], i * 4 + g + 1)
                        v.tensor_copy(o_raw[:, g, :], PS[:, 6 + g % 2, :]).then_inc(s_or[a], 1)

                def normalise(a):
                    dve.wait_ge(s_ort[a], i + 1)
                    src = PS[:, 0:4, :].rearrange("p j (h c) -> p j h c", h=H)
                    link(v.reciprocal(rden[:], src[:, :, :, DH]))
                    for j in range(NT):
                        last = v.tensor_tensor(o_tok[:, j].rearrange("p (h d) -> p h d", h=H), src[:, j, :, 0:DH],
                                               rden[:, j].rearrange("p (h o) -> p h o", o=1).to_broadcast([P, H, DH]),
                                               ALU.mult)
                    last.then_inc(s_on[a], 1)
                    dve.wait_ge(s_ot[a], i + 1)
                    v.tensor_copy(o_t[a][:], PS[:, 4, :]).then_inc(s_otc[a], 1)

                def spread(t):
                    return t.rearrange("p (j o) -> p j o", o=1).to_broadcast([P, NT, E])

                def top_two(k):
                    score = top[:, 0]
                    link(v.tensor_reduce(tc[:, 0], score, AX.X, ALU.max))
                    link(v.tensor_tensor(top[:, 1], score, spread(tc[:, 0]), ALU.is_equal))
                    link(v.tensor_tensor(top[:, 1], top[:, 1], rev[:], ALU.mult))
                    link(v.tensor_reduce(tc[:, 1], top[:, 1], AX.X, ALU.max))
                    link(v.tensor_tensor(top[:, 2], top[:, 1], spread(tc[:, 1]), ALU.is_equal))
                    link(v.scalar_tensor_tensor(top[:, 3], top[:, 2], -3e38, score, ALU.mult, ALU.add))
                    link(v.tensor_reduce(tc[:, 2], top[:, 3], AX.X, ALU.max))
                    v.tensor_tensor(tc[:, 4], tc[:, 2], tc[:, 0], ALU.subtract).then_inc(s_gd[k], 1)
                    link(v.tensor_tensor(top[:, 4], top[:, 3], spread(tc[:, 2]), ALU.is_equal))
                    link(v.tensor_tensor(top[:, 4], top[:, 4], rev[:], ALU.mult))
                    link(v.tensor_reduce(tc[:, 3], top[:, 4], AX.X, ALU.max))
                    link(v.tensor_tensor(top[:, 5], top[:, 4], spread(tc[:, 3]), ALU.is_equal))
                    dve.wait_ge(s_ge[k], i + 1)
                    link(v.tensor_scalar_add(tc[:, 6], tc[:, 5], 1.0))
                    link(v.reciprocal(tc[:, 6], tc[:, 6]))
                    link(v.tensor_tensor(tc[:, 7], tc[:, 5], tc[:, 6], ALU.mult))
                    v.tensor_tensor(top[:, 1], top[:, 2], spread(tc[:, 6]), ALU.mult)
                    link(v.tensor_tensor(top[:, 4], top[:, 5], spread(tc[:, 7]), ALU.mult))
                    v.tensor_tensor(top[:, 6], top[:, 1], top[:, 4], ALU.add).then_inc(s_cb[k], 1)

                def split_combine(k, bank):
                    dve.wait_ge(s_cbt[k], i + 1)
                    src = PS[0:E, bank, :]
                    v.tensor_copy(wt_full[:], src)
                    link(v.tensor_copy(wparts[0:E], src))
                    link(v.tensor_tensor(wt_f, src, wparts[0:E], ALU.subtract))
                    link(v.tensor_copy(wt_mid[:], wt_f))
                    v.tensor_copy(wparts[32:32 + E], wt_mid[:])
                    link(v.tensor_tensor(wt_f, wt_f, wt_mid[:], ALU.subtract))
                    v.tensor_copy(wparts[64:64 + E], wt_f).then_inc(s_wp[k], 1)

                dve.wait_ge(s_x, i * 16 + 16)
                norm(x, xn, 0, 1e-5, False, s_xn, i * 2 + 1)
                norm(xn, tmp, 1, 1e-6, True, s_xr, i + 1)
                split_parts("win")
                copy_v("win", v0, 4, bv0)
                split_parts("mla")
                copy_v("mla", vm, 0, None)
                for n, (j, h0) in enumerate(WIN_MAX):
                    b = 2 * (n % 3)
                    lo = WIN if j == 0 else 0
                    dve.wait_ge(s_sc["win"], i * 16 + n + 1)
                    src = PS[:, b:b + 2, 0:2 * WQ].rearrange("p b (h c) -> p b h c", h=2)[:, :, :, lo:WQ]
                    v.tensor_reduce(negmax[:, h0 // HT, h0 % HT:h0 % HT + 4, j], src, AX.X, ALU.max, negate=True)\
                     .then_inc(s_mx["win"], 1)
                    if n == len(WIN_MAX) // 2 + 2:
                        split_max("win", 0)
                split_max("win", 1)
                copy_o_raw("win")
                normalise("win")
                for n, (j, h0, nh, per) in enumerate(MLA_MAX):
                    b = 2 * (n % 3)
                    keys = P * (j + 1)
                    dve.wait_ge(s_sc["mla"], i * len(MLA_MAX) + n + 1)
                    src = PS[:, b:b + 2, 0:per * keys].rearrange("p b (h c) -> p b h c", h=per)
                    v.tensor_reduce(negmax[:, h0 // HT, h0 % HT:h0 % HT + nh, j], src, AX.X, ALU.max,
                                    negate=True).then_inc(s_mx["mla"], 1)
                    if n == len(MLA_MAX) // 2 + 2:
                        split_max("mla", 0)
                split_max("mla", 1)
                copy_o_raw("mla")
                normalise("mla")
                dve.wait_ge(s_mot, i + 1)
                link(v.tensor_tensor(xn[:].rearrange("p j d -> p (j d)"), PS[:, 6, :],
                                     xn[:].rearrange("p j d -> p (j d)"), ALU.add))
                norm(xn, tmp, 2, 1e-6, True, s_rr, i + 1)
                dve.wait_ge(s_out, i * 16 + 16)
                v.tensor_tensor(x1[:], x[:], xn[:], ALU.add).then_inc(s_x1, 1)
                dve.wait_ge(s_lg[0], i + 1)
                link(v.tensor_copy(top[:, 0], PS[:, 5, 0:NT * E].rearrange("p (j e) -> p j e", j=NT)))
                top_two(0)
                split_combine(0, 6)
                N0 = E * C0
                for n in range(N0):
                    dve.wait_ge(s_si[0], i * N0 + n + 1)
                    if n % C0 == 0:
                        dve.wait_ge(s_wb[0], i * E + n // C0 + 1)
                    if n >= 3:
                        dve.wait_ge(s_dn[0], i * N0 + n - 2)
                    v.tensor_tensor(hid_b[:, n % 3], hid_a[:, n % 3], PS[:, 4 + n // C0 % 2, :], ALU.mult)\
                     .then_inc(s_hid[0], 1)
                dve.wait_ge(s_yt[0], i + 1)
                dve.wait_ge(s_x1, i + 1)
                link(v.tensor_tensor(x1[:].rearrange("p j d -> p (j d)"), PS[:, 7, :],
                                     x1[:].rearrange("p j d -> p (j d)"), ALU.add))
                norm(x1, xn, 3, 1e-5, False, s_xn, i * 2 + 2)
                link(v.tensor_tensor(tmp[:], xn[:], xn[:], ALU.mult))
                link(v.tensor_reduce(mv[:, :, 0], tmp[:], AX.X, ALU.add))
                split_parts("rel")
                copy_v("rel", v0, 3, bv1)
                dve.wait_ge(s_dist, i + 1)
                dots = PS[:, 4, 0:NT * E].rearrange("p (j e) -> p j e", j=NT)
                link(v.tensor_scalar(top[:, 7], dots, -2.0, None, ALU.mult))
                link(v.tensor_tensor(top[:, 6], spread(mv[:, :, 0]),
                                     cnorm[:].rearrange("p (o e) -> p o e", o=1).to_broadcast([P, NT, E]), ALU.add))
                link(v.tensor_tensor(top[:, 7], top[:, 7], top[:, 6], ALU.add))
                v.tensor_scalar_max(top[:, 7], top[:, 7], 1e-12).then_inc(s_gs, 1)
                dve.wait_ge(s_pow, i * 5 + 5)
                top_two(1)
                split_combine(1, 5)
                base = i * NS
                cnt2 = [0]

                def link2(ins):
                    cnt2[0] += 1
                    ins.then_inc(s_link2, 1)
                    dve.wait_ge(s_link2, i * 2 * NS + cnt2[0])

                def max_tile(t):
                    b = 2 * (t % 3)
                    dve.wait_ge(s_rs, base + t + 1)
                    src = PS[:, b:b + 2, :].rearrange("p b (k c) -> p c (b k)", k=2)
                    if t >= 2:
                        dve.wait_ge(s_rmt, base + t - 1)
                    v.tensor_reduce(mcol[:, t % 2], src, AX.X, ALU.max).then_inc(s_rm, 1)

                def max_row(t):
                    dve.wait_ge(s_rmt, base + t + 1)
                    v.tensor_reduce(cm[:], PS[:, 6, 0:2 * P].rearrange("p (c k) -> p c k", c=2), AX.X, ALU.max,
                                    negate=True).then_inc(s_rc, 1)
                    dve.wait_ge(s_rct, base + t + 1)
                    src = PS[0:2, 6, 2 * P:3 * P]
                    if t >= 1:
                        dve.wait_ge(s_rsh, base + t)
                    link2(v.tensor_copy(crow[0:2], src))
                    link2(v.tensor_tensor(crow_mid[:], src, crow[0:2], ALU.subtract))
                    v.tensor_copy(crow[32:34], crow_mid[:]).then_inc(s_rcs, 1)

                def copy_quarter(q):
                    dve.wait_ge(s_pv["rel"], i * 4 + q + 1)
                    v.tensor_copy(o_raw[:, :, q * P:q * P + P],
                                  PS[:, 7, :].rearrange("p (g l) -> p g l", g=4)).then_inc(s_or["rel"], 1)

                for t in range(NS + 1):
                    if t >= 1:
                        max_row(t - 1)
                    if t < NS:
                        max_tile(t)
                    if t > NSQ and t % NSQ == 1 and t < NS:
                        copy_quarter(t // NSQ - 1)
                copy_quarter(NT - 1)
                normalise("rel")
                N1 = E * C1
                for n in range(N1):
                    e = n // C1
                    dve.wait_ge(s_si[1], i * N1 + n + 1)
                    v.scalar_tensor_tensor(hid_b[0:CW, n % 3], PS[0:CW, 2 * (n % 2) + 1, :],
                                           bu[:, e, n % C1:n % C1 + 1], hid_a[0:CW, n % 3],
                                           ALU.add, ALU.mult).then_inc(s_hu, 1)
                    dve.wait_ge(s_hu, i * N1 + n + 1)
                    if n % C1 == 0:
                        dve.wait_ge(s_wb[1], i * E + e + 1)
                    if n >= 3:
                        dve.wait_ge(s_dn[1], i * N1 + n - 2)
                    v.tensor_tensor(hid_c[0:CW, n % 3], hid_b[0:CW, n % 3], PS[0:CW, 4 + e % 2, :], ALU.mult)\
                     .then_inc(s_hid[1], 1)
                dve.wait_ge(s_yt[1], i + 1)
                v.tensor_tensor(x1[:].rearrange("p j d -> p (j d)"), PS[:, 7, :],
                                x1[:].rearrange("p j d -> p (j d)"), ALU.add).then_inc(s_x2, 1)
            assert cnt[0] == NLINK, cnt[0]

        @block.tensor
        def _(pe):
            mm = nc.tensor.matmul
            pe.wait_ge(s_load, NLOAD)
            pe.wait_ge(s_vset, 3)
            pe.wait_ge(s_rel_ld, 192)
            with pe.Fori(0, B) as i:
                def transpose_tiles(bank, src):
                    for j in range(NT):
                        last = nc.tensor.transpose(PS[:, bank, j * P:j * P + P], src[:, j, :], ident[:])
                    return last

                def by_token(bank, x_t, w, n):
                    for j in range(NT):
                        last = mm(PS[:, bank, j * n:j * n + n], x_t[:, j * P:j * P + P], w, start=True, stop=True)
                    return last

                def transpose_max(a, half, groups):
                    pe.wait_ge(s_mx[a], i * groups + (half + 1) * groups // 2)
                    nc.tensor.transpose(PS[:, 6, half * P:half * P + P],
                                        negmax[:, half].rearrange("p h j -> p (h j)"), ident[:])\
                      .then_inc(s_mxt[a], 1)

                def finish(a):
                    for j in range(NT):
                        for g in range(4):
                            last = nc.tensor.transpose(PS[:, j, g * P:g * P + P], o_raw[:, g, j * P:j * P + P], ident[:])
                    last.then_inc(s_ort[a], 1)
                    pe.wait_ge(s_on[a], i + 1)
                    transpose_tiles(4, o_tok).then_inc(s_ot[a], 1)

                pe.wait_ge(s_xn, i * 2 + 1)
                transpose_tiles(0, xn).then_inc(s_tr, 1)
                pe.wait_ge(s_xr, i + 1)
                transpose_tiles(1, tmp).then_inc(s_tr, 1)
                pe.wait_ge(s_xnt, i * 3 + 1)
                mm(PS[:, 2, :], W["L0_attn_Wq"][:], xn_t[:], start=True, stop=True).then_inc(s_proj["win"], 1)
                mm(PS[:, 3, :], W["L0_attn_Wk"][:], xn_t[:], start=True, stop=True).then_inc(s_proj["win"], 1)
                by_token(4, xn_t, W["L0_attn_Wv"][:], D).then_inc(s_vproj["win"], 1)
                pe.wait_ge(s_xnt, i * 3 + 2)
                mm(PS[:, 5, :], W["L0_ffn_Wq"][:], h_t[:], start=True, stop=True).then_inc(s_proj["mla"], 1)
                mm(PS[0:LAT, 6, :], wdkv[:], h_t[:], start=True, stop=True).then_inc(s_lat, 1)
                pe.wait_ge(s_ct, i + 1)
                mm(PS[:, 7, :], wuk[:], c_t[:], start=True, stop=True).then_inc(s_proj["mla"], 1)
                by_token(0, c_t, wuv[:], D).then_inc(s_vproj["mla"], 1)

                pe.wait_ge(s_qkf["mla"], i * 2 + 2)
                pe.wait_ge(s_v["win"], i + 1)
                pe.wait_ge(s_v["mla"], i + 1)
                pe.wait_ge(s_stk["win"], i * QST["win"] + QST["win"])
                pe.wait_ge(s_stkk["win"], i * KST["win"] + KST["win"])
                pe.wait_ge(s_zero, i * 16 + 16)
                for n, (j, h0) in enumerate(WIN_MAX):
                    b = 2 * (n % 3)
                    lo = WIN if j == 0 else 0
                    if n >= 3:
                        pe.wait_ge(s_mx["win"], i * 16 + n - 2)
                    for r in range(4):
                        h = h0 + r
                        c = (r % 2) * WQ
                        out = PS[:, b + r // 2, c + lo:c + WQ]
                        mm(out, q_stack[:, h, j * P:j * P + P], k_stack[:, h, j * P - WIN + lo:j * P + P],
                           start=(r % 2 == 0), stop=True, skip_group_check=True)
                        last = mm(out, identb[:], band_qk[:, lo:WQ], start=False, stop=True, skip_group_check=True)
                    last.then_inc(s_sc["win"], 1)
                    if n == len(WIN_MAX) // 2 + 1:
                        transpose_max("win", 0, len(WIN_MAX))
                transpose_max("win", 1, len(WIN_MAX))

                def win_scores(n):
                    b = 3 * (n % 2)
                    if n % 4 == 0:
                        pe.wait_ge(s_sh["win", n // 4], i * 32 + 32)
                    if n >= 2:
                        pe.wait_ge(s_ex["win"], i * 8 + n - 1)
                    for r in range(2):
                        h = 2 * n + r
                        for kt in range(NT):
                            w = WQ if kt < NT - 1 else P
                            out = PS[:, b + r, kt * WQ:kt * WQ + w] if kt < NT - 1 else PS[:, b + 2, r * P:r * P + P]
                            first = kt == 0 or (kt == NT - 1 and r == 0)
                            mm(out, k_stack[:, h, kt * P:kt * P + P], q_stack[:, h, kt * P:kt * P + w],
                               start=first, stop=True, skip_group_check=True)
                            last = mm(out, identb[:], band_kq[:, 0:w], start=False, stop=True, skip_group_check=True)
                    last.then_inc(s_st["win"], 1)

                def win_pv(g):
                    if g == 0:
                        pe.wait_ge(s_cp["win"], i * 2 + 2)
                    pe.wait_ge(s_ex["win"], i * 8 + 2 * g + 2)
                    if g >= 2:
                        pe.wait_ge(s_or["win"], i * 4 + g - 1)
                    p4 = probs[:, g % 2 * 5120:g % 2 * 5120 + 2560].rearrange("p (r c) -> p r c", r=4)
                    for kt in range(NT):
                        w = WQ if kt < NT - 1 else P
                        for r in range(4):
                            last = mm(PS[32 * r:32 * r + VW, 6 + g % 2, kt * P:kt * P + w],
                                      v0[:, kt, 4 * g + r, :], p4[:, r, kt * WQ:kt * WQ + w],
                                      start=(kt == 0), stop=True, skip_group_check=True,
                                      tile_position=(0, 32 * r))
                    last.then_inc(s_pv["win"], 1)

                for n in range(8):
                    win_scores(n)
                    if n >= 2 and n % 2 == 0:
                        win_pv(n // 2 - 1)
                win_pv(3)
                pe.wait_ge(s_or["win"], i * 4 + 4)
                finish("win")

                pe.wait_ge(s_stk["mla"], i * QST["mla"] + QST["mla"])
                pe.wait_ge(s_stkk["mla"], i * KST["mla"] + KST["mla"])
                pe.wait_ge(s_otc["win"], i + 1)
                for n, (j, h0, nh, per) in enumerate(MLA_MAX):
                    b = 2 * (n % 3)
                    keys = P * (j + 1)
                    if n >= 3:
                        pe.wait_ge(s_mx["mla"], i * len(MLA_MAX) + n - 2)
                    for r in range(nh):
                        h = h0 + r
                        c = (r % per) * keys
                        mm(PS[:, b + r // per, c:c + keys], q_stack[:, h, j * P:j * P + P], k_stack[:, h, 0:keys],
                           start=(r % per == 0), stop=True, skip_group_check=True)
                        last = mm(PS[:, b + r // per, c + keys - P:c + keys], identb[:], causal_qk[:],
                                  start=False, stop=True, skip_group_check=True)
                    last.then_inc(s_sc["mla"], 1)
                    if n == len(MLA_MAX) // 2 + 1:
                        transpose_max("mla", 0, len(MLA_MAX))
                transpose_max("mla", 1, len(MLA_MAX))

                def mla_scores(h):
                    b = 3 * (h % 2)
                    if h % HT == 0:
                        pe.wait_ge(s_sh["mla", h // HT], i * 32 + 32)
                    if h >= 2:
                        pe.wait_ge(s_ex["mla"], i * H + h - 1)
                    for kt, (bank, c, first) in enumerate(((0, 0, True), (1, 0, True), (2, 0, True), (1, 384, False))):
                        w = T - kt * P
                        mm(PS[:, b + bank, c:c + w], k_stack[:, h, kt * P:kt * P + P], q_stack[:, h, kt * P:T],
                           start=first, stop=True, skip_group_check=True)
                        last = mm(PS[:, b + bank, c:c + P], identb[:], causal_kq[:], start=False, stop=True,
                                  skip_group_check=True)
                    last.then_inc(s_st["mla"], 1)

                def mla_pv(g):
                    if g == 0:
                        pe.wait_ge(s_cp["mla"], i * 2 + 2)
                    pe.wait_ge(s_ex["mla"], i * H + 4 * g + 4)
                    if g >= 2:
                        pe.wait_ge(s_or["mla"], i * 4 + g - 1)
                    p4 = probs[:, g % 2 * 5120:g % 2 * 5120 + 5120].rearrange("p (r c) -> p r c", r=4)
                    for kt, c in enumerate((0, 512, 1024, 896)):
                        w = T - kt * P
                        for r in range(4):
                            last = mm(PS[32 * r:32 * r + VW, 6 + g % 2, kt * P:T], vm[:, kt, 4 * g + r, :],
                                      p4[:, r, c:c + w], start=(kt == 0), stop=True, skip_group_check=True,
                                      tile_position=(0, 32 * r))
                    last.then_inc(s_pv["mla"], 1)

                for h in range(H):
                    mla_scores(h)
                    if h >= 5 and h % 4 == 1:
                        mla_pv(h // 4 - 1)
                mla_pv(3)
                pe.wait_ge(s_or["mla"], i * 4 + 4)
                finish("mla")
                pe.wait_ge(s_otc["mla"], i + 1)
                mm(PS[:, 5, :], W["L0_ffn_Wo"][:], o_t["mla"][:], start=True, stop=True).then_inc(s_mo, 1)
                pe.wait_ge(s_moc, i + 1)
                transpose_tiles(6, y_t.rearrange("p (j t) -> p j t", j=NT)).then_inc(s_mot, 1)
                pe.wait_ge(s_rr, i + 1)
                transpose_tiles(7, tmp).then_inc(s_rt, 1)
                pe.wait_ge(s_h2, i + 1)
                by_token(5, h_t, gate_w[:], E).then_inc(s_lg[0], 1)

                def spread_combine(k, e):
                    C = (C0, C1)[k]
                    if e >= 2:
                        pe.wait_ge(s_hid[k], i * E * C + (e - 1) * C)
                    mm(PS[:, 4 + e % 2, :], sel_w[:, e, :], wparts[:], start=True, stop=True).then_inc(s_wb[k], 1)

                def up0(n):
                    e, c = n // C0, n % C0
                    if n >= 4:
                        pe.wait_ge(s_si[0], i * E * C0 + n - 3)
                    mm(PS[:, n % 4, :], w1[:, e, c * P:c * P + P], h_t[:], start=True, stop=True)\
                      .then_inc(s_up[0], 1)

                for n in range(3):
                    up0(n)
                pe.wait_ge(s_cb[0], i + 1)
                for j in range(NT):
                    last = nc.tensor.transpose(PS[0:E, 6, j * P:j * P + P], top[:, 6, j, :], ident[:])
                last.then_inc(s_cbt[0], 1)
                pe.wait_ge(s_wp[0], i + 1)
                mm(PS[:, 6, :], W["L0_attn_Wo"][:], o_t["win"][:], start=True, stop=False, skip_group_check=True)
                for n in range(E * C0):
                    if n % C0 == 0:
                        spread_combine(0, n // C0)
                    if n + 3 < E * C0:
                        up0(n + 3)
                    pe.wait_ge(s_hid[0], i * E * C0 + n + 1)
                    last = mm(PS[:, 6, :], w2[:, n // C0, n % C0, :], hid_b[:, n % 3], start=False,
                              stop=(n == E * C0 - 1), skip_group_check=True)
                    last.then_inc(s_dn[0], 1)
                pe.wait_ge(s_dn[0], i * E * C0 + E * C0)
                pe.nop().then_inc(s_yo[0], 1)
                pe.wait_ge(s_yc[0], i + 1)
                transpose_tiles(7, y_t.rearrange("p (j t) -> p j t", j=NT)).then_inc(s_yt[0], 1)

                pe.wait_ge(s_xn, i * 2 + 2)
                transpose_tiles(0, xn).then_inc(s_tr, 1)
                pe.wait_ge(s_xnt, i * 3 + 3)
                mm(PS[:, 1, :], W["L1_attn_Wq"][:], xn_t[:], start=True, stop=True).then_inc(s_proj["rel"], 1)
                mm(PS[:, 2, :], W["L1_attn_Wk"][:], xn_t[:], start=True, stop=True).then_inc(s_proj["rel"], 1)
                by_token(3, xn_t, W["L1_attn_Wv"][:], D).then_inc(s_vproj["rel"], 1)
                by_token(4, xn_t, cen_t[:], E).then_inc(s_dist, 1)
                pe.wait_ge(s_cb[1], i + 1)
                for j in range(NT):
                    last = nc.tensor.transpose(PS[0:E, 5, j * P:j * P + P], top[:, 6, j, :], ident[:])
                last.then_inc(s_cbt[1], 1)
                pe.wait_ge(s_wp[1], i + 1)
                pe.wait_ge(s_qkf["rel"], i * 2 + 2)
                pe.wait_ge(s_v["rel"], i + 1)
                pe.wait_ge(s_stk["rel"], i * QST["rel"] + QST["rel"])
                pe.wait_ge(s_stkk["rel"], i * KST["rel"] + KST["rel"])
                base = i * NS

                def scores(t, kt):
                    l0, hh = t // 2 * LB, t % 2
                    if kt == 0 and t >= 3:
                        pe.wait_ge(s_ex["rel"], base + t - 2)
                    qs = q_stack[:, hh * HT:hh * HT + HT, l0:l0 + LB]
                    out = PS[:, 2 * (t % 3) + kt // 2, kt % 2 * 2 * P:kt % 2 * 2 * P + 2 * P]\
                        .rearrange("p (h l) -> p h l", h=HT)
                    for h in range(HT):
                        mm(out[:, h, :], k_stack[:, hh * HT + h, kt * P:kt * P + P], qs[:, h, :],
                           start=(kt % 2 == 0 and h == 0), stop=True, skip_group_check=True)
                    for u in range(LB // 2):
                        c = kt * P + T - 1 - (l0 + 2 * u)
                        last = mm(out[:, :, 2 * u:2 * u + 2], rel_stack[:, c:c + P], qs[:, :, 2 * u:2 * u + 2],
                                  start=False, stop=True, skip_group_check=True)
                    if kt == NT - 1:
                        last.then_inc(s_rs, 1)

                def transpose_tile_max(t):
                    pe.wait_ge(s_rm, base + t + 1)
                    for c in range(2):
                        last = nc.tensor.transpose(PS[:, 6, c * P:c * P + P], mcol[:, t % 2, c * P:c * P + P],
                                                   ident[:])
                    last.then_inc(s_rmt, 1)

                def transpose_row_max(t):
                    pe.wait_ge(s_rc, base + t + 1)
                    nc.tensor.transpose(PS[0:2, 6, 2 * P:3 * P], cm[:], ident[:]).then_inc(s_rct, 1)

                def shift(t):
                    pe.wait_ge(s_rcs, base + t + 1)
                    for k in range(4):
                        for c in range(2):
                            last = mm(PS[:, 2 * (t % 3) + k // 2, (k % 2) * 2 * P + c * P:(k % 2) * 2 * P + c * P + P],
                                      sel_c[:, c, :], crow[:], start=False, stop=True, skip_group_check=True)
                    last.then_inc(s_rsh, 1)

                def sum_quarter(q):
                    pe.wait_ge(s_ex["rel"], base + (q + 1) * NSQ)
                    if q >= 1:
                        pe.wait_ge(s_or["rel"], i * 4 + q)
                    pr = probs[:, 0:NT * H * P].rearrange("p (k h l) -> p k h l", k=NT, h=H)
                    for g in range(4):
                        for kt in range(NT):
                            for r in range(4):
                                last = mm(PS[32 * r:32 * r + VW, 7, g * P:g * P + P], v0[:, kt, 4 * g + r, :],
                                          pr[:, kt, 4 * g + r, :], start=(g == 0 and kt == 0), stop=True,
                                          skip_group_check=True, tile_position=(0, 32 * r))
                    last.then_inc(s_pv["rel"], 1)

                for t in range(NS + 2):
                    if t < NS:
                        scores(t, 0)
                        scores(t, 1)
                    if t >= 2:
                        shift(t - 2)
                    if t < NS:
                        scores(t, 2)
                    if 1 <= t <= NS:
                        transpose_tile_max(t - 1)
                    if t < NS:
                        scores(t, 3)
                    if 1 <= t <= NS:
                        transpose_row_max(t - 1)
                    if t > NSQ and t % NSQ == 1:
                        sum_quarter(t // NSQ - 1)
                pe.wait_ge(s_or["rel"], i * 4 + 4)
                finish("rel")

                def up1(n):
                    e, c = n // C1, n % C1
                    if n >= 2:
                        pe.wait_ge(s_hu, i * E * C1 + n - 1)
                    mm(PS[0:CW, 2 * (n % 2), :], wg[:, e, c * CW:c * CW + CW], xn_t[:], start=True, stop=True)
                    mm(PS[0:CW, 2 * (n % 2) + 1, :], wu[:, e, c * CW:c * CW + CW], xn_t[:], start=True, stop=True)\
                      .then_inc(s_up[1], 1)

                pe.wait_ge(s_otc["rel"], i + 1)
                mm(PS[:, 6, :], W["L1_attn_Wo"][:], o_t["rel"][:], start=True, stop=False, skip_group_check=True)
                mm(PS[:, 6, :], b2[:], wt_full[:], start=False, stop=False, skip_group_check=True)
                up1(0)
                for n in range(E * C1):
                    if n % C1 == 0:
                        spread_combine(1, n // C1)
                    if n + 1 < E * C1:
                        up1(n + 1)
                    pe.wait_ge(s_hid[1], i * E * C1 + n + 1)
                    last = mm(PS[:, 6, :], wd[:, n // C1, n % C1, :], hid_c[0:CW, n % 3], start=False,
                              stop=(n == E * C1 - 1), skip_group_check=True)
                    last.then_inc(s_dn[1], 1)
                pe.wait_ge(s_dn[1], i * E * C1 + E * C1)
                pe.nop().then_inc(s_yo[1], 1)
                pe.wait_ge(s_yc[1], i + 1)
                transpose_tiles(7, y_t.rearrange("p (j t) -> p j t", j=NT)).then_inc(s_yt[1], 1)


_TRANSPOSED = ["L0_attn_Wq", "L0_attn_Wk", "L0_attn_Wv", "L0_attn_Wo",
               "L1_attn_Wq", "L1_attn_Wk", "L1_attn_Wv", "L1_attn_Wo"]


def kernel(**inputs):
    import numpy as np
    import concourse.bacc as bacc
    from concourse.bass_utils import run_bass_kernel_spmd

    nc = bacc.Bacc("TRN2", target_bir_lowering=False, num_devices=1)
    arrays, dram = {}, {}
    for name, a in inputs.items():
        a = np.asarray(a)
        if name in _TRANSPOSED:
            a = a.T
        if name in ("L1_ffn_bg", "L1_ffn_b1"):
            a = a.reshape(-1, a.shape[1] // 3).T
        arrays[name] = np.ascontiguousarray(a)
    arrays["centroid_t"] = np.ascontiguousarray(arrays["L1_ffn_centroid"].T)
    arrays["rel_emb_t"] = np.ascontiguousarray(arrays.pop("L1_attn_rel_emb").T)
    for name, a in arrays.items():
        dram[name] = nc.dram_tensor("in_" + name, a.shape, mybir.dt.from_np(a.dtype), kind="ExternalInput").ap()
    dram["L1_attn_rel_emb"] = inputs["L1_attn_rel_emb"]
    x = arrays["L0_attn_x"]
    dram["out"] = nc.dram_tensor("out", x.shape, mybir.dt.from_np(x.dtype), kind="ExternalOutput").ap()
    two_layers(nc, dram)
    r = run_bass_kernel_spmd(nc, [{"in_" + n: a for n, a in arrays.items()}], core_ids=[0])
    return r.results[0]["out"]
```

```python
from contextlib import ExitStack

import concourse.bass as bass
from concourse import mybir

F32 = mybir.dt.float32
BF16 = mybir.dt.bfloat16
ALU = mybir.AluOpType
ACT = mybir.ActivationFunctionType
AX = mybir.AxisListType


def two_layers(nc, dram):
    B, T, D = dram["L0_attn_x"].shape
    H, DH = 16, 8
    HT = H // 2
    LB = 32
    P = 128
    NT = T // P
    E = dram["L0_ffn_gate_w"].shape[1]
    F0 = dram["L0_ffn_w1"].shape[2]
    F1 = dram["L1_ffn_Wg"].shape[2]
    C0 = F0 // P
    C1 = 3
    CW = F1 // C1
    LAT = dram["L0_ffn_Wdkv"].shape[1]
    WIN = 32
    WQ = P + WIN
    SCALE = float(DH) ** -0.5
    LOW = -1e30
    NREL = dram["L1_attn_rel_emb"].shape[0]
    QP = 3 * T + 1
    VW = 16
    SHIFT = 112
    NA = 8
    NCONST = 29
    MLA_TWO = [(j, h0, n, n // 2) for j, n in ((0, 8), (1, 4), (2, 2), (3, 2)) for h0 in range(0, HT, n)]
    MLA_ONE = [(j, h0, n, n) for j, n in ((0, 4), (1, 2), (2, 1), (3, 1)) for h0 in range(HT, H, n)]
    NG2, NG = len(MLA_TWO), len(MLA_TWO) + len(MLA_ONE)
    LEAD = 4
    SCORED = 3 * HT + HT
    WIN_MAX = [(j, h0) for half in (0, HT) for j in range(NT) for h0 in range(half, half + HT, 4)]
    NS = NT * (P // LB) * 2
    NSQ = NS // NT

    ctx = ExitStack()
    with ctx:
        def sb(name, shape, dt=F32):
            return ctx.enter_context(nc.sbuf_tensor(name, shape, dt))

        def sem(name):
            return ctx.enter_context(nc.semaphore(name))

        names = ["L0_attn_Wq", "L0_attn_Wk", "L0_attn_Wv", "L0_attn_Wo", "L0_ffn_Wq", "L0_ffn_Wo",
                 "L1_attn_Wq", "L1_attn_Wk", "L1_attn_Wv", "L1_attn_Wo"]
        W = {n: sb("w_" + n, [P, D]) for n in names}
        wdkv = sb("wdkv", [P, LAT])
        wuk = sb("wuk", [LAT, D])
        wuv = sb("wuv", [LAT, D])
        gate_w = sb("gate_w", [P, E])
        w1 = sb("w1", [P, E, F0])
        w2 = sb("w2", [P, E, C0, D])
        wg = sb("wg", [P, E, F1])
        wu = sb("wu", [P, E, F1])
        wd = sb("wd", [CW, E, C1, D])
        cen_t = sb("cen_t", [P, E])
        b2 = sb("b2", [3 * 32, D])
        cols = ["L0_attn_bq", "L0_attn_bk", "L0_attn_bo", "L1_attn_bq", "L1_attn_bk", "L1_attn_bo",
                "L0_ffn_g1", "L0_ffn_g2"]
        col = {n: sb("c_" + n, [P, 1]) for n in cols}
        bg = sb("bg", [CW, E, C1])
        bu = sb("bu", [CW, E, C1])
        bv0 = sb("bv0", [P, D])
        bv1 = sb("bv1", [P, D])
        bk0s = sb("bk0s", [P, 1])
        bk1s = sb("bk1s", [P, 1])
        cnorm = sb("cnorm", [P, E])
        ident = sb("ident", [P, P])
        identb = sb("identb", [P, P], BF16)
        causal_qk = sb("causal_qk", [P, P], BF16)
        causal_kq = sb("causal_kq", [P, P], BF16)
        band_qk = sb("band_qk", [P, WQ], BF16)
        band_kq = sb("band_kq", [P, WQ], BF16)
        sel_w = sb("sel_w", [P, E, P], BF16)
        sel_c = sb("sel_c", [P, 2, P], BF16)
        rev = sb("rev", [P, NT, E])
        power = sb("power", [P, 2, NT * E])
        rel_stack = sb("rel_stack", [P, 2 * T], BF16)
        q_stack = sb("q_stack", [P, H, T], BF16)
        k_stack = sb("k_stack", [P, H, T], BF16)
        probs = sb("probs", [P, 2 * 4 * 1280])
        v0 = sb("v0", [P, NT, H, VW])
        v1 = sb("v1", [P, NT, H, VW])
        vm = sb("vm", [P, NT, H, VW])
        x = sb("x", [P, NT, D])
        xn = sb("xn", [P, NT, D])
        x1 = sb("x1", [P, NT, D])
        tmp = sb("tmp", [P, NT, D])
        xn_t = sb("xn_t", [P, T])
        h_t = sb("h_t", [P, T])
        c_t = sb("c_t", [LAT, T])
        q_f = sb("q_f", [P, T])
        k_f = sb("k_f", [P, T])
        q_parts = sb("q_parts", [P, 2 * QP], BF16)
        q_plain = sb("q_plain", [P, 3, T], BF16)
        k_parts = sb("k_parts", [P, 3, T], BF16)
        o_quarter = sb("o_quarter", [P, D])
        o_raw = sb("o_raw", [P, 4, T])
        o_t = {"win": sb("o_t_win", [P, T]), "mla": sb("o_t_mla", [P, T])}
        o_t["rel"] = o_t["mla"]
        o_tok = tmp
        stats = sb("stats", [P, NT, 6])
        mv = sb("mv", [P, NT, 2])
        rstd = sb("rstd", [P, NT])
        rvar = sb("rvar", [P, NT])
        wt_full = sb("wt_full", [3 * 32, T])
        wtok = sb("wtok", [P, NT, 3 * 32])
        wt_hi = sb("wt_hi", [P, NT, E], BF16)
        negmax = sb("negmax", [P, 2, 4 * HT, NT])
        cpart = sb("cpart", [NT * HT, 2, 2, P], BF16)
        rden = sb("rden", [P, NT, H])
        top = sb("top", [P, 8, NT, E])
        tc = sb("tc", [P, 8, NT])
        roots = sb("roots", [P, 2, NT])
        wparts = sb("wparts", [P, T], BF16)
        mcol = sb("mcol", [P, 2, HT * LB])
        cm = sb("cm", [P, 2])
        pause = sb("pause", [P, 1])
        one = sb("one", [P, 1])
        crow = sb("crow", [P, P], BF16)
        crow_mid = sb("crow_mid", [2, P])
        hid_a = probs[:, 0:NA * T].rearrange("p (n t) -> p n t", n=NA)
        hid_b = probs[:, NA * T:(NA + 3) * T].rearrange("p (n t) -> p n t", n=3)
        hid_c = probs[:, (NA + 3) * T:(NA + 6) * T].rearrange("p (n t) -> p n t", n=3)
        y_t = probs[:, (NA + 6) * T:(NA + 7) * T]
        PS = ctx.enter_context(nc.psum_tensor("ps", [P, 8, 512], F32))

        scr = {(a, n): nc.dram_tensor(f"scr_{a}_{n}", [3 * DH, H, T], BF16, kind="Internal").ap()
               for a, names in (("win", ("q", "k")), ("mla", ("q", "k")), ("rel", ("qe", "qo", "k")))
               for n in names}
        zrow_d = nc.dram_tensor("zrow_d", [2, H * T], BF16, kind="Internal").ap()
        rel_d = nc.dram_tensor("rel_d", [3, DH, 1024], BF16, kind="Internal").ap()

        ATT = ("win", "mla", "rel")
        s_b2 = sem("bias_rows_zeroed")
        s_load = sem("weights_loaded")
        s_relx = sem("rel_table_loaded")
        s_const = sem("constants_made")
        s_vset = sem("vector_setup")
        s_rel_sp = sem("rel_parts_stored")
        s_rel_ld = sem("rel_stack_loaded")
        s_x = sem("x_loaded")
        s_link = sem("vector_chain")
        s_pow = sem("powers_done")
        s_gs = sem("power_inputs_ready")
        s_link0 = sem("vector_setup_chain")
        s_xn = sem("xn_done")
        s_xr = sem("xr_done")
        s_tr = sem("xn_transposed")
        s_xnt = sem("xn_t_copied")
        s_proj = {a: sem("qk_projected_" + a) for a in ATT}
        s_vproj = {a: sem("v_projected_" + a) for a in ATT}
        s_lat = sem("latent_projected")
        s_ct = sem("c_t_copied")
        s_qkf = {a: sem("qk_copied_" + a) for a in ATT}
        s_parts = {a: sem("parts_split_" + a) for a in ATT}
        s_v = {a: sem("v_copied_" + a) for a in ATT}
        s_scr = {a: sem("parts_stored_" + a) for a in ATT}
        s_stk = {a: sem("q_stack_loaded_" + a) for a in ATT}
        s_zero = sem("upper_key_rows_cleared")
        s_stkk = {a: sem("k_stack_loaded_" + a) for a in ATT}
        s_sc = {a: sem("scores_for_max_" + a) for a in ("win", "mla")}
        s_mx = {a: sem("max_taken_" + a) for a in ("win", "mla")}
        s_mxt = {a: sem("max_transposed_" + a) for a in ("win", "mla")}
        s_cp = {a: sem("max_split_" + a) for a in ("win", "mla")}
        s_sh = {(a, n): sem(f"shift_rows_{n}_loaded_{a}") for a in ("win", "mla") for n in range(2)}
        s_st = {a: sem("scores_t_" + a) for a in ("win", "mla")}
        s_ex = {a: sem("probs_ready_" + a) for a in ATT}
        s_pv = {a: sem("pv_done_" + a) for a in ATT}
        s_or = {a: sem("o_raw_copied_" + a) for a in ATT}
        s_ort = {a: sem("o_raw_transposed_" + a) for a in ATT}
        s_on = {a: sem("o_normalised_" + a) for a in ATT}
        s_ot = {a: sem("o_transposed_" + a) for a in ATT}
        s_otc = {a: sem("o_t_copied_" + a) for a in ATT}
        s_mo = sem("mla_out_projected")
        s_ao = sem("rel_out_projected")
        s_linkf = sem("first_norms_chain")
        s_linkp = sem("parts_chain")
        s_rr = sem("moe_input_normed")
        s_rt = sem("moe_input_transposed")
        s_h2 = sem("moe_input_t_copied")
        s_lg = {0: sem("logits_0"), 1: sem("logits_1")}
        s_gd = {0: sem("gate_gap_0"), 1: sem("gate_gap_1")}
        s_ge = {0: sem("gate_exp_0"), 1: sem("gate_exp_1")}
        s_cb = {0: sem("combine_0"), 1: sem("combine_1")}
        s_cbt = {0: sem("combine_transposed_0"), 1: sem("combine_transposed_1")}
        s_wp = {0: sem("combine_parts_copied_0"), 1: sem("combine_parts_copied_1")}
        s_wf = sem("combine_parts_copied_as_float32")
        s_wb = {0: sem("combine_spread_0"), 1: sem("combine_spread_1")}
        s_up = {0: sem("up_done_0"), 1: sem("up_done_1")}
        s_si = {0: sem("silu_done_0"), 1: sem("silu_done_1")}
        s_hu = sem("gated_up_1")
        s_hid = {0: sem("hidden_scaled_0"), 1: sem("hidden_scaled_1")}
        s_dn = {0: sem("down_done_0"), 1: sem("down_done_1")}
        s_yo = {0: sem("layer_out_done_0"), 1: sem("layer_out_done_1")}
        s_yc = {0: sem("layer_out_copied_0"), 1: sem("layer_out_copied_1")}
        s_yt = {0: sem("layer_out_transposed_0"), 1: sem("layer_out_transposed_1")}
        s_dist = sem("squared_distance")
        s_x1 = sem("x1_done")
        s_xm = sem("x1_with_experts_done")
        s_x2 = sem("x2_done")
        s_out = sem("zero_rows_and_out_stored")
        s_rs = sem("rel_scores")
        s_rm = sem("rel_max_over_key_tiles")
        s_rmt = sem("rel_max_transposed")
        s_rc = sem("rel_max_over_keys")
        s_rct = sem("rel_max_row_transposed")
        s_rcs = sem("rel_max_split")
        s_rsh = sem("rel_scores_shifted")
        s_link2 = sem("rel_vector_chain")

        block = ctx.enter_context(nc.Block())

        col_loads = [(col[n][:], dram[n].rearrange("(p o) -> p o", o=1)) for n in cols]
        loads = [(W[n][:], dram[n]) for n in names] + [
            (wdkv[:], dram["L0_ffn_Wdkv"]), (wuk[:], dram["L0_ffn_Wuk"]), (wuv[:], dram["L0_ffn_Wuv"]),
            (gate_w[:], dram["L0_ffn_gate_w"]), (cen_t[:], dram["centroid_t"]), 
            (w1[:], dram["L0_ffn_w1"].rearrange("e c f -> c e f")),
            (wg[:], dram["L1_ffn_Wg"].rearrange("e c f -> c e f")),
            (wu[:], dram["L1_ffn_W1"].rearrange("e c f -> c e f")),
            (bv0[:], dram["L0_attn_bv"].rearrange("(o d) -> o d", o=1).to_broadcast([P, D])),
            (bv1[:], dram["L1_attn_bv"].rearrange("(o d) -> o d", o=1).to_broadcast([P, D])),
            (tmp[:].rearrange("p a b -> p (a b)"),
             dram["L1_ffn_centroid"].rearrange("(o e) d -> o (e d)", o=1)[:, 0:4 * D].to_broadcast([P, 4 * D])),
            (x1[:].rearrange("p a b -> p (a b)"),
             dram["L1_ffn_centroid"].rearrange("(o e) d -> o (e d)", o=1)[:, 4 * D:8 * D].to_broadcast([P, 4 * D])),
        ] + [(b2[32 * n:32 * n + E, :], dram["L1_ffn_b2"]) for n in range(3)] + col_loads
        for e in range(E):
            loads.append((w2[:, e, :, :], dram["L0_ffn_w2"][e].rearrange("(c p) d -> p c d", p=P)))
            loads.append((wd[:, e, :, :], dram["L1_ffn_W2"][e].rearrange("(c p) d -> p c d", p=CW)))
        bias_loads = [(bg[:], dram["L1_ffn_bg"]),
                      (bu[:], dram["L1_ffn_b1"])]
        NLINKP = 6
        NLOAD = 16 * (len(loads) + 2)
        SCR = {"win": 16 * 6, "mla": 16 * 6, "rel": 16 * 9}
        QST = {"win": 16 * 4, "mla": 16 * 4, "rel": 16 * 7}
        KST = {"win": 16 * 3, "mla": 16 * 3, "rel": 16 * 6}

        @block.sync
        def _(sp):
            rel_t = dram["rel_emb_t"]
            tail = NREL - 256
            relx = probs[0:DH, 0:1024]
            sp.dma_start(relx[:, 0:256], rel_t[:, tail:NREL]).then_inc(s_relx, 16)
            sp.dma_start(relx[:, 256:256 + NREL], rel_t).then_inc(s_relx, 16)
            with nc.allow_non_contiguous_dma(reason="one row repeated, and short biases"):
                for dst, src in bias_loads:
                    sp.dma_start(dst.rearrange("p e c -> p (e c)"), src).then_inc(s_load, 16)
                sp.wait_ge(s_b2, 1)
                for dst, src in loads:
                    sp.dma_start(dst, src).then_inc(s_load, 16)
            sp.wait_ge(s_vset, 1)
            sp.dma_start(zrow_d.rearrange("a (b c) -> (a b) c", c=P), wparts[:, 0:P]).then_inc(s_out, 16)
            sp.wait_ge(s_vset, 2)
            sp.wait_ge(s_out, 16)
            sp.dma_start(k_stack[64:SHIFT].rearrange("p h t -> p (h t)"),
                         zrow_d[0:1].to_broadcast([SHIFT - 64, H * T])).then_inc(s_zero, 16)
            for p in range(3):
                sp.dma_start(rel_d[p], k_stack[0:DH, 2 * p:2 * p + 2, :].rearrange("p a b -> p (a b)"))\
                  .then_inc(s_rel_sp, 16)
            sp.wait_ge(s_rel_sp, 48)
            for n in range(2):
                for s, p in enumerate((0, 1, 2, 0, 1, 0)):
                    sp.dma_start(rel_stack[64 * n + DH * s:64 * n + DH * s + DH, n:2 * T],
                                 rel_d[p][:, 0:2 * T - n]).then_inc(s_rel_ld, 16)
            sp.wait_ge(s_load, NLOAD)
            sp.wait_ge(s_vset, 3)
            sp.wait_ge(s_out, 16)
            def store_parts(e, a):
                sp.wait_ge(s_parts[a], e * 2 + 2)
                for p in range(3):
                    if a == "rel":
                        parts = (("qe", q_parts[:, p * T:p * T + T]),
                                 ("qo", q_parts[:, 3 * T + p * T:3 * T + p * T + T]))
                    else:
                        parts = (("q", q_plain[:, p, :]),)
                    for n, src in parts + (("k", k_parts[:, p, :]),):
                        dst = scr[a, n][DH * p:DH * p + DH].rearrange("d h t -> h d t")
                        sp.dma_start(dst, src).then_inc(s_scr[a], 16)

            def load_q_stack(e, a):
                sp.wait_ge(s_scr[a], e * SCR[a] + SCR[a])
                sp.dma_start(q_stack[SHIFT:SHIFT + 2].rearrange("p h t -> p (h t)"), zrow_d)\
                  .then_inc(s_stk[a], 16)
                for n, name in enumerate(("qe", "qo") if a == "rel" else ("q",)):
                    for s, m, p in ((0, 3, 0), (3, 2, 1), (5, 1, 2)):
                        r = 64 * n + DH * s
                        src = scr[a, name][DH * p:DH * p + DH].rearrange("(o d) h t -> o d (h t)", o=1)
                        sp.dma_start(q_stack[r:r + DH * m], src.to_broadcast([m, DH, H * T]))\
                          .then_inc(s_stk[a], 16)

            def load_shift(e, a, half):
                sp.wait_ge(s_cp[a], e * 2 + half + 1)
                for p in range(2):
                    dst = q_stack[SHIFT + p:SHIFT + p + 1, half * HT:half * HT + HT]\
                        .rearrange("o h (j q) -> o (h j) q", j=NT)
                    sp.dma_start(dst, cpart[:, half, p, :]).then_inc(s_sh[a, half], 16)

            def load_x(e):
                sp.dma_start(x[:], dram["L0_attn_x"][e].rearrange("(j p) d -> p j d", p=P)).then_inc(s_x, 16)

            def element(i, final):
                load_shift(i, "mla", 0)
                load_shift(i, "mla", 1)
                store_parts(i, "win")
                sp.wait_ge(s_st["mla"], i * SCORED + SCORED)
                load_q_stack(i, "win")
                load_shift(i, "win", 0)
                load_shift(i, "win", 1)
                if not final:
                    sp.wait_ge(s_x1, i + 1)
                    load_x(i + 1)
                store_parts(i, "rel")
                sp.wait_ge(s_st["win"], i * 8 + 8)
                load_q_stack(i, "rel")
                if not final:
                    store_parts(i + 1, "mla")
                    sp.wait_ge(s_rs, i * NS + NS)
                    sp.dma_start(k_stack[64:SHIFT].rearrange("p h t -> p (h t)"),
                                 zrow_d[0:1].to_broadcast([SHIFT - 64, H * T])).then_inc(s_zero, 16)
                    load_q_stack(i + 1, "mla")
                sp.wait_ge(s_x2, i * 4 + 4)
                sp.dma_start(dram["out"][i].rearrange("(j p) d -> p j d", p=P), x1[:]).then_inc(s_out, 16)

            load_x(0)
            store_parts(0, "mla")
            load_q_stack(0, "mla")
            with sp.Fori(0, B - 1) as i:
                element(i, False)
            element(B - 1, True)
            sp.wait_ge(s_out, 16 * B + 16)

        @block.gpsimd
        def _(pool):
            made = [0]

            def done(ins):
                made[0] += 1
                ins.then_inc(s_const, 1)

            def after():
                pool.wait_ge(s_const, made[0])

            done(pool.memset(ident[:], 0.0))
            done(pool.memset(causal_qk[:], 0.0))
            done(pool.memset(causal_kq[:], 0.0))
            done(pool.memset(band_qk[:], 0.0))
            done(pool.memset(band_kq[:], 0.0))
            done(pool.memset(sel_w[:], 0.0))
            done(pool.memset(sel_c[:], 0.0))
            done(pool.memset(power[:, 0, :], 0.5))
            done(pool.memset(one[:], 1.0))
            done(pool.memset(power[:, 1, :], -0.5))
            for e in range(E):
                done(pool.memset(rev[:, :, e:e + 1], float(E - e)))
            after()

            def keep(t, op, fill, base, pattern, mult):
                done(pool.affine_select(out=t, in_=t, compare_op=op, fill=fill, base=base,
                                        pattern=pattern, channel_multiplier=mult))

            keep(ident[:], ALU.not_equal, 1.0, 0, [[-1, P]], 1)
            keep(causal_qk[:], ALU.is_ge, LOW, 0, [[-1, P]], 1)
            keep(causal_kq[:], ALU.is_ge, LOW, 0, [[1, P]], -1)
            keep(band_qk[:], ALU.is_ge, LOW, WIN, [[-1, WQ]], 1)
            keep(band_kq[:], ALU.is_ge, LOW, 0, [[1, WQ]], -1)
            for n in range(3):
                keep(sel_w[:], ALU.not_equal, 1.0, -32 * n, [[-1, E], [0, P]], 1)
                after()
            for n in range(2):
                keep(sel_c[:], ALU.not_equal, 1.0, -32 * n, [[-1, 2], [0, P]], 1)
                after()
            keep(band_qk[:], ALU.is_ge, LOW, WIN - 1 - WIN, [[1, WQ]], -1)
            keep(band_kq[:], ALU.is_ge, LOW, WIN - 1, [[-1, WQ]], 1)
            cnt = [0]

            def link(e, ins):
                cnt[0] += 1
                ins.then_inc(s_linkp, 1)
                pool.wait_ge(s_linkp, e * NLINKP + cnt[0])

            def power_of(e, n):
                pool.wait_ge(s_gs, e * 5 + n + 1)
                if n == 4:
                    nc.gpsimd.tensor_tensor(roots[:], tc[:, 0:3:2],
                                            power[:, 0, 0:2 * NT].rearrange("p (n j) -> p n j", n=2),
                                            ALU.pow).then_inc(s_pow, 1)
                else:
                    nc.gpsimd.tensor_tensor(rstd[:], rvar[:], power[:, 1, 0:NT], ALU.pow).then_inc(s_pow, 1)

            def split_parts(e, a, first=False):
                if a == "mla":
                    cnt[0] = 0
                if a != "mla":
                    before = {"win": "mla", "rel": "win"}[a]
                    pool.wait_ge(s_scr[before], e * SCR[before] + SCR[before])
                elif not first:
                    pool.wait_ge(s_scr["rel"], e * SCR["rel"])
                pool.wait_ge(s_qkf[a], e * 2 + 2)
                if a == "rel":
                    q = q_f[:].rearrange("p (u n) -> p n u", n=2)
                    qp = q_parts[:].rearrange("p (n x) -> p n x", n=2)
                    qd = [qp[:, :, p * T:p * T + T - 1:2] for p in range(3)]
                else:
                    q = q_f[:]
                    qd = [q_plain[:, p] for p in range(3)]
                g = nc.gpsimd
                ones = one[:].to_broadcast([P, T])
                if a == "rel":
                    ones = ones.rearrange("p (n u) -> p n u", n=2)
                g.tensor_tensor(qd[0], q, ones, ALU.mult)
                link(e, g.tensor_tensor(k_parts[:, 0], k_f[:], one[:].to_broadcast([P, T]), ALU.mult))
                g.tensor_tensor(qd[1], q, qd[0], ALU.subtract)
                g.tensor_tensor(k_parts[:, 1], k_f[:], k_parts[:, 0], ALU.subtract)
                g.tensor_tensor(q, q, qd[0], ALU.subtract)
                link(e, g.tensor_tensor(k_f[:], k_f[:], k_parts[:, 0], ALU.subtract))
                g.tensor_tensor(qd[2], q, qd[1], ALU.subtract).then_inc(s_parts[a], 1)
                g.tensor_tensor(k_parts[:, 2], k_f[:], k_parts[:, 1], ALU.subtract).then_inc(s_parts[a], 1)

            def first_stages(e, first=False):
                power_of(e, 0)
                power_of(e, 1)
                split_parts(e, "mla", first)

            def second_stages(e):
                split_parts(e, "win")
                power_of(e, 2)
                pool.wait_ge(s_out, e * 16 + 16)
                nc.gpsimd.tensor_tensor(x1[:], x[:], xn[:], ALU.add).then_inc(s_x1, 1)
                power_of(e, 3)
                power_of(e, 4)
                split_parts(e, "rel")

            first_stages(0, True)
            with pool.Fori(0, B - 1) as i:
                second_stages(i)
                first_stages(i + 1)
            cnt[0] = 2
            second_stages(B - 1)
            assert cnt[0] == NLINKP, cnt[0]

        @block.scalar
        def _(act):
            def ident_of(out, in_, bias=0.0, scale=1.0):
                return nc.scalar.activation(out, in_, ACT.Identity, bias=bias, scale=scale)

            act.wait_ge(s_load, NLOAD)
            act.wait_ge(s_vset, 3)

            def copy_qk(e, a, n, bank, bias, scale=1.0, first=False):
                if a != "mla":
                    act.wait_ge(s_parts[{"win": "mla", "rel": "win"}[a]], e * 2 + 2)
                elif not first:
                    act.wait_ge(s_parts["rel"], e * 2)
                act.wait_ge(s_proj[a], e * 2 + n + 1)
                ident_of((q_f, k_f)[n][:], PS[:, bank, :], bias=bias, scale=scale).then_inc(s_qkf[a], 1)

            def load_k_stack(e, a):
                act.wait_ge(s_scr[a], e * SCR[a] + SCR[a])
                for n in range(2 if a == "rel" else 1):
                    for s, m in ((0, 3), (3, 2), (5, 1)):
                        r = 64 * n + DH * s
                        act.dma_start(k_stack[r:r + DH * m], scr[a, "k"][0:DH * m]).then_inc(s_stkk[a], 16)

            def copy_xn_t(e):
                act.wait_ge(s_tr, e * 3 + 1)
                ident_of(xn_t[:], PS[:, 7, :]).then_inc(s_xnt, 1)

            def copy_h_t(e):
                act.wait_ge(s_tr, e * 3 + 2)
                ident_of(h_t[:], PS[:, 7, :], scale=col["L0_ffn_g1"][:, 0:1]).then_inc(s_xnt, 1)

            def copy_win_q(e):
                copy_qk(e, "win", 0, 7, col["L0_attn_bq"][:, 0:1])

            def copy_win_k(e):
                copy_qk(e, "win", 1, 7, bk0s[:, 0:1], SCALE)

            def copy_c_t(e):
                act.wait_ge(s_lat, e + 1)
                ident_of(c_t[:], PS[0:LAT, 7, :]).then_inc(s_ct, 1)

            def copy_mla_q(e, first=False):
                copy_qk(e, "mla", 0, 7, 0.0, first=first)

            def copy_mla_k(e, first=False):
                copy_qk(e, "mla", 1, 7, 0.0, SCALE, first=first)

            def copy_mla_v(e):
                act.wait_ge(s_vproj["mla"], e + 1)
                ident_of(vm[:, :, :, 0:DH], PS[:, 7, :].rearrange("p (j h d) -> p j h d", j=NT, h=H))\
                    .then_inc(s_v["mla"], 1)

            def element(i, final):
                def copy_quarter_back(a, q):
                    act.wait_ge(s_ot[a], i * 4 + q + 1)
                    ident_of(o_t[a][:, q * P:q * P + P], PS[:, 7, 0:P]).then_inc(s_otc[a], 1)

                copy_win_q(i)
                copy_win_k(i)
                copy_mla_v(i)
                def exp_mla(h, bank, n, parts):
                    done_before = 3 * h + parts if h < HT else 3 * HT + h - HT
                    act.wait_ge(s_st["mla"], i * SCORED + done_before + 1)
                    o = (h // 4) % 2 * 5120 + (h % 4) * 1280 + parts * T
                    width = min(n * T, 1280 - parts * T)
                    nc.scalar.activation(probs[:, o:o + width],
                                         PS[:, bank:bank + n, :].rearrange("p b c -> p (b c)")[:, 0:width],
                                         ACT.Exp).then_inc(s_ex["mla"], 1)

                for h in range(HT):
                    for b in range(3):
                        exp_mla(h, 3 + b, 1, b)
                for h in range(HT, H):
                    if h % 4 == 0:
                        act.wait_ge(s_pv["mla"], i * 4 + h // 4 - 1)
                    exp_mla(h, 3 * (h % 2), 3, 0)
                load_k_stack(i, "win")
                act.wait_ge(s_rt, i + 1)
                ident_of(h_t[:], PS[:, 7, :], scale=col["L0_ffn_g2"][:, 0:1]).then_inc(s_h2, 1)
                act.wait_ge(s_pv["mla"], i * 4 + 4)
                for n in range(H // 2):
                    if n >= 4 and n % 2 == 0:
                        act.wait_ge(s_pv["win"], i * 4 + n // 2 - 1)
                    act.wait_ge(s_st["win"], i * (H // 2) + n + 1)
                    b = 3 * (n % 2)
                    p4 = probs[:, (n // 2) % 2 * 5120:(n // 2) % 2 * 5120 + 2560].rearrange("p (r c) -> p r c", r=4)
                    p2 = p4[:, 2 * (n % 2):2 * (n % 2) + 2, :]
                    nc.scalar.activation(p2[:, :, 0:3 * WQ], PS[:, b:b + 2, 0:3 * WQ], ACT.Exp)
                    nc.scalar.activation(p2[:, :, 3 * WQ:3 * WQ + P],
                                         PS[:, b + 2, 0:2 * P].rearrange("p (r c) -> p r c", r=2),
                                         ACT.Exp).then_inc(s_ex["win"], 1)
                    if n == 0:
                        act.wait_ge(s_gd[0], i + 1)
                        nc.scalar.activation(tc[:, 5], tc[:, 4], ACT.Exp).then_inc(s_ge[0], 1)
                N0 = E * C0
                for n in range(N0):
                    act.wait_ge(s_up[0], i * N0 + n + 1)
                    if n >= NA:
                        act.wait_ge(s_hid[0], i * N0 + n - NA + 1)
                    nc.scalar.activation(hid_a[:, n % NA], PS[:, n % 4, :], ACT.Silu).then_inc(s_si[0], 1)
                    m = n - (NA - 1)
                    if 0 < m < 2 * NT and m % 2 == 1:
                        copy_quarter_back("win", m // 2)
                act.wait_ge(s_yo[0], i + 1)
                ident_of(y_t, PS[:, 6, :], bias=col["L0_attn_bo"][:, 0:1]).then_inc(s_yc[0], 1)
                act.wait_ge(s_tr, i * 3 + 3)
                ident_of(xn_t[:], PS[:, 0, :]).then_inc(s_xnt, 1)
                copy_qk(i, "rel", 0, 1, col["L1_attn_bq"][:, 0:1])
                copy_qk(i, "rel", 1, 2, bk1s[:, 0:1], SCALE)
                act.wait_ge(s_gd[1], i + 1)
                nc.scalar.activation(tc[:, 5], tc[:, 4], ACT.Exp).then_inc(s_ge[1], 1)
                N1 = E * C1
                for n in range(N1):
                    act.wait_ge(s_up[1], i * N1 + n + 1)
                    if n >= NA:
                        act.wait_ge(s_hu, i * N1 + n - NA + 1)
                    nc.scalar.activation(hid_a[0:CW, n % NA], PS[0:CW, 2 * (n % 2), :], ACT.Silu,
                                         bias=bg[:, n // C1, n % C1:n % C1 + 1]).then_inc(s_si[1], 1)
                    if n == 1:
                        act.wait_ge(s_wp[1], i + 1)
                        ident_of(wt_full[:], wparts[0:96]).then_inc(s_wf, 1)
                    if n == N1 // 2:
                        load_k_stack(i, "rel")
                act.wait_ge(s_yo[1], i + 1)
                ident_of(y_t, PS[:, 6, :], bias=col["L1_attn_bo"][:, 0:1]).then_inc(s_yc[1], 1)
                pr = probs[:, 0:NT * H * P].rearrange("p (k h l) -> p k h l", k=NT, h=H)

                for t in range(NS):
                    q, hh = t // 2, t % 2
                    if t >= NSQ and t % NSQ == 0:
                        act.wait_ge(s_pv["rel"], i * 4 + t // NSQ)
                    act.wait_ge(s_rsh, i * NS + t + 1)
                    b = 2 * (t % 3)
                    l = q % (P // LB) * LB
                    nc.scalar.activation(pr[:, :, hh * HT:hh * HT + HT, l:l + LB],
                                         PS[:, b:b + 2, :].rearrange("p b (k h l) -> p (b k) h l", k=2, h=HT),
                                         ACT.Exp).then_inc(s_ex["rel"], 1)
                    if t + 2 >= NSQ + 3 and (t + 2) % NSQ == 3:
                        copy_quarter_back("rel", (t + 2) // NSQ - 1)
                    if not final and t + 2 == 13:
                        copy_xn_t(i + 1)
                    if not final and t + 2 == 14:
                        copy_h_t(i + 1)
                    if not final and t + 2 == 15:
                        copy_mla_q(i + 1)
                    if not final and t + 2 == 16:
                        copy_c_t(i + 1)
                    if not final and t + 2 == 21:
                        copy_mla_k(i + 1)
                    if not final and t + 2 == NS:
                        act.wait_ge(s_rs, i * NS + NS)
                        load_k_stack(i + 1, "mla")
                copy_quarter_back("rel", NT - 1)

            copy_xn_t(0)
            copy_h_t(0)
            copy_mla_q(0, True)
            copy_c_t(0)
            copy_mla_k(0, True)
            load_k_stack(0, "mla")
            with act.Fori(0, B - 1) as i:
                element(i, False)
            element(B - 1, True)

        NLINK = 65

        @block.vector
        def _(dve):
            v = nc.vector
            cnt = [0]

            def link0(ins):
                cnt[0] += 1
                ins.then_inc(s_link0, 1)
                dve.wait_ge(s_link0, cnt[0])

            v.memset(wparts[:], 0.0).then_inc(s_vset, 1)
            v.memset(b2[:], 0.0).then_inc(s_b2, 1)
            v.memset(rel_stack[:], 0.0)
            v.memset(q_stack[:], 0.0)
            v.memset(k_stack[0:96], 0.0)
            v.memset(k_stack[96:P], 1.0)
            v.memset(crow[:], 0.0)
            v.memset(q_parts[:], 0.0)
            v.memset(negmax[:], 0.0)
            v.memset(PS[:, 6:8, :], 0.0)
            v.memset(wtok[:], 0.0)
            v.memset(v0[:], 0.0)
            v.memset(v1[:], 0.0)
            link0(v.memset(vm[:], 0.0))
            v.memset(v0[:, :, :, DH:DH + 1], 1.0)
            v.memset(v1[:, :, :, DH:DH + 1], 1.0)
            v.memset(vm[:, :, :, DH:DH + 1], 1.0)
            dve.wait_ge(s_relx, 32)
            relx = probs[0:DH, 0:1024]
            link0(v.tensor_copy(relx[:, 256 + NREL:1024],
                                relx[:, 255 + NREL:256 + NREL].to_broadcast([DH, 1024 - 256 - NREL])))
            rp = [k_stack[0:DH, 2 * p:2 * p + 2, :].rearrange("p a b -> p (a b)") for p in range(3)]
            link0(v.tensor_copy(rp[0], relx))
            link0(v.tensor_tensor(relx, relx, rp[0], ALU.subtract))
            link0(v.tensor_copy(rp[1], relx))
            v.tensor_tensor(rp[2], relx, rp[1], ALU.subtract).then_inc(s_vset, 1)
            dve.wait_ge(s_const, NCONST)
            dve.wait_ge(s_load, NLOAD)
            v.tensor_copy(identb[:], ident[:])
            v.tensor_scalar_mul(bk0s[:], col["L0_attn_bk"][:], SCALE)
            v.tensor_scalar_mul(bk1s[:], col["L1_attn_bk"][:], SCALE)
            v.tensor_tensor(xn[:], tmp[:], tmp[:], ALU.mult)
            link0(v.tensor_tensor(x[:], x1[:], x1[:], ALU.mult))
            v.tensor_reduce(cnorm[:, 0:NT], xn[:], AX.X, ALU.add)
            v.tensor_reduce(cnorm[:, NT:E], x[:], AX.X, ALU.add).then_inc(s_vset, 1)
            dve.wait_ge(s_vset, 3)
            def norm_stats(src, chain):
                for j in range(NT):
                    last = v.bn_stats(stats[:, j], src[:, j])
                chain(last)
                v.memset(pause[:], 0.0)
                for j in range(NT):
                    last = v.bn_aggr(mv[:, j], stats[:, j])
                chain(last)

            def norm_variance(e, eps, rms, chain):
                if rms:
                    chain(v.tensor_tensor(rvar[:], mv[:, :, 0], mv[:, :, 0], ALU.mult))
                    chain(v.tensor_tensor(rvar[:], rvar[:], mv[:, :, 1], ALU.add))
                    v.tensor_scalar_add(rvar[:], rvar[:], eps).then_inc(s_gs, 1)
                else:
                    v.tensor_scalar_add(rvar[:], mv[:, :, 1], eps).then_inc(s_gs, 1)

            def norm_apply(e, src, dst, n, rms):
                dve.wait_ge(s_pow, e * 5 + n + 1)
                for j in range(NT):
                    if rms:
                        last = v.tensor_scalar_mul(dst[:, j], src[:, j], rstd[:, j:j + 1])
                    else:
                        last = v.tensor_scalar(dst[:, j], src[:, j], mv[:, j, 0:1], rstd[:, j:j + 1],
                                               ALU.subtract, ALU.mult)
                return last

            def linkf(e, n, ins):
                ins.then_inc(s_linkf, 1)
                dve.wait_ge(s_linkf, e * 6 + n)

            def first_norm_a(e):
                n = [0]

                def chain(ins):
                    n[0] += 1
                    linkf(e, n[0], ins)

                dve.wait_ge(s_x, e * 16 + 16)
                norm_stats(x, chain)
                norm_variance(e, 1e-5, False, chain)

            def first_norm_b(e):
                norm_apply(e, x, xn, 0, False).then_inc(s_xn, 1)

            def first_norm_c(e):
                n = [2]

                def chain(ins):
                    n[0] += 1
                    linkf(e, n[0], ins)

                dve.wait_ge(s_xn, e * 2 + 1)
                norm_stats(xn, chain)
                norm_variance(e, 1e-6, True, chain)

            def first_norm_d(e):
                norm_apply(e, xn, tmp, 1, True).then_inc(s_xr, 1)

            def copy_v(e, a, dst, bias):
                dve.wait_ge(s_vproj[a], e + 1)
                out = dst[:, :, :, 0:DH]
                src = PS[:, 7, :].rearrange("p (j h d) -> p j h d", j=NT, h=H)
                for j in range(NT):
                    last = v.tensor_tensor(out[:, j], src[:, j], bias[:].rearrange("p (h d) -> p h d", h=H), ALU.add)
                last.then_inc(s_v[a], 1)

            def element(i, final):
                cnt[0] = 0

                def link(ins):
                    cnt[0] += 1
                    ins.then_inc(s_link, 1)
                    dve.wait_ge(s_link, i * NLINK + cnt[0])

                def norm(src, dst, n, eps, rms, out_sem, out_value):
                    norm_stats(src, link)
                    norm_variance(i, eps, rms, link)
                    norm_apply(i, src, dst, n, rms).then_inc(out_sem, 1)
                    dve.wait_ge(out_sem, out_value)

                def split_max(a, half):
                    dve.wait_ge(s_mxt[a], i * 2 + half + 1)
                    if a == "win":
                        dve.wait_ge(s_sh["mla", half], i * 32 + 32)
                    src = PS[0:NT * HT, 6, half * P:half * P + P]
                    link(v.tensor_copy(cpart[:, half, 0], src))
                    v.tensor_tensor(cpart[:, half, 1], src, cpart[:, half, 0], ALU.subtract).then_inc(s_cp[a], 1)

                def copy_o_raw(a, first, end):
                    for g in range(first, end):
                        dve.wait_ge(s_pv[a], i * 4 + g + 1)
                        v.tensor_copy(o_raw[:, g, :], PS[:, 6 + g % 2, :]).then_inc(s_or[a], 1)

                def normalise(a):
                    dve.wait_ge(s_ort[a], i + 1)
                    src = PS[:, 0:4, :].rearrange("p j (h c) -> p j h c", h=H)
                    link(v.reciprocal(rden[:], src[:, :, :, DH]))
                    for j in range(NT):
                        last = v.tensor_tensor(o_tok[:, j].rearrange("p (h d) -> p h d", h=H), src[:, j, :, 0:DH],
                                               rden[:, j].rearrange("p (h o) -> p h o", o=1).to_broadcast([P, H, DH]),
                                               ALU.mult)
                    last.then_inc(s_on[a], 1)
                    dve.wait_ge(s_ot[a], i + 1)
                    v.tensor_copy(o_t[a][:], PS[:, 4, :]).then_inc(s_otc[a], 1)

                def spread(t):
                    return t.rearrange("p (j o) -> p j o", o=1).to_broadcast([P, NT, E])

                def normalise_quarter(a, q):
                    dve.wait_ge(s_ort[a], i * 4 + q + 1)
                    src = PS[:, 7, :].rearrange("p (h c) -> p h c", h=H)
                    link(v.reciprocal(rden[:, q], src[:, :, DH]))
                    v.tensor_tensor(o_quarter[:].rearrange("p (h d) -> p h d", h=H), src[:, :, 0:DH],
                                    rden[:, q].rearrange("p (h o) -> p h o", o=1).to_broadcast([P, H, DH]),
                                    ALU.mult).then_inc(s_on[a], 1)

                def top_two(k):
                    score = top[:, 0]
                    link(v.tensor_reduce(tc[:, 0], score, AX.X, ALU.max))
                    link(v.tensor_tensor(top[:, 1], score, spread(tc[:, 0]), ALU.is_equal))
                    link(v.tensor_tensor(top[:, 1], top[:, 1], rev[:], ALU.mult))
                    link(v.tensor_reduce(tc[:, 1], top[:, 1], AX.X, ALU.max))
                    link(v.tensor_tensor(top[:, 2], top[:, 1], spread(tc[:, 1]), ALU.is_equal))
                    link(v.scalar_tensor_tensor(top[:, 3], top[:, 2], -3e38, score, ALU.mult, ALU.add))
                    if k == 0:
                        link(v.tensor_reduce(tc[:, 2], top[:, 3], AX.X, ALU.max))
                        v.tensor_tensor(tc[:, 4], tc[:, 2], tc[:, 0], ALU.subtract).then_inc(s_gd[k], 1)
                    else:
                        v.tensor_reduce(tc[:, 2], top[:, 3], AX.X, ALU.max).then_inc(s_gs, 1)
                        dve.wait_ge(s_gs, i * 5 + 5)
                    link(v.tensor_tensor(top[:, 4], top[:, 3], spread(tc[:, 2]), ALU.is_equal))
                    link(v.tensor_tensor(top[:, 4], top[:, 4], rev[:], ALU.mult))
                    link(v.tensor_reduce(tc[:, 3], top[:, 4], AX.X, ALU.max))
                    link(v.tensor_tensor(top[:, 5], top[:, 4], spread(tc[:, 3]), ALU.is_equal))
                    if k == 1:
                        dve.wait_ge(s_pow, i * 5 + 5)
                        v.tensor_tensor(tc[:, 4], roots[:, 1], roots[:, 0], ALU.subtract).then_inc(s_gd[k], 1)

                def weigh_two(k):
                    dve.wait_ge(s_ge[k], i + 1)
                    link(v.tensor_scalar_add(tc[:, 6], tc[:, 5], 1.0))
                    link(v.reciprocal(tc[:, 6], tc[:, 6]))
                    link(v.tensor_tensor(tc[:, 7], tc[:, 5], tc[:, 6], ALU.mult))
                    v.tensor_tensor(top[:, 1], top[:, 2], spread(tc[:, 6]), ALU.mult)
                    link(v.tensor_tensor(top[:, 4], top[:, 5], spread(tc[:, 7]), ALU.mult))
                    link(v.tensor_tensor(top[:, 6], top[:, 1], top[:, 4], ALU.add))
                    link(v.tensor_copy(wt_hi[:], top[:, 6]))
                    v.tensor_copy(wtok[:, :, 0:E], wt_hi[:])
                    link(v.tensor_tensor(top[:, 6], top[:, 6], wt_hi[:], ALU.subtract))
                    link(v.tensor_copy(wt_hi[:], top[:, 6]))
                    v.tensor_copy(wtok[:, :, 32:32 + E], wt_hi[:])
                    v.tensor_tensor(wtok[:, :, 64:64 + E], top[:, 6], wt_hi[:], ALU.subtract).then_inc(s_cb[k], 1)

                def copy_combine(k, bank):
                    dve.wait_ge(s_cbt[k], i + 1)
                    v.tensor_copy(wparts[0:96], PS[0:96, bank, :]).then_inc(s_wp[k], 1)

                def max_mla(n, j, h0, nh, per, bank, banks):
                    keys = P * (j + 1)
                    dve.wait_ge(s_sc["mla"], i * NG + n + 1)
                    src = PS[:, bank:bank + banks, 0:per * keys].rearrange("p b (h c) -> p b h c", h=per)
                    v.tensor_reduce(negmax[:, h0 // HT, h0 % HT:h0 % HT + nh, j], src, AX.X, ALU.max,
                                    negate=True).then_inc(s_mx["mla"], 1)

                for n, (j, h0, nh, per) in enumerate(MLA_TWO):
                    max_mla(n, j, h0, nh, per, 2 * (n % 3), 2)
                    if n == NG2 - 2:
                        copy_v(i, "win", v1, bv0)
                for m, (j, h0, nh, per) in enumerate(MLA_ONE):
                    if m == 1:
                        split_max("mla", 0)
                    max_mla(NG2 + m, j, h0, nh, per, m % 3, 1)
                split_max("mla", 1)
                copy_o_raw("mla", 0, 4)
                normalise("mla")
                for n, (j, h0) in enumerate(WIN_MAX):
                    b = 2 * (n % 3)
                    lo = WIN if j == 0 else 0
                    dve.wait_ge(s_sc["win"], i * 16 + n + 1)
                    src = PS[:, b:b + 2, 0:2 * WQ].rearrange("p b (h c) -> p b h c", h=2)[:, :, :, lo:WQ]
                    v.tensor_reduce(negmax[:, h0 // HT, h0 % HT:h0 % HT + 4, j], src, AX.X, ALU.max, negate=True)\
                     .then_inc(s_mx["win"], 1)
                    if n == len(WIN_MAX) // 2 + 2:
                        split_max("win", 0)
                    if n == 0:
                        dve.wait_ge(s_mo, i + 1)
                        link(v.tensor_tensor(xn[:].rearrange("p j d -> p (j d)"), PS[:, 7, :],
                                             xn[:].rearrange("p j d -> p (j d)"), ALU.add))
                        norm_stats(xn, link)
                        norm_variance(i, 1e-6, True, link)
                    if n == 2:
                        norm_apply(i, xn, tmp, 2, True).then_inc(s_rr, 1)
                split_max("win", 1)
                dve.wait_ge(s_lg[0], i + 1)
                link(v.tensor_copy(top[:, 0], PS[:, 7, 0:NT * E].rearrange("p (j e) -> p j e", j=NT)))
                top_two(0)
                weigh_two(0)
                copy_o_raw("win", 0, 1)
                copy_combine(0, 7)
                copy_o_raw("win", 1, 4)
                N0 = E * C0
                for n in range(N0):
                    dve.wait_ge(s_si[0], i * N0 + n + 1)
                    if n % C0 == 0:
                        dve.wait_ge(s_wb[0], i * E + n // C0 + 1)
                    if n >= 3:
                        dve.wait_ge(s_dn[0], i * N0 + n - 2)
                    v.tensor_tensor(hid_b[:, n % 3], hid_a[:, n % NA], PS[:, 4 + n // C0 % 2, :], ALU.mult)\
                     .then_inc(s_hid[0], 1)
                    if n < 2 * NT and n % 2 == 1:
                        normalise_quarter("win", n // 2)
                dve.wait_ge(s_yt[0], i + 1)
                dve.wait_ge(s_x1, i + 1)
                link(v.tensor_tensor(x1[:].rearrange("p j d -> p (j d)"), PS[:, 7, :],
                                     x1[:].rearrange("p j d -> p (j d)"), ALU.add))
                norm(x1, xn, 3, 1e-5, False, s_xn, i * 2 + 2)
                link(v.tensor_tensor(tmp[:], xn[:], xn[:], ALU.mult))
                link(v.tensor_reduce(mv[:, :, 0], tmp[:], AX.X, ALU.add))
                dve.wait_ge(s_dist, i + 1)
                dots = PS[:, 4, 0:NT * E].rearrange("p (j e) -> p j e", j=NT)
                link(v.tensor_scalar(top[:, 7], dots, -2.0, None, ALU.mult))
                link(v.tensor_tensor(top[:, 6], spread(mv[:, :, 0]),
                                     cnorm[:].rearrange("p (o e) -> p o e", o=1).to_broadcast([P, NT, E]), ALU.add))
                link(v.tensor_tensor(top[:, 7], top[:, 7], top[:, 6], ALU.add))
                link(v.tensor_scalar_max(top[:, 0], top[:, 7], 1e-12))
                top_two(1)
                weigh_two(1)
                copy_v(i, "rel", v0, bv1)
                N1 = E * C1

                def gate(n):
                    dve.wait_ge(s_si[1], i * N1 + n + 1)
                    v.scalar_tensor_tensor(hid_b[0:CW, n % 3], PS[0:CW, 2 * (n % 2) + 1, :],
                                           bu[:, n // C1, n % C1:n % C1 + 1], hid_a[0:CW, n % NA],
                                           ALU.add, ALU.mult).then_inc(s_hu, 1)

                gate(0)
                copy_combine(1, 5)
                for n in range(N1):
                    e = n // C1
                    if n + 1 < N1:
                        gate(n + 1)
                    dve.wait_ge(s_hu, i * N1 + n + 1)
                    if n % C1 == 0:
                        dve.wait_ge(s_wb[1], i * E + e + 1)
                    if n >= 3:
                        dve.wait_ge(s_dn[1], i * N1 + n - 2)
                    v.tensor_tensor(hid_c[0:CW, n % 3], hid_b[0:CW, n % 3], PS[0:CW, 4 + e % 2, :], ALU.mult)\
                     .then_inc(s_hid[1], 1)
                    if not final and n == 4:
                        first_norm_a(i + 1)
                    if not final and n == 8:
                        first_norm_b(i + 1)
                    if not final and n == 12:
                        first_norm_c(i + 1)
                    if not final and n == 16:
                        first_norm_d(i + 1)
                base = i * NS
                cnt2 = [0]

                def link2(ins):
                    cnt2[0] += 1
                    ins.then_inc(s_link2, 1)
                    dve.wait_ge(s_link2, i * 2 * NS + cnt2[0])

                def max_tile(t):
                    b = 2 * (t % 3)
                    dve.wait_ge(s_rs, base + t + 1)
                    src = PS[:, b:b + 2, :].rearrange("p b (k c) -> p c (b k)", k=2)
                    if t >= 2:
                        dve.wait_ge(s_rmt, base + t - 1)
                    v.tensor_reduce(mcol[:, t % 2], src, AX.X, ALU.max).then_inc(s_rm, 1)

                def max_row(t):
                    dve.wait_ge(s_rmt, base + t + 1)
                    v.tensor_reduce(cm[:], PS[:, 6, 0:2 * P].rearrange("p (c k) -> p c k", c=2), AX.X, ALU.max,
                                    negate=True).then_inc(s_rc, 1)
                    dve.wait_ge(s_rct, base + t + 1)
                    src = PS[0:2, 6, 2 * P:3 * P]
                    if t >= 1:
                        dve.wait_ge(s_rsh, base + t)
                    link2(v.tensor_copy(crow[0:2], src))
                    link2(v.tensor_tensor(crow_mid[:], src, crow[0:2], ALU.subtract))
                    v.tensor_copy(crow[32:34], crow_mid[:]).then_inc(s_rcs, 1)

                def copy_quarter(q):
                    dve.wait_ge(s_pv["rel"], i * 4 + q + 1)
                    v.tensor_copy(o_raw[:, :, q * P:q * P + P],
                                  PS[:, 7, :].rearrange("p (g l) -> p g l", g=4)).then_inc(s_or["rel"], 1)

                def add_quarter(q):
                    dve.wait_ge(s_ao, i * 4 + q + 1)
                    if q == 0:
                        dve.wait_ge(s_xm, i + 1)
                    v.tensor_tensor(x1[:, q], PS[:, 7, P:2 * P], x1[:, q], ALU.add).then_inc(s_x2, 1)

                for t in range(NS + 1):
                    if t >= 1:
                        max_row(t - 1)
                    if t < NS:
                        max_tile(t)
                    if t == 0:
                        dve.wait_ge(s_yt[1], i + 1)
                        v.tensor_tensor(x1[:].rearrange("p j d -> p (j d)"), PS[:, 7, :],
                                        x1[:].rearrange("p j d -> p (j d)"), ALU.add).then_inc(s_xm, 1)
                    if t > NSQ and t % NSQ == 1 and t < NS:
                        copy_quarter(t // NSQ - 1)
                    if t >= NSQ + 2 and t % NSQ == 2:
                        normalise_quarter("rel", t // NSQ - 1)
                    if t >= NSQ + 4 and t % NSQ == 4:
                        add_quarter(t // NSQ - 1)
                copy_quarter(NT - 1)
                normalise_quarter("rel", NT - 1)
                add_quarter(NT - 1)

            first_norm_a(0)
            first_norm_b(0)
            first_norm_c(0)
            first_norm_d(0)
            with dve.Fori(0, B - 1) as i:
                element(i, False)
            assert cnt[0] == NLINK, cnt[0]
            element(B - 1, True)

        @block.tensor
        def _(pe):
            mm = nc.tensor.matmul
            pe.wait_ge(s_load, NLOAD)
            pe.wait_ge(s_vset, 3)
            pe.wait_ge(s_rel_ld, 192)
            def transpose_tiles(bank, src):
                for j in range(NT):
                    last = nc.tensor.transpose(PS[:, bank, j * P:j * P + P], src[:, j, :], ident[:])
                return last

            def by_token(bank, x_t, w, n):
                for j in range(NT):
                    last = mm(PS[:, bank, j * n:j * n + n], x_t[:, j * P:j * P + P], w, start=True, stop=True)
                return last

            def project_xn(e):
                pe.wait_ge(s_xn, e * 2 + 1)
                transpose_tiles(7, xn).then_inc(s_tr, 1)

            def project_h(e):
                pe.wait_ge(s_xr, e + 1)
                pe.wait_ge(s_xnt, e * 3 + 1)
                transpose_tiles(7, tmp).then_inc(s_tr, 1)

            def project_mla_q(e):
                pe.wait_ge(s_xnt, e * 3 + 2)
                mm(PS[:, 7, :], W["L0_ffn_Wq"][:], h_t[:], start=True, stop=True).then_inc(s_proj["mla"], 1)

            def project_latent(e):
                pe.wait_ge(s_qkf["mla"], e * 2 + 1)
                mm(PS[0:LAT, 7, :], wdkv[:], h_t[:], start=True, stop=True).then_inc(s_lat, 1)

            def project_mla_k(e):
                pe.wait_ge(s_ct, e + 1)
                mm(PS[:, 7, :], wuk[:], c_t[:], start=True, stop=True).then_inc(s_proj["mla"], 1)

            def project_win_q(e):
                pe.wait_ge(s_qkf["mla"], e * 2 + 2)
                mm(PS[:, 7, :], W["L0_attn_Wq"][:], xn_t[:], start=True, stop=True).then_inc(s_proj["win"], 1)

            def project_win_k(e):
                pe.wait_ge(s_qkf["win"], e * 2 + 1)
                mm(PS[:, 7, :], W["L0_attn_Wk"][:], xn_t[:], start=True, stop=True).then_inc(s_proj["win"], 1)

            def project_win_v(e):
                pe.wait_ge(s_qkf["win"], e * 2 + 2)
                by_token(7, xn_t, W["L0_attn_Wv"][:], D).then_inc(s_vproj["win"], 1)

            def project_mla_v(e):
                pe.wait_ge(s_v["win"], e + 1)
                by_token(7, c_t, wuv[:], D).then_inc(s_vproj["mla"], 1)

            def element(i, final):
                def transpose_max(a, half, of):
                    pe.wait_ge(s_mx[a], i * {"win": len(WIN_MAX), "mla": NG}[a] + of)
                    nc.tensor.transpose(PS[:, 6, half * P:half * P + P],
                                        negmax[:, half].rearrange("p h j -> p (h j)"), ident[:])\
                      .then_inc(s_mxt[a], 1)

                def finish(a):
                    for j in range(NT):
                        for g in range(4):
                            last = nc.tensor.transpose(PS[:, j, g * P:g * P + P], o_raw[:, g, j * P:j * P + P], ident[:])
                    last.then_inc(s_ort[a], 1)
                    pe.wait_ge(s_on[a], i + 1)
                    transpose_tiles(4, o_tok).then_inc(s_ot[a], 1)

                def transpose_quarter(a, q):
                    pe.wait_ge(s_or[a], i * 4 + q + 1)
                    for g in range(4):
                        last = nc.tensor.transpose(PS[:, 7, g * P:g * P + P], o_raw[:, g, q * P:q * P + P], ident[:])
                    last.then_inc(s_ort[a], 1)

                def transpose_quarter_back(a, q):
                    pe.wait_ge(s_on[a], i * 4 + q + 1)
                    nc.tensor.transpose(PS[:, 7, 0:P], o_quarter[:], ident[:]).then_inc(s_ot[a], 1)

                pe.wait_ge(s_stk["mla"], i * QST["mla"] + QST["mla"])
                pe.wait_ge(s_stkk["mla"], i * KST["mla"] + KST["mla"])
                pe.wait_ge(s_zero, i * 16 + 16)
                def mla_group(n, j, h0, nh, per, bank):
                    keys = P * (j + 1)
                    for r in range(nh):
                        h = h0 + r
                        c = (r % per) * keys
                        mm(PS[:, bank + r // per, c:c + keys], q_stack[:, h, j * P:j * P + P], k_stack[:, h, 0:keys],
                           start=(r % per == 0), stop=True, skip_group_check=True)
                        last = mm(PS[:, bank + r // per, c + keys - P:c + keys], identb[:], causal_qk[:],
                                  start=False, stop=True, skip_group_check=True)
                    last.then_inc(s_sc["mla"], 1)

                def mla_group_one(m):
                    pe.wait_ge(s_mx["mla"], i * NG + NG2 + max(0, m - 2))
                    mla_group(NG2 + m, *MLA_ONE[m], m % 3)

                for n, group in enumerate(MLA_TWO):
                    if n >= 3:
                        pe.wait_ge(s_mx["mla"], i * NG + n - 2)
                    mla_group(n, *group, 2 * (n % 3))
                    if n == 3:
                        project_win_q(i)
                    if n == 5:
                        project_win_k(i)
                    if n == 8:
                        project_win_v(i)
                mla_group_one(0)
                transpose_max("mla", 0, NG2)
                for m in range(1, LEAD):
                    mla_group_one(m)
                project_mla_v(i)

                MLA_BLOCKS = (((0, 0),), ((1, 0), (3, 384)), ((2, 0),))

                def mla_blocks(h, bank, blocks):
                    for kt, c in blocks:
                        w = T - kt * P
                        mm(PS[:, bank, c:c + w], k_stack[:, h, kt * P:kt * P + P], q_stack[:, h, kt * P:T],
                           start=(c == 0), stop=True, skip_group_check=True)
                        last = mm(PS[:, bank, c:c + P], identb[:], causal_kq[:], start=False, stop=True,
                                  skip_group_check=True)
                    return last

                def mla_pv(g):
                    pe.wait_ge(s_ex["mla"], i * SCORED + (12 * (g + 1) if g < 2 else 3 * HT + 4 * (g - 1)))
                    if g == 0:
                        pe.wait_ge(s_cp["mla"], i * 2 + 2)
                        pe.wait_ge(s_v["mla"], i + 1)
                    if g >= 2:
                        pe.wait_ge(s_or["mla"], i * 4 + g - 1)
                    p4 = probs[:, g % 2 * 5120:g % 2 * 5120 + 5120].rearrange("p (r c) -> p r c", r=4)
                    for kt, c in enumerate((0, 512, 1024, 896)):
                        for r in range(4):
                            last = mm(PS[32 * r:32 * r + VW, 6 + g % 2, kt * P:T], vm[:, kt, 4 * g + r, :],
                                      p4[:, r, c:c + T - kt * P], start=(kt == 0), stop=True, skip_group_check=True,
                                      tile_position=(0, 32 * r))
                    last.then_inc(s_pv["mla"], 1)

                pe.wait_ge(s_sh["mla", 0], i * 32 + 32)
                m = LEAD
                for h in range(HT):
                    for b in range(3):
                        if h >= 1:
                            pe.wait_ge(s_ex["mla"], i * SCORED + 3 * (h - 1) + b + 1)
                        mla_blocks(h, 3 + b, MLA_BLOCKS[b]).then_inc(s_st["mla"], 1)
                        if m < len(MLA_ONE):
                            mla_group_one(m)
                            m += 1
                transpose_max("mla", 1, NG)
                mla_pv(0)
                mla_pv(1)
                for h in range(HT, H):
                    if h == HT:
                        pe.wait_ge(s_mx["mla"], i * NG + NG)
                        pe.wait_ge(s_sh["mla", 1], i * 32 + 32)
                    if h == HT + 1:
                        pe.wait_ge(s_ex["mla"], i * SCORED + 3 * HT)
                    if h >= HT + 2:
                        pe.wait_ge(s_ex["mla"], i * SCORED + 3 * HT + h - HT - 1)
                    for b in range(3):
                        last = mla_blocks(h, 3 * (h % 2) + b, MLA_BLOCKS[b])
                    last.then_inc(s_st["mla"], 1)
                    if h == HT + 5:
                        mla_pv(2)
                mla_pv(3)
                pe.wait_ge(s_or["mla"], i * 4 + 4)
                finish("mla")
                pe.wait_ge(s_otc["mla"], i + 1)
                by_token(7, o_t["mla"], W["L0_ffn_Wo"][:], D).then_inc(s_mo, 1)

                pe.wait_ge(s_stk["win"], i * QST["win"] + QST["win"])
                pe.wait_ge(s_stkk["win"], i * KST["win"] + KST["win"])
                for n, (j, h0) in enumerate(WIN_MAX):
                    b = 2 * (n % 3)
                    lo = WIN if j == 0 else 0
                    if n >= 3:
                        pe.wait_ge(s_mx["win"], i * 16 + n - 2)
                    for r in range(4):
                        h = h0 + r
                        c = (r % 2) * WQ
                        out = PS[:, b + r // 2, c + lo:c + WQ]
                        mm(out, q_stack[:, h, j * P:j * P + P], k_stack[:, h, j * P - WIN + lo:j * P + P],
                           start=(r % 2 == 0), stop=True, skip_group_check=True)
                        last = mm(out, identb[:], band_qk[:, lo:WQ], start=False, stop=True, skip_group_check=True)
                    last.then_inc(s_sc["win"], 1)
                    if n == len(WIN_MAX) // 2 + 1:
                        transpose_max("win", 0, len(WIN_MAX) // 2)
                    if n == 5:
                        pe.wait_ge(s_rr, i + 1)
                        transpose_tiles(7, tmp).then_inc(s_rt, 1)
                    if n == 7:
                        pe.wait_ge(s_h2, i + 1)
                        by_token(7, h_t, gate_w[:], E).then_inc(s_lg[0], 1)
                transpose_max("win", 1, len(WIN_MAX))

                def win_scores(n):
                    b = 3 * (n % 2)
                    if n % 4 == 0:
                        pe.wait_ge(s_sh["win", n // 4], i * 32 + 32)
                    if n >= 2:
                        pe.wait_ge(s_ex["win"], i * 8 + n - 1)
                    for r in range(2):
                        h = 2 * n + r
                        for kt in range(NT):
                            w = WQ if kt < NT - 1 else P
                            out = PS[:, b + r, kt * WQ:kt * WQ + w] if kt < NT - 1 else PS[:, b + 2, r * P:r * P + P]
                            first = kt == 0 or (kt == NT - 1 and r == 0)
                            mm(out, k_stack[:, h, kt * P:kt * P + P], q_stack[:, h, kt * P:kt * P + w],
                               start=first, stop=True, skip_group_check=True)
                            last = mm(out, identb[:], band_kq[:, 0:w], start=False, stop=True, skip_group_check=True)
                    last.then_inc(s_st["win"], 1)

                def win_pv(g):
                    if g == 0:
                        pe.wait_ge(s_cp["win"], i * 2 + 2)
                    if g == 1:
                        pe.wait_ge(s_wp[0], i + 1)
                    pe.wait_ge(s_ex["win"], i * 8 + 2 * g + 2)
                    if g >= 2:
                        pe.wait_ge(s_or["win"], i * 4 + g - 1)
                    p4 = probs[:, g % 2 * 5120:g % 2 * 5120 + 2560].rearrange("p (r c) -> p r c", r=4)
                    for kt in range(NT):
                        w = WQ if kt < NT - 1 else P
                        for r in range(4):
                            last = mm(PS[32 * r:32 * r + VW, 6 + g % 2, kt * P:kt * P + w],
                                      v1[:, kt, 4 * g + r, :], p4[:, r, kt * WQ:kt * WQ + w],
                                      start=(kt == 0), stop=True, skip_group_check=True,
                                      tile_position=(0, 32 * r))
                    last.then_inc(s_pv["win"], 1)

                for n in range(8):
                    win_scores(n)
                    if n == 3:
                        pe.wait_ge(s_cb[0], i + 1)
                        for j in range(NT):
                            last = nc.tensor.transpose(PS[0:96, 7, j * P:j * P + P], wtok[:, j, :], ident[:])
                        last.then_inc(s_cbt[0], 1)
                    if n >= 2 and n % 2 == 0:
                        win_pv(n // 2 - 1)
                def spread_combine(k, e):
                    C = (C0, C1)[k]
                    if e >= 2:
                        pe.wait_ge(s_hid[k], i * E * C + (e - 1) * C)
                    mm(PS[:, 4 + e % 2, :], sel_w[:, e, :], wparts[:], start=True, stop=True).then_inc(s_wb[k], 1)

                def up0(n):
                    e, c = n // C0, n % C0
                    if n >= 4:
                        pe.wait_ge(s_si[0], i * E * C0 + n - 3)
                    mm(PS[:, n % 4, :], w1[:, e, c * P:c * P + P], h_t[:], start=True, stop=True)\
                      .then_inc(s_up[0], 1)

                pe.wait_ge(s_ex["win"], i * 8 + 7)
                for n in range(3):
                    up0(n)
                win_pv(3)
                for n in range(3, NA - 1):
                    up0(n)
                spread_combine(0, 0)
                for n in range(E * C0):
                    if (n + 1) % C0 == 0 and n + 1 < E * C0:
                        spread_combine(0, (n + 1) // C0)
                    if n + NA - 1 < E * C0:
                        up0(n + NA - 1)
                    pe.wait_ge(s_hid[0], i * E * C0 + n + 1)
                    last = mm(PS[:, 6, :], w2[:, n // C0, n % C0, :], hid_b[:, n % 3], start=(n == 0),
                              stop=(n == E * C0 - 1), skip_group_check=True)
                    last.then_inc(s_dn[0], 1)
                    if n < 2 * NT and n % 2 == 0:
                        if n >= 2:
                            pe.wait_ge(s_otc["win"], i * 4 + n // 2)
                        transpose_quarter("win", n // 2)
                    if n < 2 * NT and n % 2 == 1:
                        transpose_quarter_back("win", n // 2)
                    if n == 2 * NT + 2:
                        pe.wait_ge(s_otc["win"], i * 4 + 4)
                        mm(PS[:, 6, :], W["L0_attn_Wo"][:], o_t["win"][:], start=False, stop=False,
                           skip_group_check=True)
                pe.wait_ge(s_dn[0], i * E * C0 + E * C0)
                pe.nop().then_inc(s_yo[0], 1)
                pe.wait_ge(s_yc[0], i + 1)
                transpose_tiles(7, y_t.rearrange("p (j t) -> p j t", j=NT)).then_inc(s_yt[0], 1)

                pe.wait_ge(s_xn, i * 2 + 2)
                transpose_tiles(0, xn).then_inc(s_tr, 1)
                pe.wait_ge(s_xnt, i * 3 + 3)
                by_token(4, xn_t, cen_t[:], E).then_inc(s_dist, 1)
                mm(PS[:, 1, :], W["L1_attn_Wq"][:], xn_t[:], start=True, stop=True).then_inc(s_proj["rel"], 1)
                mm(PS[:, 2, :], W["L1_attn_Wk"][:], xn_t[:], start=True, stop=True).then_inc(s_proj["rel"], 1)
                by_token(7, xn_t, W["L1_attn_Wv"][:], D).then_inc(s_vproj["rel"], 1)

                def up1(n):
                    e, c = n // C1, n % C1
                    if n < 2:
                        pe.wait_ge(s_qkf["rel"], i * 2 + n + 1)
                    if n >= 2:
                        pe.wait_ge(s_hu, i * E * C1 + n - 1)
                    mm(PS[0:CW, 2 * (n % 2), :], wg[:, e, c * CW:c * CW + CW], xn_t[:], start=True, stop=True)
                    mm(PS[0:CW, 2 * (n % 2) + 1, :], wu[:, e, c * CW:c * CW + CW], xn_t[:], start=True, stop=True)\
                      .then_inc(s_up[1], 1)

                up1(0)
                up1(1)
                pe.wait_ge(s_cb[1], i + 1)
                for j in range(NT):
                    last = nc.tensor.transpose(PS[0:96, 5, j * P:j * P + P], wtok[:, j, :], ident[:])
                last.then_inc(s_cbt[1], 1)
                up1(2)
                pe.wait_ge(s_wp[1], i + 1)
                for n in range(E * C1):
                    if n == C1:
                        pe.wait_ge(s_wf, i + 1)
                        mm(PS[:, 6, :], b2[:], wt_full[:], start=False, stop=False, skip_group_check=True)
                    if n == 0:
                        spread_combine(1, 0)
                    if (n + 1) % C1 == 0 and n + 1 < E * C1:
                        spread_combine(1, (n + 1) // C1)
                    if n >= 1 and n + 2 < E * C1:
                        up1(n + 2)
                    pe.wait_ge(s_hid[1], i * E * C1 + n + 1)
                    last = mm(PS[:, 6, :], wd[:, n // C1, n % C1, :], hid_c[0:CW, n % 3], start=(n == 0),
                              stop=(n == E * C1 - 1), skip_group_check=True)
                    last.then_inc(s_dn[1], 1)
                pe.wait_ge(s_dn[1], i * E * C1 + E * C1)
                pe.nop().then_inc(s_yo[1], 1)

                pe.wait_ge(s_v["rel"], i + 1)
                pe.wait_ge(s_stk["rel"], i * QST["rel"] + QST["rel"])
                pe.wait_ge(s_stkk["rel"], i * KST["rel"] + KST["rel"])
                base = i * NS

                def scores(t, kt):
                    l0, hh = t // 2 * LB, t % 2
                    if kt == 0 and t >= 3:
                        pe.wait_ge(s_ex["rel"], base + t - 2)
                    qs = q_stack[:, hh * HT:hh * HT + HT, l0:l0 + LB]
                    out = PS[:, 2 * (t % 3) + kt // 2, kt % 2 * 2 * P:kt % 2 * 2 * P + 2 * P]\
                        .rearrange("p (h l) -> p h l", h=HT)
                    for h in range(HT):
                        mm(out[:, h, :], k_stack[:, hh * HT + h, kt * P:kt * P + P], qs[:, h, :],
                           start=(kt % 2 == 0 and h == 0), stop=True, skip_group_check=True)
                    for u in range(LB // 2):
                        c = kt * P + T - 1 - (l0 + 2 * u)
                        last = mm(out[:, :, 2 * u:2 * u + 2], rel_stack[:, c:c + P], qs[:, :, 2 * u:2 * u + 2],
                                  start=False, stop=True, skip_group_check=True)
                    if kt == NT - 1:
                        last.then_inc(s_rs, 1)

                def transpose_tile_max(t):
                    pe.wait_ge(s_rm, base + t + 1)
                    for c in range(2):
                        last = nc.tensor.transpose(PS[:, 6, c * P:c * P + P], mcol[:, t % 2, c * P:c * P + P],
                                                   ident[:])
                    last.then_inc(s_rmt, 1)

                def transpose_row_max(t):
                    pe.wait_ge(s_rc, base + t + 1)
                    nc.tensor.transpose(PS[0:2, 6, 2 * P:3 * P], cm[:], ident[:]).then_inc(s_rct, 1)

                def shift(t):
                    pe.wait_ge(s_rcs, base + t + 1)
                    for k in range(4):
                        for c in range(2):
                            last = mm(PS[:, 2 * (t % 3) + k // 2, (k % 2) * 2 * P + c * P:(k % 2) * 2 * P + c * P + P],
                                      sel_c[:, c, :], crow[:], start=False, stop=True, skip_group_check=True)
                    last.then_inc(s_rsh, 1)

                def sum_quarter(q, first=0, end=4):
                    pe.wait_ge(s_ex["rel"], base + (q + 1) * NSQ - (1 if end == 2 else 0))
                    if q >= 1:
                        pe.wait_ge(s_or["rel"], i * 4 + q)
                    pr = probs[:, 0:NT * H * P].rearrange("p (k h l) -> p k h l", k=NT, h=H)
                    for g in range(first, end):
                        for kt in range(NT):
                            for r in range(4):
                                last = mm(PS[32 * r:32 * r + VW, 7, g * P:g * P + P], v0[:, kt, 4 * g + r, :],
                                          pr[:, kt, 4 * g + r, :], start=(g == 0 and kt == 0), stop=True,
                                          skip_group_check=True, tile_position=(0, 32 * r))
                    if end == 4:
                        last.then_inc(s_pv["rel"], 1)

                def project_quarter(q):
                    pe.wait_ge(s_otc["rel"], i * 4 + q + 1)
                    mm(PS[:, 7, P:2 * P], o_t["rel"][:, q * P:q * P + P], W["L1_attn_Wo"][:],
                       start=True, stop=True).then_inc(s_ao, 1)

                for t in range(NS + 2):
                    if t < NS:
                        scores(t, 0)
                        scores(t, 1)
                    if t >= 2:
                        shift(t - 2)
                    if t < NS:
                        scores(t, 2)
                    if 1 <= t <= NS:
                        transpose_tile_max(t - 1)
                    if t < NS:
                        scores(t, 3)
                    if t == 0:
                        pe.wait_ge(s_yc[1], i + 1)
                        transpose_tiles(7, y_t.rearrange("p (j t) -> p j t", j=NT)).then_inc(s_yt[1], 1)
                    if 1 <= t <= NS:
                        transpose_row_max(t - 1)
                    if t == NS:
                        sum_quarter(NT - 1, 0, 2)
                    if t > NSQ and t % NSQ == 1:
                        if not final and t // NSQ == 2:
                            pe.wait_ge(s_ct, i + 2)
                        if not final and t // NSQ == 3:
                            pe.wait_ge(s_qkf["mla"], i * 2 + 4)
                        sum_quarter(t // NSQ - 1, 2 if t > NS else 0)
                    if t >= NSQ + 2 and t % NSQ == 2:
                        transpose_quarter("rel", t // NSQ - 1)
                    if t >= NSQ + 3 and t % NSQ == 3:
                        transpose_quarter_back("rel", t // NSQ - 1)
                    if t >= NSQ + 4 and t % NSQ == 4:
                        project_quarter(t // NSQ - 1)
                    if not final and t == 13:
                        pe.wait_ge(s_x2, i * 4 + 1)
                        project_xn(i + 1)
                    if not final and t == 14:
                        project_h(i + 1)
                    if not final and t == 15:
                        project_mla_q(i + 1)
                    if not final and t == 16:
                        project_latent(i + 1)
                    if not final and t == 21:
                        pe.wait_ge(s_x2, i * 4 + 2)
                        project_mla_k(i + 1)
                transpose_quarter("rel", NT - 1)
                transpose_quarter_back("rel", NT - 1)
                project_quarter(NT - 1)

            project_xn(0)
            project_h(0)
            project_mla_q(0)
            project_latent(0)
            project_mla_k(0)
            with pe.Fori(0, B - 1) as i:
                element(i, False)
            element(B - 1, True)


_TRANSPOSED = ["L0_attn_Wq", "L0_attn_Wk", "L0_attn_Wv", "L0_attn_Wo",
               "L1_attn_Wq", "L1_attn_Wk", "L1_attn_Wv", "L1_attn_Wo"]


def kernel(**inputs):
    import numpy as np
    import concourse.bacc as bacc
    from concourse.bass_utils import run_bass_kernel_spmd

    nc = bacc.Bacc("TRN2", target_bir_lowering=False, num_devices=1)
    arrays, dram = {}, {}
    for name, a in inputs.items():
        a = np.asarray(a)
        if name in _TRANSPOSED:
            a = a.T
        if name in ("L1_ffn_bg", "L1_ffn_b1"):
            a = a.reshape(-1, a.shape[1] // 3).T
        arrays[name] = np.ascontiguousarray(a)
    arrays["centroid_t"] = np.ascontiguousarray(arrays["L1_ffn_centroid"].T)
    arrays["rel_emb_t"] = np.ascontiguousarray(arrays.pop("L1_attn_rel_emb").T)
    for name, a in arrays.items():
        dram[name] = nc.dram_tensor("in_" + name, a.shape, mybir.dt.from_np(a.dtype), kind="ExternalInput").ap()
    dram["L1_attn_rel_emb"] = inputs["L1_attn_rel_emb"]
    x = arrays["L0_attn_x"]
    dram["out"] = nc.dram_tensor("out", x.shape, mybir.dt.from_np(x.dtype), kind="ExternalOutput").ap()
    two_layers(nc, dram)
    r = run_bass_kernel_spmd(nc, [{"in_" + n: a for n, a in arrays.items()}], core_ids=[0])
    return r.results[0]["out"]
```
